# Optimizing a Trainium2 kernel written in Bass

```python
import numpy as np
import jax
import jax.numpy as jnp

def _softmax(x, axis=-1):
    return jax.nn.softmax(x, axis=axis)
def _gelu(x):
    return jax.nn.gelu(x, approximate=True)
def _silu(x):
    return jax.nn.silu(x)
def _sigmoid(x):
    return jax.nn.sigmoid(x)
def _layernorm(x, axis=-1, eps=1e-5):
    m = jnp.mean(x, axis=axis, keepdims=True)
    v = jnp.var(x, axis=axis, keepdims=True)
    return (x - m) / jnp.sqrt(v + eps)
def _scatter_add(tgt, idx, src, axis=0):
    return tgt.at[idx].add(src)
def _segment_sum(src, seg, n):
    return jax.ops.segment_sum(src, seg, n)

kernel_name = 'mk_adj_resnorm_d4_adj_256_faede5'

def setup_inputs(seed: int = 0):
    np.random.seed(seed)
    _w = jnp.asarray
    def _rec_inputs():
        import jax
        import jax.numpy as jnp
        _gk = jax.random.key(seed)
        x = -0.000125 + 0.9999 * jax.random.normal(jax.random.fold_in(_gk, 1), (128, 64, 256), jnp.float32)
        _a = jax.random.bernoulli(jax.random.fold_in(_gk, 2), 0.0625, (64, 64))
        _a = jnp.logical_or(_a, jnp.swapaxes(_a, -1, -2))
        _a = jnp.logical_or(_a, jnp.eye(64, dtype=bool))
        _af = _a.astype(jnp.float32)
        _af = _af * jax.random.uniform(jax.random.fold_in(_gk, 3), (64, 64), jnp.float32, 0.05, 0.000488281)
        adj = _af
        return x, adj
    x, adj = _rec_inputs()
    def _L0_gnn_setup():
        import jax, jax.numpy as jnp
        import numpy as np
        B, T, D, H = (64, 2048, 256, 256)
        MAX_SKIP = 4

        def _lstm_last(Wih, Whh, bih, bhh, xs):
            N, _, Hd = xs.shape
            bias = bih + bhh

            def step(carry, x_t):
                h, c = carry
                g = x_t @ Wih.T + h @ Whh.T + bias
                i, f, gg, o = jnp.split(g, 4, axis=-1)
                c = jax.nn.sigmoid(f) * c + jax.nn.sigmoid(i) * jnp.tanh(gg)
                h = jax.nn.sigmoid(o) * jnp.tanh(c)
                return ((h, c), None)
            init = (jnp.zeros((N, Hd), xs.dtype), jnp.zeros((N, Hd), xs.dtype))
            (h_last, _), _ = jax.lax.scan(step, init, jnp.swapaxes(xs, 0, 1))
            return h_last
        key = jax.random.key(seed)
        ks = jax.random.split(key, 8)
        s = 0.05
        x = jax.random.normal(ks[0], (B, T, D), jnp.float32)
        adj = jax.random.uniform(ks[1], (T, T), jnp.float32) / T
        Wg0 = jax.random.normal(ks[2], (D, H), jnp.float32) * s
        bg0 = jnp.zeros((H,), jnp.float32)
        Wg1 = jax.random.normal(ks[3], (H, H), jnp.float32) * s
        bg1 = jnp.zeros((H,), jnp.float32)
        Wih = jax.random.normal(ks[4], (MAX_SKIP, 4 * H, H), jnp.float32) * s
        Whh = jax.random.normal(ks[5], (MAX_SKIP, 4 * H, H), jnp.float32) * s
        bih = jax.random.normal(ks[6], (MAX_SKIP, 4 * H), jnp.float32) * s
        bhh = jax.random.normal(ks[7], (MAX_SKIP, 4 * H), jnp.float32) * s
        return dict(x=x, adj=adj, Wg0=Wg0, bg0=bg0, Wg1=Wg1, bg1=bg1, Wih=Wih, Whh=Whh, bih=bih, bhh=bhh)
    _L0_gnn_all = _L0_gnn_setup()
    _L0_gnn_in = {k: v for k, v in _L0_gnn_all.items() if k in ('Wg0', 'bg0', 'Wg1', 'bg1', 'Wih', 'Whh', 'bih', 'bhh', )}
    del _L0_gnn_all

    def _L1_gnn_setup():
        import jax, jax.numpy as jnp
        import numpy as np
        N = 4096
        NFEAT, NHID, NCLASS = (256, 512, 256)
        B = 4

        def _slconv(x, adj, S, W):
            support = jnp.einsum('bnf,fh->bnh', x, W)
            weighting = adj * S
            return jnp.einsum('nm,bmh->bnh', weighting, support)
        key = jax.random.key(seed)
        ks = jax.random.split(key, 6)
        x = jax.random.normal(ks[0], (B, N, NFEAT), dtype=jnp.float32)
        adj = jax.random.uniform(ks[1], (N, N), dtype=jnp.float32)
        S = jnp.ones((N, N), dtype=jnp.float32)
        W1 = jax.random.normal(ks[2], (NFEAT, NHID), dtype=jnp.float32) / np.sqrt(NFEAT)
        W2 = jax.random.normal(ks[3], (NHID, 2 * NHID), dtype=jnp.float32) / np.sqrt(NHID)
        W3 = jax.random.normal(ks[4], (2 * NHID, NCLASS), dtype=jnp.float32) / np.sqrt(2 * NHID)
        return {'x': x, 'adj': adj, 'S': S, 'W1': W1, 'W2': W2, 'W3': W3}
    _L1_gnn_all = _L1_gnn_setup()
    _L1_gnn_in = {k: v for k, v in _L1_gnn_all.items() if k in ('W1', 'W2', 'W3', )}
    del _L1_gnn_all

    def _L2_gnn_setup():
        import jax, jax.numpy as jnp
        import numpy as np
        B, N, D_IN, HID, D_OUT = (64, 1024, 256, 128, 256)
        key = jax.random.key(seed)
        kf, ka, kw1, kw2 = jax.random.split(key, 4)
        features = jax.random.normal(kf, (B, N, D_IN), dtype=jnp.float32)
        A = jax.random.uniform(ka, (N, N), dtype=jnp.float32)
        A = 0.5 * (A + A.T)
        lim1 = float(np.sqrt(6.0 / (D_IN + HID)))
        lim2 = float(np.sqrt(6.0 / (HID + D_OUT)))
        W1 = jax.random.uniform(kw1, (D_IN, HID), minval=-lim1, maxval=lim1, dtype=jnp.float32)
        b1 = jnp.zeros((HID,), jnp.float32)
        W2 = jax.random.uniform(kw2, (HID, D_OUT), minval=-lim2, maxval=lim2, dtype=jnp.float32)
        b2 = jnp.zeros((D_OUT,), jnp.float32)
        return {'features': features, 'A': A, 'W1': W1, 'b1': b1, 'W2': W2, 'b2': b2}
    _L2_gnn_all = _L2_gnn_setup()
    _L2_gnn_in = {k: v for k, v in _L2_gnn_all.items() if k in ('W1', 'b1', 'W2', 'b2', )}
    del _L2_gnn_all

    def _L3_gnn_setup():
        import jax, jax.numpy as jnp
        import numpy as np
        BT, N, D, HEADS, E = (1024, 64, 256, 4, 512)
        LRELU_SLOPE = 0.2
        EPS = 1e-08
        key = jax.random.key(seed)
        ks = jax.random.split(key, 8)
        d = D
        return {'H': jax.random.normal(ks[0], (BT, N, d), jnp.float32), 'W_lin': jax.random.normal(ks[1], (d, d), jnp.float32) / np.sqrt(d).astype(np.float32), 'W_val': jax.random.normal(ks[2], (d, d), jnp.float32) / np.sqrt(d).astype(np.float32), 'a': jax.random.normal(ks[3], (HEADS, d // HEADS), jnp.float32), 'W_out': jax.random.normal(ks[4], (d, d), jnp.float32) / np.sqrt(d).astype(np.float32), 'A0': jax.random.uniform(ks[5], (N, N), jnp.float32), 'src': jax.random.randint(ks[6], (E,), 0, N, jnp.int32), 'dst': jax.random.randint(ks[7], (E,), 0, N, jnp.int32)}
    _L3_gnn_all = _L3_gnn_setup()
    _L3_gnn_in = {k: v for k, v in _L3_gnn_all.items() if k in ('W_lin', 'W_val', 'a', 'W_out', 'src', 'dst', )}
    del _L3_gnn_all

    return {
        "x": x,
        "adj": adj,
        "L0_gnn_Wg0": _L0_gnn_in["Wg0"],
        "L0_gnn_bg0": _L0_gnn_in["bg0"],
        "L0_gnn_Wg1": _L0_gnn_in["Wg1"],
        "L0_gnn_bg1": _L0_gnn_in["bg1"],
        "L0_gnn_Wih": _L0_gnn_in["Wih"],
        "L0_gnn_Whh": _L0_gnn_in["Whh"],
        "L0_gnn_bih": _L0_gnn_in["bih"],
        "L0_gnn_bhh": _L0_gnn_in["bhh"],
        "L1_gnn_W1": _L1_gnn_in["W1"],
        "L1_gnn_W2": _L1_gnn_in["W2"],
        "L1_gnn_W3": _L1_gnn_in["W3"],
        "L2_gnn_W1": _L2_gnn_in["W1"],
        "L2_gnn_b1": _L2_gnn_in["b1"],
        "L2_gnn_W2": _L2_gnn_in["W2"],
        "L2_gnn_b2": _L2_gnn_in["b2"],
        "L3_gnn_W_lin": _L3_gnn_in["W_lin"],
        "L3_gnn_W_val": _L3_gnn_in["W_val"],
        "L3_gnn_a": _L3_gnn_in["a"],
        "L3_gnn_W_out": _L3_gnn_in["W_out"],
        "L3_gnn_src": _L3_gnn_in["src"],
        "L3_gnn_dst": _L3_gnn_in["dst"],
    }

def reference(x, adj, L0_gnn_Wg0, L0_gnn_bg0, L0_gnn_Wg1, L0_gnn_bg1, L0_gnn_Wih, L0_gnn_Whh, L0_gnn_bih, L0_gnn_bhh, L1_gnn_W1, L1_gnn_W2, L1_gnn_W3, L2_gnn_W1, L2_gnn_b1, L2_gnn_W2, L2_gnn_b2, L3_gnn_W_lin, L3_gnn_W_val, L3_gnn_a, L3_gnn_W_out, L3_gnn_src, L3_gnn_dst):
    import jax
    import jax.numpy as jnp
    def _L0_gnn_ref(x, adj, Wg0, bg0, Wg1, bg1, Wih, Whh, bih, bhh):
        import jax, jax.numpy as jnp
        import numpy as np
        B, T, D, H = (64, 2048, 256, 256)
        MAX_SKIP = 4

        def _lstm_last(Wih, Whh, bih, bhh, xs):
            N, _, Hd = xs.shape
            bias = bih + bhh

            def step(carry, x_t):
                h, c = carry
                g = x_t @ Wih.T + h @ Whh.T + bias
                i, f, gg, o = jnp.split(g, 4, axis=-1)
                c = jax.nn.sigmoid(f) * c + jax.nn.sigmoid(i) * jnp.tanh(gg)
                h = jax.nn.sigmoid(o) * jnp.tanh(c)
                return ((h, c), None)
            init = (jnp.zeros((N, Hd), xs.dtype), jnp.zeros((N, Hd), xs.dtype))
            (h_last, _), _ = jax.lax.scan(step, init, jnp.swapaxes(xs, 0, 1))
            return h_last
        h = jax.nn.relu(jnp.einsum('ts,bsh->bth', adj, x @ Wg0 + bg0))
        h = jax.nn.relu(jnp.einsum('ts,bsh->bth', adj, h @ Wg1 + bg1))
        Bv, Tv, Hd = h.shape
        for p in range(1, MAX_SKIP + 1):
            nw = Tv // p
            wins = h[:, :nw * p, :].reshape(Bv * nw, p, Hd)
            last = _lstm_last(Wih[p - 1], Whh[p - 1], bih[p - 1], bhh[p - 1], wins)
            idx = jnp.arange(nw) * p + (p - 1)
            h = h.at[:, idx, :].set(last.reshape(Bv, nw, Hd))
        return h

    def _L1_gnn_ref(x, adj, S, W1, W2, W3):
        import jax, jax.numpy as jnp
        import numpy as np
        N = 4096
        NFEAT, NHID, NCLASS = (256, 512, 256)
        B = 4

        def _slconv(x, adj, S, W):
            support = jnp.einsum('bnf,fh->bnh', x, W)
            weighting = adj * S
            return jnp.einsum('nm,bmh->bnh', weighting, support)
        h = jax.nn.relu(_slconv(x, adj, S, W1))
        h = jax.nn.relu(_slconv(h, adj, S, W2))
        return _slconv(h, adj, S, W3)

    def _L2_gnn_ref(features, A, W1, b1, W2, b2):
        import jax, jax.numpy as jnp
        import numpy as np
        B, N, D_IN, HID, D_OUT = (64, 1024, 256, 128, 256)
        deg = jnp.sum(A, axis=0) + jnp.sum(A, axis=1) - jnp.diagonal(A)
        d_inv_sqrt = jnp.where(deg > 0, jax.lax.rsqrt(deg), 0.0)
        L = jnp.diag(deg) - A
        L_norm = d_inv_sqrt[:, None] * L * d_inv_sqrt[None, :]
        _, U = jnp.linalg.eigh(L_norm)
        agg = jnp.einsum('mn,bnd->bmd', U.T, features)
        h = jax.nn.relu(agg @ W1 + b1)
        out = h @ W2 + b2
        return jnp.einsum('nm,bmd->bnd', U, out)

    def _L3_gnn_ref(H, W_lin, W_val, a, W_out, A0, src, dst):
        import jax, jax.numpy as jnp
        import numpy as np
        BT, N, D, HEADS, E = (1024, 64, 256, 4, 512)
        LRELU_SLOPE = 0.2
        EPS = 1e-08
        bt, n, d = H.shape
        h, dh = a.shape
        Xq = (H @ W_lin.T).reshape(bt, n, h, dh)
        Xv = (H @ W_val.T).reshape(bt, n, h, dh)
        Qs = Xq[:, src]
        Kt = Xq[:, dst]
        e = jnp.einsum('behd,hd->beh', jax.nn.leaky_relu(Qs + Kt, LRELU_SLOPE), a)
        e = e + jnp.log(A0[src, dst] + EPS)[None, :, None]
        e_t = e.transpose(1, 0, 2)
        m = jax.ops.segment_max(e_t, src, num_segments=n)
        ex = jnp.exp(e_t - m[src])
        denom = jax.ops.segment_sum(ex, src, num_segments=n)
        attn = ex / denom[src]
        Vt = Xv[:, dst].transpose(1, 0, 2, 3)
        Y = jax.ops.segment_sum(attn[..., None] * Vt, src, num_segments=n)
        Y = Y.transpose(1, 0, 2, 3).reshape(bt, n, d)
        return Y @ W_out.T

    x = _layernorm(x + _L0_gnn_ref(x, adj, L0_gnn_Wg0, L0_gnn_bg0, L0_gnn_Wg1, L0_gnn_bg1, L0_gnn_Wih, L0_gnn_Whh, L0_gnn_bih, L0_gnn_bhh), axis=-1)
    x = _layernorm(x + _L1_gnn_ref(x, adj, adj, L1_gnn_W1, L1_gnn_W2, L1_gnn_W3), axis=-1)
    x = _layernorm(x + _L2_gnn_ref(x, adj, L2_gnn_W1, L2_gnn_b1, L2_gnn_W2, L2_gnn_b2), axis=-1)
    x = _layernorm(x + _L3_gnn_ref(x, L3_gnn_W_lin, L3_gnn_W_val, L3_gnn_a, L3_gnn_W_out, adj, L3_gnn_src, L3_gnn_dst), axis=-1)
    return x


_drawn_inputs = setup_inputs


def setup_inputs(seed=0):
    import zlib

    import numpy as np

    out = dict(_drawn_inputs(seed))
    spreads = {'L0_gnn_bg0': (0.0, 0.8),
     'L0_gnn_bg1': (0.0, 0.8),
     'L2_gnn_b1': (0.0, 0.1),
     'L2_gnn_b2': (0.0, 0.1)}
    factors = {'L0_gnn_Wg0': 8.0,
     'L0_gnn_Wg1': 8.0,
     'L0_gnn_Wih': 6.449,
     'L0_gnn_Whh': 6.605,
     'L1_gnn_W1': 64.0,
     'L1_gnn_W2': 64.0,
     'L1_gnn_W3': 64.0}
    for name, (base, spread) in spreads.items():
        noise = np.random.default_rng([zlib.crc32(name.encode()), seed]).standard_normal(out[name].shape)
        drawn = base * np.exp(spread * noise) if base else spread * noise
        out[name] = jnp.asarray(drawn.astype(out[name].dtype))
    for name, factor in factors.items():
        out[name] = (out[name] * factor).astype(out[name].dtype)
    return out
```

```python
from contextlib import ExitStack

import concourse.bass as bass
from concourse import mybir

ALU = mybir.AluOpType
ACT = mybir.ActivationFunctionType
F32 = mybir.dt.float32
BF16 = mybir.dt.bfloat16
I32 = mybir.dt.int32
AX_X = mybir.AxisListType.X

BATCH, T, D = 128, 64, 256
P = 128
GB = 16
NGRP = BATCH // GB
GT = GB * T
TILES = GT // P
HALF = TILES // 2
HN = HALF * P
EDGES = 512
HEADS = 4
LN_EPS = 1e-5
TINY = 1e-30
MAX_SKIP = 4
SECTIONS = 32
PASSES = 5


def prepare(nc, dram, keep):
    N = T
    with ExitStack() as ctx:
        def sb(name, shape, dt=F32):
            return ctx.enter_context(nc.sbuf_tensor(name, shape, dt))

        def sem(name):
            return ctx.enter_context(nc.semaphore(name))

        ps = ctx.enter_context(nc.psum_tensor("ps_prep", [P, 8, 512], F32))
        adj = sb("adj_sb", [P, N])
        adjT = sb("adjT_sb", [P, N])
        pidx = sb("pidx", [P, P], I32)
        pidx_f = sb("pidx_f", [P, P])
        iota_i = sb("iota_i", [P, P], I32)
        iota = sb("iota", [P, P])
        ident = keep["ident"]
        ones = sb("ones", [N, P])
        neg_id = sb("neg_id", [P, N])
        is_q = sb("is_q", [P, 1])
        half_pow = sb("half_pow", [P, N])
        mhalf_pow = sb("mhalf_pow", [P, N])
        M = sb("M", [P, N])
        V = sb("V", [P, N])
        Vr = sb("Vr", [P, N])
        Wr = sb("Wr", [P, N])
        OH = sb("OH", [P, N])
        MK = sb("MK", [P, N])
        SEL = sb("SEL", [N, P])
        DG = sb("DG", [N, N])
        junk = sb("junk", [P, 8, N])
        sc = sb("sc", [P, 32])
        k1 = sb("k1", [P, 1])
        D_ = sb("Drow", [N, N])
        E_ = sb("Erow", [N, N])
        nE2 = sb("nE2", [N, N])
        DL = sb("DL", [N, N, SECTIONS])
        neg = sb("neg", [N, N, SECTIONS])
        lam = sb("lam", [N, SECTIONS])
        steps = sb("steps", [N, SECTIONS])
        rc = sb("rc", [N, SECTIONS])
        cnt = sb("cnt", [N, SECTIONS])
        st = sb("st", [N, 64])
        PD = sb("PD", [N, N, 2])
        QP = sb("QP", [N, N, 2])
        nE2P = sb("nE2P", [N, N, 2])
        nEP = sb("nEP", [N, N, 2])
        RP = sb("RP", [N, N, 2])
        ZP = sb("ZP", [N, N, 2])
        gam = sb("gam", [N, N])
        dlt = sb("dlt", [N, N])
        Z = sb("Z", [N, N])
        BD = sb("BDc", [N, 32, 6])
        BE = sb("BEc", [N, 32, 6])
        BE2 = sb("BE2c", [N, 32, 6])
        BC = sb("BCc", [N, 32, 6])
        BZ = sb("BZc", [N, 32, 6])
        BM = sb("BMc", [N, 32, 6])
        QT2 = sb("QT2", [N, P])
        Z2 = sb("Z2", [N, P])
        Zs = sb("Zs", [N, N])

        loaded = sem("adj_loaded")
        made = sem("consts_made")
        link_s = sem("dve_link")
        hh = sem("hh_link")
        sel_ok = sem("sel_ready")
        row_ok = sem("row_ready")
        n2_ok = sem("n2_ready")
        nrm_ok = sem("norm_ready")
        dg_ok = sem("diag_ready")
        w_ok = sem("w_ready")
        pw_in = sem("pow_in")
        pw_out = sem("pow_out")
        tr_in = sem("tr_in")
        tr_out = sem("tr_out")
        ms = sem("ms_link")
        steps_k = N - 2

        block = ctx.enter_context(nc.Block())

        @block.sync
        def _(sp):
            for half in range(2):
                rows = slice(half * N, half * N + N)
                sp.dma_start(adj[rows, :], dram["adj"]).then_inc(loaded, 16)
                sp.dma_start(adjT[rows, :], dram["adjT"]).then_inc(loaded, 16)
            keep["load_weights"](sp)

        @block.gpsimd
        def _(pool):
            nc.gpsimd.iota(pidx[:, :], pattern=[[0, P]], base=0, channel_multiplier=1).then_inc(made, 1)
            nc.gpsimd.iota(iota_i[:, :], pattern=[[1, P]], base=0, channel_multiplier=0).then_inc(made, 1)
            nc.gpsimd.memset(half_pow[:, :], 0.5).then_inc(made, 1)
            nc.gpsimd.memset(mhalf_pow[:, :], -0.5).then_inc(made, 1)
            nc.gpsimd.memset(ones[:, :], 1.0).then_inc(made, 1)
            pool.wait_ge(made, 5)
            pool.wait_ge(pw_in, 1)
            nc.gpsimd.tensor_tensor(sc[:, 1:2], sc[:, 0:1], mhalf_pow[:, 0:1], ALU.pow).then_inc(pw_out, 1)
            with pool.Fori(0, steps_k) as k:
                pool.wait_ge(n2_ok, k + 1)
                nc.gpsimd.tensor_tensor(sc[:, 4:5], sc[:, 3:4], half_pow[:, 0:1], ALU.pow).then_inc(nrm_ok, 1)
            pool.wait_ge(pw_in, 2)
            nc.gpsimd.tensor_tensor(st[:, 11:12], st[:, 10:11], mhalf_pow[0:N, 0:1], ALU.pow).then_inc(pw_out, 1)

        @block.tensor
        def _(pe):
            pe.wait_ge(tr_in, 1)
            nc.tensor.matmul(ps[0:N, 7, 0:N], ones[:, 0:N], DG[:, :], start=True, stop=True)
            nc.tensor.matmul(ps[0:N, 7, N:2 * N], ones[:, 0:N], adjT[0:N, :], start=True, stop=True)\
                .then_inc(tr_out, 1)
            with pe.Fori(0, steps_k) as k:
                pe.wait_ge(sel_ok, k + 1)
                nc.tensor.matmul(ps[:, 0, 0:N], SEL[:, :], M[0:N, :], start=True, stop=True).then_inc(row_ok, 1)
                pe.wait_ge(dg_ok, k + 1)
                nc.tensor.matmul(ps[:, 1, 0:N], ones[:, :], DG[:, :], start=True, stop=True).then_inc(w_ok, 1)
            pe.wait_ge(tr_in, 2)
            nc.tensor.matmul(ps[0:N, 2, 0:N], ones[:, 0:N], DG[:, :], start=True, stop=True)
            nc.tensor.matmul(ps[0:N, 2, N:2 * N], ones[:, 0:N], SEL[:, 0:N], start=True, stop=True)
            nc.tensor.transpose(ps[0:N, 3, 0:P], M[:, :], ident[:, :]).then_inc(tr_out, 1)
            pe.wait_ge(tr_in, 3)
            nc.tensor.matmul(ps[0:N, 4, 0:N], ones[:, 0:N], DG[:, :], start=True, stop=True).then_inc(tr_out, 1)
            pe.wait_ge(tr_in, 4)
            nc.tensor.transpose(ps[0:N, 5, 0:N], Zs[:, :], ident[0:N, 0:N]).then_inc(tr_out, 1)
            pe.wait_ge(tr_in, 5)
            nc.tensor.matmul(ps[:, 6, 0:N], QT2[:, :], Z2[:, 0:N], start=True, stop=True)
            nc.tensor.matmul(ps[:, 6, N:2 * N], Z2[:, :], QT2[:, 0:N], start=True, stop=True).then_inc(tr_out, 1)

        @block.vector
        def _(dve):
            done = [0]

            def link(ins):
                done[0] += 1
                ins.then_inc(link_s, 1)
                dve.wait_ge(link_s, done[0])

            v = nc.vector
            dve.wait_ge(made, 5)
            dve.wait_ge(loaded, 64)
            link(v.tensor_copy(pidx_f[:, :], pidx[:, :]))
            link(v.tensor_copy(iota[:, :], iota_i[:, :]))
            link(v.tensor_tensor(ident[:, :], pidx_f[:, :], iota[:, :], ALU.is_equal))
            link(v.tensor_scalar(is_q[:, :], pidx_f[:, 0:1], float(N), -1.0, ALU.is_ge, ALU.mult))
            link(v.memset(neg_id[:, :], 0.0))
            link(v.tensor_scalar(neg_id[0:N, :], ident[0:N, 0:N], -1.0, None, ALU.mult))
            bda, bdw = keep["bd_adjT"], keep["bd_wT"]
            link(v.memset(bda[:, :], 0.0))
            link(v.memset(bdw[:, :], 0.0))
            for half in range(2):
                r = slice(half * N, half * N + N)
                v.tensor_copy(bda[r, r], adjT[r, :])
                link(v.tensor_tensor(bdw[r, r], adjT[r, :], adjT[r, :], ALU.mult))
            link(v.tensor_reduce(sc[:, 5:6], adj[:, :], AX_X, ALU.add))
            link(v.tensor_reduce(sc[:, 6:7], adjT[:, :], AX_X, ALU.add))
            link(v.memset(OH[:, :], 0.0))
            for half in range(2):
                r = slice(half * N, half * N + N)
                link(v.tensor_copy(OH[r, :], ident[r, r]))
            link(v.tensor_tensor_reduce(junk[:, 0, :], adj[:, :], OH[:, :], 1.0, 0.0, ALU.mult, ALU.add, sc[:, 7:8]))
            link(v.tensor_tensor(sc[:, 8:9], sc[:, 5:6], sc[:, 6:7], ALU.add))
            link(v.tensor_tensor(sc[:, 9:10], sc[:, 8:9], sc[:, 7:8], ALU.subtract))
            link(v.tensor_scalar(sc[:, 10:11], sc[:, 9:10], 0.0, None, ALU.is_gt))
            v.tensor_scalar(sc[:, 0:1], sc[:, 9:10], 1e-37, None, ALU.max).then_inc(pw_in, 1)
            dve.wait_ge(pw_out, 1)
            link(v.tensor_tensor(sc[:, 2:3], sc[:, 1:2], sc[:, 10:11], ALU.mult))
            link(v.tensor_scalar(Vr[:, :], OH[:, :], sc[:, 9:10], None, ALU.mult))
            link(v.tensor_tensor(V[:, :], Vr[:, :], adj[:, :], ALU.subtract))
            link(v.tensor_tensor(Wr[:, :], Vr[:, :], adjT[:, :], ALU.subtract))
            link(v.tensor_tensor(MK[:, :], V[:, :], Wr[:, :], ALU.add))
            link(v.tensor_scalar(MK[:, :], MK[:, :], sc[:, 2:3], 0.5, ALU.mult, ALU.mult))
            link(v.tensor_scalar(DG[:, :], ident[0:N, 0:N], sc[0:N, 2:3], None, ALU.mult))
            v.memset(SEL[:, :], 0.0).then_inc(tr_in, 1)
            dve.wait_ge(tr_out, 1)
            link(v.tensor_tensor(M[0:N, :], MK[0:N, :], ps[0:N, 7, 0:N], ALU.mult))
            keep["weights_wait"](dve)
            w = keep["w"]
            link(v.tensor_copy(w["rowsum"][0:1, :].rearrange("p (b n) -> p b n", n=N),
                               ps[0:1, 7, N:2 * N].rearrange("p (o n) -> p o n", o=1).to_broadcast([1, HN // N, N])))
            link(v.tensor_tensor(w["bias"][:, :], w["bias"][:, :], w["bih"][:, :], ALU.add))
            link(v.tensor_copy(M[N:P, :], ident[N:P, N:P]))
            link(v.memset(k1[:, :], 1.0))
            link(v.tensor_scalar(SEL[:, :], pidx_f[0:N, :], 0.0, None, ALU.is_equal))
            v.memset(sc[:, 30:31], 0.0).then_inc(sel_ok, 1)

            STEP = 24
            with dve.Fori(0, steps_k) as k:
                base = dve.snap(k * STEP)
                n = [0]

                def hlink(ins, wait=True):
                    n[0] += 1
                    ins.then_inc(hh, 1)
                    if wait:
                        dve.wait_ge(hh, base + n[0])

                hlink(v.tensor_scalar(OH[:, :], iota[:, 0:N], k1[:, 0:1], None, ALU.is_equal), False)
                hlink(v.tensor_scalar(MK[:, :], iota[:, 0:N], k1[:, 0:1], None, ALU.is_gt))
                dve.wait_ge(row_ok, k + 1)
                hlink(v.tensor_tensor(Vr[:, :], ps[:, 0, 0:N], MK[:, :], ALU.mult), False)
                hlink(v.tensor_tensor_reduce(junk[:, 0, :], ps[:, 0, 0:N], OH[:, :], 1.0, 0.0, ALU.mult, ALU.add,
                                             sc[:, 11:12]))
                hlink(v.tensor_tensor_reduce(junk[:, 1, :], Vr[:, :], Vr[:, :], 1.0, TINY, ALU.mult, ALU.add,
                                             sc[:, 12:13]))
                hlink(v.scalar_tensor_tensor(sc[:, 3:4], sc[:, 11:12], sc[:, 11:12], sc[:, 12:13], ALU.mult,
                                             ALU.add))
                hlink(v.tensor_scalar(sc[:, 13:14], sc[:, 11:12], 0.0, 2.0, ALU.is_ge, ALU.mult))
                v.tensor_scalar(sc[:, 14:15], sc[:, 13:14], -1.0, None, ALU.add).then_inc(n2_ok, 1)
                dve.wait_ge(n2_ok, k + 1)
                dve.wait_ge(nrm_ok, k + 1)
                hlink(v.scalar_tensor_tensor(sc[:, 15:16], sc[:, 4:5], sc[:, 14:15], sc[:, 11:12], ALU.mult,
                                             ALU.add))
                hlink(v.scalar_tensor_tensor(V[:, :], OH[:, :], sc[:, 15:16], Vr[:, :], ALU.mult, ALU.add))
                hlink(v.scalar_tensor_tensor(sc[:, 16:17], sc[:, 15:16], sc[:, 15:16], sc[:, 12:13], ALU.mult,
                                             ALU.add))
                hlink(v.reciprocal(sc[:, 17:18], sc[:, 16:17]), False)
                hlink(v.tensor_scalar(sc[:, 18:19], sc[:, 12:13], 2.0 * TINY, 2.0, ALU.is_gt, ALU.mult))
                hlink(v.tensor_tensor(sc[:, 19:20], sc[:, 17:18], sc[:, 18:19], ALU.mult), False)
                hlink(v.tensor_tensor_reduce(junk[:, 2, :], M[:, :], V[:, :], 1.0, 0.0, ALU.mult, ALU.add,
                                             sc[:, 20:21]))
                hlink(v.tensor_tensor(sc[:, 21:22], sc[:, 20:21], sc[:, 19:20], ALU.mult))
                v.tensor_scalar(DG[:, :], ident[0:N, 0:N], sc[0:N, 21:22], None, ALU.mult).then_inc(dg_ok, 1)
                hlink(v.tensor_tensor_reduce(junk[:, 3, :], V[:, :], neg_id[:, :], 1.0, 0.0, ALU.mult, ALU.add,
                                             sc[:, 22:23]), False)
                hlink(v.tensor_tensor(sc[:, 23:24], sc[:, 21:22], is_q[:, :], ALU.mult))
                dve.wait_ge(w_ok, k + 1)
                hlink(v.tensor_tensor_reduce(junk[:, 4, :], ps[:, 1, 0:N], V[:, :], 1.0, 0.0, ALU.mult, ALU.add,
                                             sc[:, 24:25]))
                hlink(v.tensor_scalar(sc[:, 25:26], sc[:, 24:25], sc[:, 19:20], -0.5, ALU.mult, ALU.mult))
                hlink(v.scalar_tensor_tensor(Wr[:, :], V[:, :], sc[:, 25:26], ps[:, 1, 0:N], ALU.mult, ALU.add))
                hlink(v.tensor_tensor_reduce(junk[:, 5, :], Wr[:, :], neg_id[:, :], 1.0, sc[:, 23:24], ALU.mult,
                                             ALU.add, sc[:, 26:27]), False)
                hlink(v.scalar_tensor_tensor(M[:, :], Wr[:, :], sc[:, 22:23], M[:, :], ALU.mult, ALU.add))
                hlink(v.scalar_tensor_tensor(M[:, :], V[:, :], sc[:, 26:27], M[:, :], ALU.mult, ALU.add), False)
                hlink(v.tensor_scalar(k1[:, :], k1[:, :], 1.0, None, ALU.add))
                v.tensor_scalar(SEL[:, :], pidx_f[0:N, :], k1[0:N, 0:1], -1.0, ALU.subtract, ALU.is_equal).then_inc(sel_ok, 1)
                assert n[0] == STEP, n[0]
            dve.wait_ge(sel_ok, steps_k + 1)

            link(v.tensor_tensor(MK[0:N, :], iota[0:N, 0:N], pidx_f[0:N, 0:N], ALU.subtract))
            link(v.tensor_scalar(MK[0:N, :], MK[0:N, :], -1.0, None, ALU.is_equal))
            link(v.tensor_tensor(SEL[:, 0:N], M[0:N, :], MK[0:N, :], ALU.mult))
            v.tensor_tensor(DG[:, :], M[0:N, :], ident[0:N, 0:N], ALU.mult).then_inc(tr_in, 1)
            dve.wait_ge(tr_out, 2)
            link(v.tensor_copy(D_[:, :], ps[0:N, 2, 0:N]))
            link(v.tensor_copy(E_[:, :], ps[0:N, 2, N:2 * N]))
            link(v.tensor_copy(QT2[:, 0:N], ps[0:N, 3, N:P]))
            link(v.tensor_copy(QT2[:, N:P], ps[0:N, 3, N:P]))
            aE, G, t0 = Vr[0:N, :], V[0:N, :], Wr[0:N, :]
            link(v.scalar_tensor_tensor(aE, E_[:, :], -1.0, E_[:, :], ALU.mult, ALU.max))
            link(v.tensor_tensor(t0, E_[:, :], E_[:, :], ALU.mult))
            link(v.tensor_scalar(nE2[:, :], t0, TINY, -1.0, ALU.max, ALU.mult))
            link(v.tensor_copy(G, aE))
            link(v.tensor_tensor(G[:, 1:N], aE[:, 1:N], aE[:, 0:N - 1], ALU.add))
            link(v.tensor_tensor(t0, D_[:, :], G, ALU.subtract))
            link(v.tensor_reduce(st[:, 0:1], t0, AX_X, ALU.min))
            link(v.tensor_tensor(t0, D_[:, :], G, ALU.add))
            link(v.tensor_reduce(st[:, 1:2], t0, AX_X, ALU.max))
            link(v.tensor_tensor(st[:, 2:3], st[:, 1:2], st[:, 0:1], ALU.subtract))
            link(v.tensor_scalar(st[:, 3:4], st[:, 2:3], 1.002, 1e-6, ALU.mult, ALU.add))
            link(v.scalar_tensor_tensor(st[:, 0:1], st[:, 3:4], -1e-3, st[:, 0:1], ALU.mult, ALU.add))
            link(v.tensor_scalar(st[:, 4:5], st[:, 3:4], 1.0 / (SECTIONS + 1), None, ALU.mult))
            link(v.tensor_scalar(steps[:, :], iota[0:N, 0:SECTIONS], 1.0, None, ALU.add))

            CHAIN = 2 * (N - 1)
            PER = CHAIN + 8
            with dve.Fori(0, PASSES) as it:
                base = dve.snap(it * PER)
                n = [0]

                def mlink(ins):
                    n[0] += 1
                    ins.then_inc(ms, 1)
                    dve.wait_ge(ms, base + n[0])

                mlink(v.tensor_scalar(lam[:, :], steps[:, :], st[:, 4:5], st[:, 0:1], ALU.mult, ALU.add))
                mlink(v.tensor_tensor(DL[:, :, :], col(D_[:, :]).to_broadcast([N, N, SECTIONS]),
                                      lam[:, :].rearrange("p (o f) -> p o f", o=1).to_broadcast([N, N, SECTIONS]),
                                      ALU.subtract))
                for j in range(1, N):
                    mlink(v.reciprocal(rc[:, :], DL[:, j - 1, :]))
                    mlink(v.scalar_tensor_tensor(DL[:, j, :], rc[:, :], nE2[:, j - 1:j], DL[:, j, :], ALU.mult,
                                                 ALU.add))
                mlink(v.tensor_scalar(neg[:, :, :], DL[:, :, :], 0.0, None, ALU.is_lt))
                mlink(v.tensor_reduce(cnt[:, :], neg[:, :, :].rearrange("p k f -> p f k"), AX_X, ALU.add))
                mlink(v.tensor_scalar(lam[:, :], cnt[:, :], pidx_f[0:N, 0:1], None, ALU.is_le))
                mlink(v.tensor_reduce(st[:, 5:6], lam[:, :], AX_X, ALU.add))
                mlink(v.scalar_tensor_tensor(st[:, 0:1], st[:, 5:6], st[:, 4:5], st[:, 0:1], ALU.mult, ALU.add))
                mlink(v.tensor_scalar(st[:, 4:5], st[:, 4:5], 1.0 / (SECTIONS + 1), None, ALU.mult))
                assert n[0] == PER, n[0]
            lamc = st[:, 6:7]
            link(v.scalar_tensor_tensor(lamc, st[:, 4:5], 0.5 * (SECTIONS + 1), st[:, 0:1], ALU.mult, ALU.add))
            v.tensor_scalar(DG[:, :], ident[0:N, 0:N], lamc, None, ALU.mult).then_inc(tr_in, 1)

            K = N - 1
            link(v.tensor_scalar(PD[:, :, 0], D_[:, :], lamc, None, ALU.subtract))
            link(v.tensor_copy(PD[:, :, 1], PD[:, ::-1, 0]))
            link(v.memset(nE2P[:, :, :], 0.0))
            link(v.memset(nEP[:, :, :], 0.0))
            link(v.tensor_copy(nE2P[:, 0:K, 0], nE2[:, 0:K]))
            link(v.tensor_copy(nE2P[:, 0:K, 1], nE2[:, K - 1::-1]))
            link(v.tensor_scalar(nEP[:, 0:K, 0], E_[:, 0:K], -1.0, None, ALU.mult))
            link(v.tensor_copy(nEP[:, 0:K, 1], nEP[:, K - 1::-1, 0]))
            link(v.tensor_copy(QP[:, 0, :], PD[:, 0, :]))
            for k in range(1, N):
                link(v.reciprocal(rc[:, 0:2], QP[:, k - 1, :]))
                link(v.tensor_tensor(rc[:, 2:4], rc[:, 0:2], nE2P[:, k - 1, :], ALU.mult))
                link(v.tensor_tensor(QP[:, k, :], rc[:, 2:4], PD[:, k, :], ALU.add))
            link(v.tensor_scalar(QP[:, :, :], QP[:, :, :], 1e30, -1e30, ALU.min, ALU.max))
            link(v.reciprocal(RP[:, :, :], QP[:, :, :]))
            link(v.tensor_scalar(RP[:, :, :], RP[:, :, :], 1e30, -1e30, ALU.min, ALU.max))
            link(v.tensor_tensor(RP[:, :, :], RP[:, :, :], nEP[:, :, :], ALU.mult))
            link(v.tensor_tensor(gam[:, :], QP[:, :, 0], QP[:, ::-1, 1], ALU.add))
            link(v.tensor_tensor(gam[:, :], gam[:, :], PD[:, :, 0], ALU.subtract))
            link(v.scalar_tensor_tensor(gam[:, :], gam[:, :], -1.0, gam[:, :], ALU.mult, ALU.max))
            link(v.tensor_reduce(st[:, 7:8], gam[:, :], AX_X, ALU.min))
            link(v.tensor_scalar(dlt[:, :], gam[:, :], st[:, 7:8], None, ALU.is_le))
            link(v.tensor_copy(ZP[:, :, 0], dlt[:, :]))
            link(v.tensor_copy(ZP[:, :, 1], dlt[:, ::-1]))
            for j in range(K - 1, -1, -1):
                link(v.tensor_tensor(rc[:, 0:2], RP[:, j, :], ZP[:, j + 1, :], ALU.mult))
                link(v.tensor_tensor(ZP[:, j, :], rc[:, 0:2], ZP[:, j, :], ALU.add))
            link(v.tensor_tensor(Z[:, :], ZP[:, :, 0], ZP[:, ::-1, 1], ALU.add))
            link(v.tensor_tensor(Z[:, :], Z[:, :], dlt[:, :], ALU.subtract))
            v.tensor_tensor_reduce(gam[:, :], Z[:, :], Z[:, :], 1.0, 0.0, ALU.mult, ALU.add,
                                   st[:, 10:11]).then_inc(pw_in, 1)
            dve.wait_ge(pw_out, 2)
            link(v.tensor_scalar(Z[:, :], Z[:, :], st[:, 11:12], None, ALU.mult))

            chains = [(15, -1, 16, 15), (16, 1, 16, 15), (31, -1, 32, 31), (32, 1, 32, 31), (47, -1, 16, 47),
                      (48, 1, 16, 47)]
            link(v.memset(BD[:, :, :], 1.0))
            link(v.memset(BE[:, :, :], 0.0))
            link(v.memset(BZ[:, :, :], 0.0))
            link(v.memset(BC[:, 0, :], 1.0))
            link(v.tensor_tensor(gam[:, :], Z[:, :], Z[:, :], ALU.mult))
            for c, (start, way, size, seam) in enumerate(chains):
                last = start + way * (size - 1)
                if way > 0:
                    el = slice(start, start + size)
                    ce = slice(start, start + size - 1)
                else:
                    el = slice(start, last - 1 if last else None, -1)
                    ce = slice(start - 1, last - 1 if last else None, -1)
                v.tensor_copy(BD[:, 0:size, c], PD[:, el, 0])
                v.tensor_copy(BE[:, 0:size - 1, c], E_[:, ce])
                link(v.tensor_copy(BZ[:, 0:size, c], gam[:, el]))
                link(v.tensor_tensor(BD[:, 0, c:c + 1], BD[:, 0, c:c + 1], aE[:, seam:seam + 1], ALU.subtract))
            link(v.tensor_tensor(BE2[:, :, :], BE[:, :, :], BE[:, :, :], ALU.mult))
            for j in range(1, 32):
                link(v.reciprocal(rc[:, 0:6], BD[:, j - 1, :]))
                link(v.tensor_tensor(rc[:, 6:12], rc[:, 0:6], BE2[:, j - 1, :], ALU.mult))
                link(v.tensor_tensor(BD[:, j, :], BD[:, j, :], rc[:, 6:12], ALU.subtract))
            link(v.reciprocal(BM[:, :, :], BD[:, :, :]))
            link(v.tensor_tensor(BM[:, :, :], BM[:, :, :], BE[:, :, :], ALU.mult))
            for j in range(1, 32):
                link(v.tensor_tensor(BC[:, j, :], BC[:, j - 1, :], BM[:, j - 1, :], ALU.mult))
            link(v.tensor_tensor(BC[:, :, :], BC[:, :, :], BC[:, :, :], ALU.mult))
            link(v.tensor_reduce(st[:, 20:26], BZ[:, :, :].rearrange("p j c -> p c j"), AX_X, ALU.max))
            link(v.tensor_tensor(BM[:, :, :], BZ[:, :, :],
                                 st[:, 20:26].rearrange("p (o c) -> p o c", o=1).to_broadcast([N, 32, 6]),
                                 ALU.is_ge))
            link(v.tensor_tensor(BM[:, :, :], BM[:, :, :], BZ[:, :, :], ALU.mult))
            link(v.tensor_tensor(BM[:, :, :], BM[:, :, :], BC[:, :, :], ALU.mult))
            link(v.tensor_reduce(st[:, 26:32], BM[:, :, :].rearrange("p j c -> p c j"), AX_X, ALU.add))
            mx = st[:, 20:26].rearrange("p (b s) -> p b s", s=2)
            q2 = st[:, 26:32].rearrange("p (b s) -> p b s", s=2)
            low_side, q_at = st[:, 32:35], st[:, 35:38]
            link(v.tensor_tensor(low_side, mx[:, :, 0], mx[:, :, 1], ALU.is_ge))
            link(v.tensor_tensor(q_at, q2[:, :, 0], q2[:, :, 1], ALU.subtract))
            link(v.tensor_tensor(q_at, q_at, low_side, ALU.mult))
            link(v.tensor_tensor(q_at, q_at, q2[:, :, 1], ALU.add))
            eb = E_[:, 15:48:16]
            r_at, r2 = st[:, 38:41], st[:, 42:45]
            link(v.tensor_scalar(st[:, 45:48], eb, 0.0, 2.0, ALU.is_ge, ALU.mult))
            link(v.tensor_scalar(st[:, 45:48], st[:, 45:48], -1.0, None, ALU.add))
            link(v.tensor_tensor(r2, st[:, 45:48], Z[:, 16:49:16], ALU.mult))
            link(v.tensor_tensor(r_at, r2, Z[:, 15:48:16], ALU.add))
            link(v.tensor_reduce(st[:, 48:49], Z[:, 0:N:16], AX_X, ALU.add))
            link(v.tensor_scalar(st[:, 41:42], st[:, 48:49], -1.0, None, ALU.mult))
            dve.wait_ge(tr_out, 3)
            link(v.tensor_copy(dlt[:, :], ps[0:N, 4, 0:N]))
            link(v.tensor_tensor(dlt[:, :], dlt[:, :], dlt[:, :], ALU.mult))
            link(v.tensor_reduce(st[:, 49:50], dlt[:, :], AX_X, ALU.max))
            link(v.tensor_scalar(st[:, 50:51], st[:, 49:50], (8 * 2.0 ** -24) ** 2, None, ALU.mult))
            link(v.tensor_tensor(r2, r_at, r_at, ALU.mult))
            link(v.tensor_scalar(r2, r2, 1e-8, None, ALU.is_gt))
            link(v.tensor_tensor(st[:, 51:54], eb, eb, ALU.mult))
            link(v.tensor_tensor(st[:, 51:54], st[:, 51:54], q_at, ALU.mult))
            link(v.tensor_scalar(st[:, 51:54], st[:, 51:54], 2.0, st[:, 50:51], ALU.mult, ALU.is_gt))
            link(v.tensor_tensor(r2, r2, st[:, 51:54], ALU.max))
            sg = st[:, 54:58]
            link(v.tensor_scalar(sg, st[:, 38:42], 0.0, -2.0, ALU.is_ge, ALU.mult))
            link(v.tensor_scalar(sg, sg, 1.0, None, ALU.add))
            leaf, s15, s31, s47 = sg[:, 3:4], sg[:, 0:1], sg[:, 1:2], sg[:, 2:3]
            k15, k31, k47 = r2[:, 0:1], r2[:, 1:2], r2[:, 2:3]

            def choose(out, flag, yes, no):
                link(v.tensor_tensor(st[:, 62:63], yes, no, ALU.subtract))
                link(v.scalar_tensor_tensor(out, st[:, 62:63], flag, no, ALU.mult, ALU.add))

            choose(st[:, 58:59], k15, s15, leaf)
            choose(st[:, 59:60], k47, s47, leaf)
            choose(st[:, 60:61], low_side[:, 1:2], st[:, 58:59], st[:, 59:60])
            choose(st[:, 61:62], k31, s31, st[:, 60:61])
            v.tensor_scalar(Zs[:, :], Z[:, :], st[:, 61:62], None, ALU.mult).then_inc(tr_in, 1)
            dve.wait_ge(tr_out, 4)
            link(v.tensor_copy(Z2[:, 0:N], ps[0:N, 5, 0:N]))
            v.tensor_copy(Z2[:, N:P], ps[0:N, 5, 0:N]).then_inc(tr_in, 1)
            dve.wait_ge(tr_out, 5)
            bdu, bdut = keep["bd_U"], keep["bd_UT"]
            link(v.memset(bdu[:, :], 0.0))
            link(v.memset(bdut[:, :], 0.0))
            for half in range(2):
                r = slice(half * N, half * N + N)
                link(v.tensor_copy(bdu[r, r], ps[r, 6, 0:N]))
                link(v.tensor_copy(bdut[r, r], ps[r, 6, N:2 * N]))


def col(ap):
    return ap.rearrange("p (n o) -> p n o", o=1)


def settle(eng, passed):
    eng.sem_inc(passed, 1)


def layer_norm(nc, eng, link, ln, half, src, dst, turn, stats, mv, var, rstd, var_ready, rstd_ready, passed):
    v = nc.vector
    for t in range(HALF):
        ins = v.bn_stats(stats[:, t, :], src[:, t, :])
    link(ins)
    settle(eng, passed)
    for t in range(HALF):
        ins = v.bn_aggr(mv[:, t, :], stats[:, t, :])
    link(ins)
    v.tensor_scalar(var[:, :], mv[:, :, 1], LN_EPS, None, ALU.add).then_inc(var_ready, 1)
    eng.wait_ge(rstd_ready, turn * ln[1] + (ln[0] + 1))
    ln[0] += 1
    for t in range(HALF):
        ins = v.tensor_scalar(dst[:, t, :], src[:, t, :], mv[:, t, 0:1], rstd[:, t:t + 1], ALU.subtract, ALU.mult)
    return ins


def lstm_units():
    units = [(1, tile, 0, fc) for tile in range(2) for fc in range(2)]
    for p in range(2, MAX_SKIP + 1):
        units += [(p, 0, step, fc) for step in range(p) for fc in range(2)]
    return units


UNITS = lstm_units()
FIRST_UNIT = {p: min(u for u, x in enumerate(UNITS) if x[0] == p) for p in range(1, MAX_SKIP + 1)}


def gates_of(step):
    return (0, 2, 3) if step == 0 else (0, 2, 1, 3)


def f_count(u):
    return sum(1 for x in UNITS[:u] if x[2] > 0)


def windows(buf, kc, p, tile, step):
    if p == 1:
        return buf[:, kc, tile * 512:(tile + 1) * 512]
    nw = T // p
    return buf[:, kc, :].rearrange("q (b t) -> q b t", t=T)[:, :, step:step + (nw - 1) * p + 1:p]


def width(p):
    return 512 if p == 1 else GB * (T // p)


def cells(ap, p):
    w = ap[:, 0:width(p)]
    return w if p == 1 else w.rearrange("q (b w) -> q b w", b=GB)


def layers_0_1(nc, dram, keep):
    with ExitStack() as ctx:
        def sb(name, shape, dt=F32):
            return ctx.enter_context(nc.sbuf_tensor(name, shape, dt))

        def sem(name):
            return ctx.enter_context(nc.semaphore(name))

        w = keep["w"]
        ps = ctx.enter_context(nc.psum_tensor("ps_a", [P, 8, 512], F32))
        X = sb("a_x", [P, TILES, D])
        XR = sb("a_xr", [P, TILES, D])
        AXT = sb("a_axt", [P, 2, GT])
        Y = sb("a_y", [P, TILES, D])
        arena = sb("a_arena", [P, 16384])
        H1T = arena[:, 0:2048].rearrange("p (c n) -> p c n", c=2)
        HT = arena[:, 2048:4096].rearrange("p (c n) -> p c n", c=2)
        HB = arena[:, 4096:6144].rearrange("p (c n) -> p c n", c=2)
        GATE = arena[:, 6144:10240].rearrange("p (f g n) -> p f g n", f=2, g=4)
        C = arena[:, 10240:11264].rearrange("p (f n) -> p f n", f=2)
        HS = arena[:, 11264:13312].rearrange("p (s f n) -> p s f n", s=2, f=2)
        TMP = arena[:, 13312:13824]
        S1 = arena[:, 0:4096].rearrange("p (t n) -> p t n", t=TILES)
        WS = arena[:, 4096:8192].rearrange("p (h c n) -> p h c n", h=2, c=4)
        S2 = arena[:, 8192:16384].rearrange("p (h c n) -> p h c n", h=2, c=8)
        stats = sb("a_stats", [P, HALF, 6])
        mv = sb("a_mv", [P, HALF, 2])
        var = sb("a_var", [P, HALF])
        rstd = sb("a_rstd", [P, HALF])
        mhalf = sb("a_mhalf", [P, HALF])
        ident, bda, bdw = keep["ident"], keep["bd_adjT"], keep["bd_wT"]

        x_in = sem("x_loaded")
        ax_ps, ax_sb = sem("ax_ps"), sem("ax_sb")
        h1_ps, h1_sb = sem("h1_ps"), sem("h1_sb")
        y_ps, y_sb = sem("y_ps"), sem("y_sb")
        h2_ps, h2_sb = sem("h2_ps"), sem("h2_sb")
        xpart = sem("lstm_x_read")
        gates_ps = sem("gates_ps")
        ig_sb, f_sb, o_sb = sem("ig_sb"), sem("f_sb"), sem("o_sb")
        c_sb = sem("c_sb")
        tc_sb = sem("tanh_c_sb")
        h_sb = sem("h_sb")
        ht_ps = sem("h_tokens_ps")
        x1_sb = sem("x1_sb")
        wx_ps, wx_sb = sem("wx_ps"), sem("wx_sb")
        s1_ps, s1_sb = sem("s1_ps"), sem("s1_sb")
        ws_ps, ws_act, ws_dve = sem("ws_ps"), sem("ws_act"), sem("ws_dve")
        s2_ps, s2_act, s2_dve = sem("s2_ps"), sem("s2_act"), sem("s2_dve")
        y3_ps, y3_sb = sem("y3_ps"), sem("y3_sb")
        x2_ps, x2_sb = sem("x2_ps"), sem("x2_sb")
        var_ready, rstd_ready = sem("var_ready"), sem("rstd_ready")
        stored = sem("x2_stored")
        dve_passed = sem("a_dve_passed")
        own = sem("dve_own")
        const = sem("a_const")
        NU = len(UNITS)
        NF = f_count(NU)
        LN_CALLS = 4

        block = ctx.enter_context(nc.Block())

        @block.sync
        def _(sp):
            src = dram["x"].rearrange("(g t p) d -> g p t d", p=P, t=TILES)
            dst = dram["x2"].rearrange("(g t p) d -> g p t d", p=P, t=TILES)
            sp.sem_inc(stored, 16)
            sp.dma_start(X[:, :, :], src[0]).then_inc(x_in, 16)
            for g in range(NGRP):
                if g + 1 < NGRP:
                    sp.wait_ge(x1_sb, 2 * (g + 1))
                    sp.dma_start(X[:, :, :], src[g + 1]).then_inc(x_in, 16)
                sp.wait_ge(x2_sb, 2 * (g + 2))
                sp.dma_start(dst[g], XR[:, :, :]).then_inc(stored, 16)
            sp.wait_ge(stored, 16 * (NGRP + 1))

        @block.gpsimd
        def _(pool):
            nc.gpsimd.memset(mhalf[:, :], -0.5).then_inc(const, 1)
            pool.wait_ge(const, 1)
            with pool.Fori(0, NGRP * LN_CALLS) as n:
                pool.wait_ge(var_ready, n + 1)
                nc.gpsimd.tensor_tensor(rstd[:, :], var[:, :], mhalf[:, :], ALU.pow).then_inc(rstd_ready, 1)

        @block.tensor
        def _(pe):
            mm = nc.tensor.matmul

            def mix_nodes(h, src, fcs, banks, mat, tok):
                for c in range(fcs):
                    for t in range(HALF):
                        last = mm(ps[:, banks + c, t * P:(t + 1) * P], src[:, tok + t, c * P:(c + 1) * P], mat[:, :],
                                  start=True, stop=True)
                return last

            keep["weights_wait"](pe)
            with pe.Fori(0, NGRP) as i:
                pe.wait_ge(x_in, i * 16 + 16)
                for h in range(2):
                    mix_nodes(h, X, 2, 4 * h, bda, 4 * h).then_inc(ax_ps, 1)
                pe.wait_ge(x2_sb, i * 2 + 2)
                for h in range(2):
                    pe.wait_ge(ax_sb, i * 2 + (h + 1))
                    for oc in range(2):
                        o = ps[:, 4 * h + 2 + oc, :]
                        mm(o, w["bg0"][0:1, oc * P:(oc + 1) * P], w["rowsum"][0:1, :], start=True, stop=False)
                        for kc in range(2):
                            last = mm(o, w["Wg0"][:, kc, oc * P:(oc + 1) * P], AXT[:, kc, h * HN:(h + 1) * HN],
                                      start=False, stop=(kc == 1))
                    last.then_inc(h1_ps, 1)
                for h in range(2):
                    pe.wait_ge(h1_sb, i * 2 + (h + 1))
                    for t in range(HALF):
                        for kc in range(2):
                            last = mm(ps[:, 4 * h + t // 2, (t % 2) * D:(t % 2 + 1) * D],
                                      H1T[:, kc, (4 * h + t) * P:(4 * h + t + 1) * P], w["Wg1"][:, kc, :],
                                      start=(kc == 0), stop=(kc == 1))
                    last.then_inc(y_ps, 1)
                for h in range(2):
                    pe.wait_ge(y_sb, i * 2 + (h + 1))
                    mix_nodes(h, Y, 2, 4 * h + 2, bda, 4 * h).then_inc(h2_ps, 1)
                pe.wait_ge(h2_sb, i * 2 + 2)
                for u, (p, tile, step, fc) in enumerate(UNITS):
                    if u >= 2:
                        pe.wait_ge(o_sb, i * NU + (u - 1))
                    if p > 1 and step == 0 and fc == 0:
                        pe.wait_ge(h_sb, i * NU + u)
                    src = HT if p == 1 else HB
                    n = width(p)
                    for g in gates_of(step):
                        for kc in range(2):
                            last = mm(ps[:, 4 * fc + g, 0:n],
                                      w["Wih"][:, p - 1, kc, g * D + fc * P:g * D + (fc + 1) * P],
                                      windows(src, kc, p, tile, step), start=(kc == 0),
                                      stop=(step == 0 and kc == 1))
                    if step > 0:
                        last.then_inc(xpart, 1)
                        if fc == 0:
                            pe.wait_ge(h_sb, i * NU + u)
                        for g in gates_of(step):
                            for kc in range(2):
                                last = mm(ps[:, 4 * fc + g, 0:n],
                                          w["Whh"][:, p - 2, kc, g * D + fc * P:g * D + (fc + 1) * P],
                                          HS[:, (step - 1) % 2, kc, 0:n], start=False, stop=(kc == 1))
                    last.then_inc(gates_ps, 1)
                pe.wait_ge(h_sb, i * NU + NU)
                for h in range(2):
                    for t in range(HALF):
                        for fc in range(2):
                            last = nc.tensor.transpose(
                                ps[:, 4 * h + t // 2, (t % 2) * D + fc * P:(t % 2) * D + (fc + 1) * P],
                                HB[:, fc, (4 * h + t) * P:(4 * h + t + 1) * P], ident[:, :])
                    last.then_inc(ht_ps, 1)
                for h in range(2):
                    pe.wait_ge(x1_sb, i * 2 + (h + 1))
                    mix_nodes(h, XR, 2, 4 * h + 2, bdw, 4 * h).then_inc(wx_ps, 1)
                for h in range(2):
                    pe.wait_ge(wx_sb, i * 2 + (h + 1))
                    for t in range(HALF):
                        for kc in range(2):
                            last = mm(ps[:, 4 * h + t, :], AXT[:, kc, (4 * h + t) * P:(4 * h + t + 1) * P],
                                      w["W1"][:, kc, :], start=(kc == 0), stop=(kc == 1))
                    last.then_inc(s1_ps, 1)
                for h in range(2):
                    pe.wait_ge(s1_sb, i * 2 + (h + 1))
                    mix_nodes(h, S1, 4, 4 * h, bdw, 4 * h).then_inc(ws_ps, 1)
                for h in range(2):
                    pe.wait_ge(ws_act, i * 2 + (h + 1))
                    pe.wait_ge(ws_dve, i * 2 + (h + 1))
                    for oc in range(8):
                        if oc >= 4:
                            if oc % 2 == 0:
                                pe.wait_ge(s2_act, i * 8 + (4 * h + (oc - 4) // 2 + 1))
                            else:
                                pe.wait_ge(s2_dve, i * 8 + (4 * h + (oc - 4) // 2 + 1))
                        for kc in range(4):
                            last = mm(ps[:, 4 * h + oc % 4, :], w["W2"][:, kc, oc * P:(oc + 1) * P],
                                      WS[:, h, kc, :], start=(kc == 0), stop=(kc == 3))
                        last.then_inc(s2_ps, 1)
                for h in range(2):
                    pe.wait_ge(s2_act, i * 8 + (4 * h + 4))
                    pe.wait_ge(s2_dve, i * 8 + (4 * h + 4))
                    for t in range(HALF):
                        for kc in range(8):
                            last = mm(ps[:, 4 * h + t // 2, (t % 2) * D:(t % 2 + 1) * D],
                                      S2[:, h, kc, t * P:(t + 1) * P], w["W3"][:, kc, :], start=(kc == 0),
                                      stop=(kc == 7))
                    last.then_inc(y3_ps, 1)
                for h in range(2):
                    pe.wait_ge(y3_sb, i * 2 + (h + 1))
                    for u in range(2):
                        last = mm(ps[:, 4 * h + 2 + u, :], bdw[:, :], Y[:, 4 * h + 2 * u:4 * h + 2 * u + 2, :],
                                  start=True, stop=True)
                    last.then_inc(x2_ps, 1)

        @block.scalar
        def _(act):
            a = nc.scalar.activation
            keep["weights_wait"](act)
            with act.Fori(0, NGRP) as i:
                for h in range(2):
                    act.wait_ge(ax_ps, i * 2 + (h + 1))
                    a(AXT[:, :, h * HN:(h + 1) * HN], ps[:, 4 * h:4 * h + 2, :], ACT.Copy).then_inc(ax_sb, 1)
                for h in range(2):
                    act.wait_ge(h1_ps, i * 2 + (h + 1))
                    a(H1T[:, :, h * HN:(h + 1) * HN], ps[:, 4 * h + 2:4 * h + 4, :], ACT.Relu).then_inc(h1_sb, 1)
                for h in range(2):
                    act.wait_ge(h2_ps, i * 2 + (h + 1))
                    a(HT[:, :, h * HN:(h + 1) * HN], ps[:, 4 * h + 2:4 * h + 4, :], ACT.Relu).then_inc(h2_sb, 1)
                for u, (p, tile, step, fc) in enumerate(UNITS):
                    n = width(p)
                    act.wait_ge(gates_ps, i * NU + (u + 1))
                    if u >= 2:
                        act.wait_ge(h_sb, i * NU + (u - 1))

                    def gate(g, func):
                        b = (p - 1) * 8 + 2 * g + fc
                        return a(GATE[:, fc, g, 0:n], ps[:, 4 * fc + g, 0:n], func, bias=w["bias"][:, b:b + 1])

                    gate(0, ACT.Sigmoid)
                    gate(2, ACT.Tanh).then_inc(ig_sb, 1)
                    if step > 0:
                        gate(1, ACT.Sigmoid).then_inc(f_sb, 1)
                    gate(3, ACT.Sigmoid).then_inc(o_sb, 1)
                    act.wait_ge(c_sb, i * NU + (u + 1))
                    a(GATE[:, fc, 2, 0:n], C[:, fc, 0:n], ACT.Tanh).then_inc(tc_sb, 1)
                for h in range(2):
                    act.wait_ge(wx_ps, i * 2 + (h + 1))
                    a(AXT[:, :, h * HN:(h + 1) * HN], ps[:, 4 * h + 2:4 * h + 4, :], ACT.Copy).then_inc(wx_sb, 1)
                for h in range(2):
                    act.wait_ge(s1_ps, i * 2 + (h + 1))
                    a(S1[:, 4 * h:4 * h + 4, :], ps[:, 4 * h:4 * h + 4, :], ACT.Relu).then_inc(s1_sb, 1)
                for h in range(2):
                    act.wait_ge(ws_ps, i * 2 + (h + 1))
                    a(WS[:, h, 0:2, :], ps[:, 4 * h:4 * h + 2, :], ACT.Copy).then_inc(ws_act, 1)
                for h in range(2):
                    for oc in range(0, 8, 2):
                        act.wait_ge(s2_ps, i * 16 + (8 * h + oc + 1))
                        a(S2[:, h, oc, :], ps[:, 4 * h + oc % 4, :], ACT.Relu).then_inc(s2_act, 1)
                for h in range(2):
                    act.wait_ge(y3_ps, i * 2 + (h + 1))
                    a(Y[:, 4 * h:4 * h + 4, :], ps[:, 4 * h:4 * h + 2, :], ACT.Copy).then_inc(y3_sb, 1)

        @block.vector
        def _(dve):
            v = nc.vector
            keep["weights_wait"](dve)
            per = keep["dve_links_a"]
            v.memset(var[:, :], 0.0).then_inc(x2_sb, 2)
            with dve.Fori(0, NGRP) as i:
                turn = dve.snap(i * per)
                n_own = [0]
                ln = [0, LN_CALLS]

                def link(ins):
                    n_own[0] += 1
                    ins.then_inc(own, 1)
                    dve.wait_ge(own, turn + n_own[0])

                for h in range(2):
                    dve.wait_ge(y_ps, i * 2 + (h + 1))
                    v.tensor_tensor(Y[:, 4 * h:4 * h + 4, :],
                                    ps[:, 4 * h:4 * h + 2, :].rearrange("p b (t n) -> p (b t) n", n=D),
                                    across(w["bg1"], HALF), ALU.add).then_inc(y_sb, 1)
                for u, (p, tile, step, fc) in enumerate(UNITS):
                    n = width(p)
                    g = [GATE[:, fc, q, 0:n] for q in range(4)]
                    c = C[:, fc, 0:n]
                    dve.wait_ge(ig_sb, i * NU + (u + 1))
                    if step == 0:
                        v.tensor_tensor(c, g[0], g[2], ALU.mult).then_inc(c_sb, 1)
                    else:
                        v.tensor_tensor(TMP[:, 0:n], g[0], g[2], ALU.mult)
                        dve.wait_ge(f_sb, i * NF + (f_count(u) + 1))
                        link(v.tensor_tensor(c, g[1], c, ALU.mult))
                        v.tensor_tensor(c, c, TMP[:, 0:n], ALU.add).then_inc(c_sb, 1)
                    last_step = step == p - 1
                    if last_step:
                        out = windows(HB, fc, p, tile, step)
                        if step > 0 and fc == 0:
                            dve.wait_ge(xpart, i * NF + (f_count(u) + 2))
                    else:
                        out = cells(HS[:, step % 2, fc, :], p)
                    dve.wait_ge(tc_sb, i * NU + (u + 1))
                    v.tensor_tensor(out, cells(g[3], p), cells(g[2], p), ALU.mult).then_inc(h_sb, 1)
                for h in range(2):
                    dve.wait_ge(ht_ps, i * 2 + (h + 1))
                    if h == 0:
                        keep["wait_stored"](dve, stored, i)
                    ins = v.tensor_tensor(XR[:, 4 * h:4 * h + 4, :], X[:, 4 * h:4 * h + 4, :],
                                          ps[:, 4 * h:4 * h + 2, :].rearrange("p b (t n) -> p (b t) n", n=D),
                                          ALU.add)
                    link(ins)
                    layer_norm(nc, dve, link, ln, h, XR[:, 4 * h:4 * h + 4, :], XR[:, 4 * h:4 * h + 4, :], i, stats,
                               mv, var, rstd, var_ready, rstd_ready, dve_passed).then_inc(x1_sb, 1)
                for h in range(2):
                    dve.wait_ge(ws_ps, i * 2 + (h + 1))
                    v.tensor_copy(WS[:, h, 2:4, :], ps[:, 4 * h + 2:4 * h + 4, :]).then_inc(ws_dve, 1)
                for h in range(2):
                    for oc in range(1, 8, 2):
                        dve.wait_ge(s2_ps, i * 16 + (8 * h + oc + 1))
                        v.tensor_scalar(S2[:, h, oc, :], ps[:, 4 * h + oc % 4, :], 0.0, None, ALU.max)\
                            .then_inc(s2_dve, 1)
                for h in range(2):
                    dve.wait_ge(x2_ps, i * 2 + (h + 1))
                    link(v.tensor_tensor(XR[:, 4 * h:4 * h + 4, :], XR[:, 4 * h:4 * h + 4, :],
                                         ps[:, 4 * h + 2:4 * h + 4, :].rearrange("p b (t n) -> p (b t) n", n=D),
                                         ALU.add))
                    layer_norm(nc, dve, link, ln, h, XR[:, 4 * h:4 * h + 4, :], XR[:, 4 * h:4 * h + 4, :], i, stats,
                               mv, var, rstd, var_ready, rstd_ready, dve_passed).then_inc(x2_sb, 1)
                assert n_own[0] == per, n_own[0]


def across(row, n):
    return row[:, :].rearrange("p (o d) -> p o d", o=1).to_broadcast([P, n, D])


def layers_2_3(nc, dram, keep):
    N = T
    CH = EDGES // P
    ROWS = GB * HEADS
    with ExitStack() as ctx:
        def sb(name, shape, dt=F32):
            return ctx.enter_context(nc.sbuf_tensor(name, shape, dt))

        def sem(name):
            return ctx.enter_context(nc.semaphore(name))

        ps = ctx.enter_context(nc.psum_tensor("ps_b", [P, 8, 512], F32))
        ident, bdu, bdut = keep["ident"], keep["bd_U"], keep["bd_UT"]
        W1 = sb("b_W1", [P, 2, 128])
        b1 = sb("b_b1", [P, 1])
        W2 = sb("b_W2", [P, D])
        b2 = sb("b_b2", [P, D])
        Wlv = sb("b_Wlv", [P, 2, 2 * D])
        Wout = sb("b_Wout", [P, 2, D])
        APAD = sb("b_apad", [P, 2, 2 * ROWS - HEADS])
        adjT = sb("b_adjT", [N, N])
        src_i = sb("b_src_i", [P, EDGES], I32)
        dst_i = sb("b_dst_i", [P, EDGES], I32)
        src_f = sb("b_src_f", [P, EDGES])
        dst_f = sb("b_dst_f", [P, EDGES])
        ecol_i = sb("b_ecol_i", [P, 2, CH], I32)
        ecol = sb("b_ecol", [P, 2, CH])
        node_i = sb("b_node_i", [P, 1], I32)
        node = sb("b_node", [P, 1])
        col_i = sb("b_col_i", [P, P], I32)
        colm = sb("b_colm", [P, P])
        SRC = sb("b_src1h", [P, EDGES])
        DST = sb("b_dst1h", [P, EDGES])
        GS = sb("b_gs", [P, EDGES])
        SRCT = sb("b_srcT", [P, CH, N])
        DSTT = sb("b_dstT", [P, CH, P])
        NEG = sb("b_neg", [ROWS, N, EDGES], BF16)
        LOGA = sb("b_loga", [ROWS, EDGES])
        ones = sb("b_ones", [N, ROWS])
        eps = sb("b_eps", [ROWS, 1])
        X = sb("b_x", [P, TILES, D])
        XR = sb("b_xr", [P, TILES, D])
        FT = sb("b_ft", [P, 2, GT])
        HT = sb("b_ht", [P, GT])
        Y = sb("b_y", [P, TILES, D])
        QV = sb("b_qv", [P, TILES, 2 * D])
        ABS = sb("b_abs", [P, 2, EDGES])
        LR = sb("b_lrelu", [P, 2, 2, EDGES])
        ES = sb("b_es", [ROWS, EDGES])
        EX = sb("b_ex", [ROWS, EDGES])
        JUNK = 8
        mjunk = sb("b_mjunk", [ROWS, JUNK, EDGES], BF16)
        m = sb("b_m", [ROWS, N])
        mT = sb("b_mT", [N, ROWS])
        EXT = sb("b_ext", [P, CH, ROWS])
        RD = sb("b_rd", [N, ROWS])
        AT = sb("b_at", [P, CH, ROWS])
        PRO = sb("b_pro", [P, 2, CH, 8, N])
        PT = sb("b_pt", [P, 2, HEADS, N])
        YT = sb("b_yt", [P, 2, GT])
        stats = sb("b_stats", [P, HALF, 6])
        mv = sb("b_mv", [P, HALF, 2])
        var = sb("b_var", [P, HALF])
        rstd = sb("b_rstd", [P, HALF])
        mhalf = sb("b_mhalf", [P, HALF])

        w_in = sem("b_weights")
        const = sem("b_const")
        prep = sem("b_prep")
        aa_in, aa_ps, z_in, z_ps, loga_sb = sem("aa_in"), sem("aa_ps"), sem("z_in"), sem("z_ps"), sem("loga_sb")
        x_in = sem("b_x_loaded")
        ux_ps, ux_sb = sem("ux_ps"), sem("ux_sb")
        hid_ps, hid_sb = sem("hid_ps"), sem("hid_sb")
        o2_ps, o2_sb = sem("o2_ps"), sem("o2_sb")
        x3_ps, x3_sb = sem("x3_ps"), sem("x3_sb")
        xt_ps, xt_sb = sem("xt_ps"), sem("xt_sb")
        qv_ps, qv_sb = sem("qv_ps"), sem("qv_sb")
        pair_ps, abs_sb, lr_sb = sem("pair_ps"), sem("abs_sb"), sem("lr_sb")
        score_ps = sem("score_ps")
        m_sb, mT_ps, mT_sb, mg_ps, d_sb, ex_sb = (sem("m_sb"), sem("mT_ps"), sem("mT_sb"), sem("mg_ps"), sem("d_sb"),
                                                  sem("ex_sb"))
        ext_ps, ext_sb, den_ps, rd_sb, rg_ps, at_sb = (sem("ext_ps"), sem("ext_sb"), sem("den_ps"), sem("rd_sb"),
                                                       sem("rg_ps"), sem("at_sb"))
        pro_sb, pt_ps, pt_sb, yt_ps, yt_sb = sem("pro_sb"), sem("pt_ps"), sem("pt_sb"), sem("yt_ps"), sem("yt_sb")
        fin_ps, fin_sb = sem("fin_ps"), sem("fin_sb")
        var_ready, rstd_ready = sem("b_var_ready"), sem("b_rstd_ready")
        stored = sem("out_stored")
        dve_passed, pe_passed = sem("b_dve_passed"), sem("b_pe_passed")
        own = sem("b_dve_own")
        LN_CALLS = 4
        block = ctx.enter_context(nc.Block())

        @block.sync
        def _(sp):
            src = dram["x2"].rearrange("(g t p) d -> g p t d", p=P, t=TILES)
            dst = dram["out"].rearrange("(g t p) d -> g p t d", p=P, t=TILES)
            sp.sem_inc(stored, 16)
            two = [(src_i, "src"), (dst_i, "dst")]
            for tile, name in two:
                sp.dma_start(tile[:, :], dram[name].rearrange("(o e) -> o e", o=1).to_broadcast([P, EDGES]))\
                    .then_inc(w_in, 16)
            for q, name in enumerate(("src", "dst")):
                sp.dma_start(ecol_i[:, q, :], dram[name + "_col"]).then_inc(w_in, 16)
            sp.dma_start(adjT[:, :], dram["adjT"]).then_inc(w_in, 16)
            sp.dma_start(W1[:, :, :], dram["L2_W1"].rearrange("(c p) n -> p c n", p=P)).then_inc(w_in, 16)
            sp.dma_start(b1[:, :], dram["L2_b1"].rearrange("(p o) -> p o", o=1)).then_inc(w_in, 16)
            sp.dma_start(W2[:, :], dram["L2_W2"]).then_inc(w_in, 16)
            sp.dma_start(b2[:, :], dram["L2_b2"].rearrange("(o d) -> o d", o=1).to_broadcast([P, D])).then_inc(w_in, 16)
            for q, name in enumerate(("W_linT", "W_valT")):
                sp.dma_start(Wlv[:, :, q * D:(q + 1) * D], dram[name].rearrange("(c p) n -> p c n", p=P))\
                    .then_inc(w_in, 16)
            sp.dma_start(Wout[:, :, :], dram["W_outT"].rearrange("(c p) n -> p c n", p=P)).then_inc(w_in, 16)
            sp.wait_ge(const, 6)
            for head in range(HEADS):
                c, s = head // 2, head % 2
                sp.dma_start(APAD[s * N:(s + 1) * N, c, ROWS - HEADS + head:ROWS - HEADS + head + 1],
                             dram["a"][head, :].rearrange("(f o) -> f o", o=1)).then_inc(w_in, 16)
            sp.dma_start(X[:, :, :], src[0]).then_inc(x_in, 16)
            for g in range(NGRP):
                if g + 1 < NGRP:
                    sp.wait_ge(x3_sb, 2 * (g + 1))
                    sp.dma_start(X[:, :, :], src[g + 1]).then_inc(x_in, 16)
                sp.wait_ge(fin_sb, 2 * (g + 2))
                sp.dma_start(dst[g], XR[:, :, :]).then_inc(stored, 16)
            sp.wait_ge(stored, 16 * (NGRP + 1))

        @block.gpsimd
        def _(pool):
            g = nc.gpsimd
            g.memset(mhalf[:, :], -0.5).then_inc(const, 1)
            g.memset(ones[:, :], 1.0).then_inc(const, 1)
            g.memset(eps[:, :], 1e-8).then_inc(const, 1)
            g.memset(APAD[:, :, :], 0.0).then_inc(const, 1)
            g.iota(node_i[:, :], pattern=[[0, 1]], base=0, channel_multiplier=1).then_inc(const, 1)
            g.iota(col_i[:, :], pattern=[[0, 2], [1, N]], base=0, channel_multiplier=0).then_inc(const, 1)
            pool.wait_ge(const, 6)
            with pool.Fori(0, NGRP * LN_CALLS) as n:
                pool.wait_ge(var_ready, n + 1)
                g.tensor_tensor(rstd[:, :], var[:, :], mhalf[:, :], ALU.pow).then_inc(rstd_ready, 1)

        @block.tensor
        def _(pe):
            mm = nc.tensor.matmul
            pe.wait_ge(aa_in, 1)
            mm(ps[0:N, 0, :], adjT[:, :], DST[0:N, :], start=True, stop=True).then_inc(aa_ps, 1)
            pe.wait_ge(z_in, 1)
            mm(ps[0:ROWS, 1, :], ones[:, :], ES[0:N, :], start=True, stop=True).then_inc(z_ps, 1)
            pe.wait_ge(loga_sb, 1)
            with pe.Fori(0, NGRP) as i:
                pe.wait_ge(x_in, i * 16 + 16)
                for h in range(2):
                    if h == 1:
                        pe.wait_ge(fin_sb, i * 2 + 2)
                    for c in range(2):
                        for t in range(HALF):
                            last = mm(ps[:, 4 * h + c, t * P:(t + 1) * P], X[:, 4 * h + t, c * P:(c + 1) * P],
                                      bdu[:, :], start=True, stop=True)
                    last.then_inc(ux_ps, 1)
                for h in range(2):
                    pe.wait_ge(ux_sb, i * 2 + (h + 1))
                    for kc in range(2):
                        last = mm(ps[:, 4 * h + 2, :], W1[:, kc, :], FT[:, kc, h * HN:(h + 1) * HN],
                                  start=(kc == 0), stop=(kc == 1))
                    last.then_inc(hid_ps, 1)
                for h in range(2):
                    pe.wait_ge(hid_sb, i * 2 + (h + 1))
                    for t in range(HALF):
                        last = mm(ps[:, 4 * h + t // 2, (t % 2) * D:(t % 2 + 1) * D],
                                  HT[:, (4 * h + t) * P:(4 * h + t + 1) * P], W2[:, :], start=True, stop=True)
                    last.then_inc(o2_ps, 1)
                for h in range(2):
                    pe.wait_ge(o2_sb, i * 2 + (h + 1))
                    for u in range(2):
                        last = mm(ps[:, 4 * h + 2 + u, :], bdut[:, :], Y[:, 4 * h + 2 * u:4 * h + 2 * u + 2, :],
                                  start=True, stop=True)
                    last.then_inc(x3_ps, 1)
                for h in range(2):
                    pe.wait_ge(x3_sb, i * 2 + (h + 1))
                    for c in range(2):
                        for t in range(HALF):
                            last = nc.tensor.transpose(ps[:, 4 * h + c, t * P:(t + 1) * P],
                                                       XR[:, 4 * h + t, c * P:(c + 1) * P], ident[:, :])
                    last.then_inc(xt_ps, 1)
                for h in range(2):
                    pe.wait_ge(xt_sb, i * 2 + (h + 1))
                    for t in range(HALF):
                        for kc in range(2):
                            last = mm(ps[:, 4 * h + t, :], FT[:, kc, (4 * h + t) * P:(4 * h + t + 1) * P],
                                      Wlv[:, kc, :], start=(kc == 0), stop=(kc == 1))
                    last.then_inc(qv_ps, 1)
                pe.wait_ge(qv_sb, i * 2 + 2)

                def pairs(b):
                    r = slice((b % 2) * N, (b % 2 + 1) * N)
                    if b >= 2:
                        pe.wait_ge(lr_sb, i * GB + (b - 1))
                    for c in range(2):
                        last = mm(ps[:, 2 * (b % 2) + c, :], QV[r, b // 2, c * P:(c + 1) * P], GS[r, :],
                                  start=True, stop=True)
                    last.then_inc(pair_ps, 1)

                def scores(b):
                    pe.wait_ge(lr_sb, i * GB + (b + 1))
                    for c in range(2):
                        at = ROWS - HEADS - HEADS * b
                        last = mm(ps[0:ROWS, 4, :], APAD[:, c, at:at + ROWS], LR[:, b % 2, c, :],
                                  start=(b == 0 and c == 0), stop=(b == GB - 1 and c == 1))
                    last.then_inc(score_ps, 1)

                pairs(0)
                for b in range(1, GB):
                    pairs(b)
                    scores(b - 1)
                scores(GB - 1)
                pe.wait_ge(m_sb, i + 1)
                settle(pe, pe_passed)
                nc.tensor.transpose(ps[0:N, 5, 0:ROWS], m[:, :], ident[0:ROWS, 0:ROWS]).then_inc(mT_ps, 1)
                pe.wait_ge(mT_sb, i + 1)
                settle(pe, pe_passed)
                mm(ps[0:ROWS, 6, :], mT[:, :], SRC[0:N, :], start=True, stop=True).then_inc(mg_ps, 1)
                pe.wait_ge(ex_sb, i + 1)
                settle(pe, pe_passed)
                for c in range(CH):
                    last = nc.tensor.transpose(ps[:, 7, c * ROWS:(c + 1) * ROWS], EX[:, c * P:(c + 1) * P],
                                               ident[0:ROWS, 0:ROWS])
                last.then_inc(ext_ps, 1)
                pe.wait_ge(ext_sb, i + 1)
                for c in range(CH):
                    last = mm(ps[0:N, 5, 0:ROWS], SRCT[:, c, :], EXT[:, c, :], start=(c == 0), stop=(c == CH - 1))
                last.then_inc(den_ps, 1)
                pe.wait_ge(rd_sb, i + 1)
                for c in range(CH):
                    last = mm(ps[:, 6, c * ROWS:(c + 1) * ROWS], SRC[0:N, c * P:(c + 1) * P], RD[:, :], start=True,
                              stop=True)
                last.then_inc(rg_ps, 1)

                def node_matrices(t):
                    pe.wait_ge(pro_sb, i * TILES + (t + 1))
                    if t >= 2:
                        pe.wait_ge(pt_sb, i * TILES + (t - 1))
                    for c in range(CH):
                        last = mm(ps[:, t % 2, :], DSTT[:, c, :], PRO[:, t % 2, c, :, :], start=(c == 0),
                                  stop=(c == CH - 1))
                    last.then_inc(pt_ps, 1)

                def values(t):
                    pe.wait_ge(pt_sb, i * TILES + (t + 1))
                    if t >= 2:
                        pe.wait_ge(yt_sb, i * TILES + (t - 1))
                    for b in range(2):
                        r = slice(b * N, (b + 1) * N)
                        for c in range(2):
                            last = mm(ps[:, 2 + 2 * (t % 2) + b, c * P:(c + 1) * P],
                                      QV[r, t, D + c * P:D + (c + 1) * P], PT[r, t % 2, 2 * c:2 * c + 2, :],
                                      start=True, stop=True)
                    last.then_inc(yt_ps, 1)

                node_matrices(0)
                for t in range(1, TILES):
                    node_matrices(t)
                    values(t - 1)
                values(TILES - 1)
                for h in range(2):
                    pe.wait_ge(yt_sb, i * TILES + (4 * h + 4))
                    if h == 0:
                        pe.wait_ge(pt_sb, i * TILES + TILES)
                    for t in range(HALF):
                        for kc in range(2):
                            last = mm(ps[:, 6 - 2 * h + t // 2, (t % 2) * D:(t % 2 + 1) * D],
                                      YT[:, kc, (4 * h + t) * P:(4 * h + t + 1) * P], Wout[:, kc, :],
                                      start=(kc == 0), stop=(kc == 1))
                    last.then_inc(fin_ps, 1)

        @block.scalar
        def _(act):
            a = nc.scalar.activation
            act.wait_ge(z_ps, 1)
            act.wait_ge(w_in, B_DMAS * 16)
            act.wait_ge(const, 6)
            a(LOGA[:, :], ps[0:ROWS, 1, :], ACT.Ln, bias=eps[:, 0:1]).then_inc(loga_sb, 1)
            with act.Fori(0, NGRP) as i:
                for h in range(2):
                    act.wait_ge(ux_ps, i * 2 + (h + 1))
                    a(FT[:, :, h * HN:(h + 1) * HN], ps[:, 4 * h:4 * h + 2, :], ACT.Copy).then_inc(ux_sb, 1)
                for h in range(2):
                    act.wait_ge(hid_ps, i * 2 + (h + 1))
                    a(HT[:, h * HN:(h + 1) * HN], ps[:, 4 * h + 2, :], ACT.Relu, bias=b1[:, 0:1]).then_inc(hid_sb, 1)
                for h in range(2):
                    act.wait_ge(xt_ps, i * 2 + (h + 1))
                    a(FT[:, :, h * HN:(h + 1) * HN], ps[:, 4 * h:4 * h + 2, :], ACT.Copy).then_inc(xt_sb, 1)
                for h in range(2):
                    act.wait_ge(qv_ps, i * 2 + (h + 1))
                    a(QV[:, 4 * h:4 * h + 4, :], ps[:, 4 * h:4 * h + 4, :], ACT.Copy).then_inc(qv_sb, 1)
                for b in range(GB):
                    act.wait_ge(pair_ps, i * GB + (b + 1))
                    if b >= 1:
                        act.wait_ge(lr_sb, i * GB + b)
                    a(ABS[:, :, :], ps[:, 2 * (b % 2):2 * (b % 2) + 2, :], ACT.Abs, scale=0.4).then_inc(abs_sb, 1)
                act.wait_ge(mT_ps, i + 1)
                a(mT[:, :], ps[0:N, 5, 0:ROWS], ACT.Copy).then_inc(mT_sb, 1)
                act.wait_ge(d_sb, i + 1)
                a(EX[:, :], ES[:, :], ACT.Exp).then_inc(ex_sb, 1)
                act.wait_ge(ext_ps, i + 1)
                a(EXT[:, :, :], ps[:, 7, 0:CH * ROWS].rearrange("p (c r) -> p c r", c=CH), ACT.Copy)\
                    .then_inc(ext_sb, 1)
                for t in range(TILES):
                    act.wait_ge(pt_ps, i * TILES + (t + 1))
                    for b in range(2):
                        r = slice(b * N, (b + 1) * N)
                        last = a(PT[r, t % 2, :, :],
                                 ps[r, t % 2, b * HEADS * N:(b + 1) * HEADS * N].rearrange("p (h n) -> p h n", n=N),
                                 ACT.Copy)
                    last.then_inc(pt_sb, 1)
                    act.wait_ge(yt_ps, i * TILES + (t + 1))
                    o = ps[:, 2 + 2 * (t % 2):4 + 2 * (t % 2), 0:D].rearrange("p b (c s n) -> p b c s n", c=2, s=2)
                    y = YT[:, :, t * P:(t + 1) * P].rearrange("p c (b n) -> p b c n", b=2)
                    for s in range(2):
                        r = slice(s * N, (s + 1) * N)
                        last = a(y[r, :, :, :], o[r, :, :, s, :], ACT.Copy)
                    last.then_inc(yt_sb, 1)

        @block.vector
        def _(dve):
            v = nc.vector
            done = [0]

            def made(ins):
                done[0] += 1
                ins.then_inc(prep, 1)
                dve.wait_ge(prep, done[0])

            dve.wait_ge(const, 6)
            dve.wait_ge(w_in, B_DMAS * 16)
            made(v.tensor_copy(node[:, :], node_i[:, :]))
            made(v.tensor_scalar(EXT[:, 0, 0:1], node[:, :], float(N), -float(N), ALU.is_ge, ALU.mult))
            made(v.tensor_tensor(node[:, :], node[:, :], EXT[:, 0, 0:1], ALU.add))
            made(v.tensor_copy(colm[:, :], col_i[:, :]))
            made(v.tensor_copy(src_f[:, :], src_i[:, :]))
            made(v.tensor_copy(dst_f[:, :], dst_i[:, :]))
            made(v.tensor_copy(ecol[:, :, :], ecol_i[:, :, :]))
            made(v.tensor_scalar(SRC[:, :], src_f[:, :], node[:, 0:1], None, ALU.is_equal))
            v.tensor_scalar(DST[:, :], dst_f[:, :], node[:, 0:1], None, ALU.is_equal).then_inc(aa_in, 1)
            dve.wait_ge(aa_in, 1)
            made(v.tensor_tensor(GS[:, :], SRC[:, :], DST[:, :], ALU.add))
            for c in range(CH):
                made(v.tensor_scalar(SRCT[:, c, :], colm[:, 0:N], ecol[:, 0, c:c + 1], None, ALU.is_equal))
                made(v.tensor_scalar(DSTT[:, c, :], colm[:, :], ecol[:, 1, c:c + 1], None, ALU.is_equal))
            dve.wait_ge(aa_ps, 1)
            v.tensor_tensor(ES[0:N, :], ps[0:N, 0, :], SRC[0:N, :], ALU.mult).then_inc(z_in, 1)
            for n in range(N):
                made(v.tensor_scalar(NEG[:, n, :], src_f[0:ROWS, :], float(n), -1e30, ALU.not_equal, ALU.mult))
            dve.wait_ge(loga_sb, 1)
            per = keep["dve_links_b"]
            v.memset(var[:, :], 0.0).then_inc(fin_sb, 2)
            with dve.Fori(0, NGRP) as i:
                turn = dve.snap(i * per)
                n_own = [0]
                ln = [0, LN_CALLS]

                def link(ins):
                    n_own[0] += 1
                    ins.then_inc(own, 1)
                    dve.wait_ge(own, turn + n_own[0])

                for h in range(2):
                    dve.wait_ge(o2_ps, i * 2 + (h + 1))
                    v.tensor_tensor(Y[:, 4 * h:4 * h + 4, :],
                                    ps[:, 4 * h:4 * h + 2, :].rearrange("p b (t n) -> p (b t) n", n=D),
                                    across(b2, HALF), ALU.add).then_inc(o2_sb, 1)
                for h in range(2):
                    dve.wait_ge(x3_ps, i * 2 + (h + 1))
                    if h == 0:
                        keep["wait_stored"](dve, stored, i)
                    link(v.tensor_tensor(XR[:, 4 * h:4 * h + 4, :], X[:, 4 * h:4 * h + 4, :],
                                         ps[:, 4 * h + 2:4 * h + 4, :].rearrange("p b (t n) -> p (b t) n", n=D),
                                         ALU.add))
                    layer_norm(nc, dve, link, ln, h, XR[:, 4 * h:4 * h + 4, :], XR[:, 4 * h:4 * h + 4, :], i, stats,
                               mv, var, rstd, var_ready, rstd_ready, dve_passed).then_inc(x3_sb, 1)
                for b in range(GB):
                    dve.wait_ge(abs_sb, i * GB + (b + 1))
                    if b >= 2:
                        dve.wait_ge(score_ps, i * GB + (b - 1))
                    v.scalar_tensor_tensor(LR[:, b % 2, :, :], ps[:, 2 * (b % 2):2 * (b % 2) + 2, :], 0.6,
                                           ABS[:, :, :], ALU.mult, ALU.add).then_inc(lr_sb, 1)
                dve.wait_ge(score_ps, i * GB + GB)
                link(v.tensor_tensor(ES[:, :], ps[0:ROWS, 4, :], LOGA[:, :], ALU.add))
                settle(dve, dve_passed)
                for n in range(N):
                    last = v.tensor_tensor_reduce(mjunk[:, n % JUNK, :], ES[:, :], NEG[:, n, :], 1.0, -3e38, ALU.add,
                                                  ALU.max, m[:, n:n + 1])
                    if n % JUNK == JUNK - 1 and n < N - 1:
                        link(last)
                        settle(dve, dve_passed)
                last.then_inc(m_sb, 1)
                dve.wait_ge(mg_ps, i + 1)
                v.tensor_tensor(ES[:, :], ES[:, :], ps[0:ROWS, 6, :], ALU.subtract).then_inc(d_sb, 1)
                dve.wait_ge(den_ps, i + 1)
                link(v.tensor_scalar(RD[:, :], ps[0:N, 5, 0:ROWS], TINY, None, ALU.max))
                v.reciprocal(RD[:, :], RD[:, :]).then_inc(rd_sb, 1)
                dve.wait_ge(rg_ps, i + 1)
                v.tensor_tensor(AT[:, :, :], EXT[:, :, :],
                                ps[:, 6, 0:CH * ROWS].rearrange("p (c r) -> p c r", c=CH), ALU.mult).then_inc(at_sb, 1)
                dve.wait_ge(at_sb, i + 1)
                for t in range(TILES):
                    if t >= 2:
                        dve.wait_ge(pt_ps, i * TILES + (t - 1))
                    for c in range(CH):
                        last = v.tensor_tensor(
                            PRO[:, t % 2, c, :, :],
                            SRCT[:, c, :].rearrange("p (o n) -> p o n", o=1).to_broadcast([P, 8, N]),
                            col(AT[:, c, 8 * t:8 * t + 8]).to_broadcast([P, 8, N]), ALU.mult)
                    last.then_inc(pro_sb, 1)
                for h in range(2):
                    dve.wait_ge(fin_ps, i * 2 + (h + 1))
                    link(v.tensor_tensor(XR[:, 4 * h:4 * h + 4, :], XR[:, 4 * h:4 * h + 4, :],
                                         ps[:, 6 - 2 * h:8 - 2 * h, :].rearrange("p b (t n) -> p (b t) n", n=D),
                                         ALU.add))
                    layer_norm(nc, dve, link, ln, h, XR[:, 4 * h:4 * h + 4, :], XR[:, 4 * h:4 * h + 4, :], i, stats,
                               mv, var, rstd, var_ready, rstd_ready, dve_passed).then_inc(fin_sb, 1)
                assert n_own[0] == per, n_own[0]


B_DMAS = 16


def build(nc, x, adj, adjT, Wg0, bg0, Wg1, bg1, WihT, WhhT, bih, bhh, L1_W1, L1_W2, L1_W3, L2_W1, L2_b1, L2_W2, L2_b2,
          W_linT, W_valT, W_outT, a, src, dst, src_col,
          dst_col, out):
    dram = dict(x=x, adj=adj, adjT=adjT, L2_W1=L2_W1, L2_b1=L2_b1, L2_W2=L2_W2, L2_b2=L2_b2, W_linT=W_linT,
                W_valT=W_valT, W_outT=W_outT, a=a, src=src, dst=dst, src_col=src_col,
                dst_col=dst_col, out=out)
    dram["x2"] = nc.dram_tensor("x2_scratch", (BATCH * T, D), F32).ap()
    with ExitStack() as ctx:
        keep = {n: ctx.enter_context(nc.sbuf_tensor(n, [P, P], F32))
                for n in ("ident", "bd_adjT", "bd_wT", "bd_U", "bd_UT")}
        weights_in = ctx.enter_context(nc.semaphore("weights_in"))
        stored_credit = 0

        def wait_stored(eng, stored, i):
            eng.wait_ge(stored, i * 16 + 16)

        keep["wait_stored"] = wait_stored
        with ExitStack() as ctx_w:
            def sb(name, shape):
                return ctx_w.enter_context(nc.sbuf_tensor(name, shape, F32))

            w = dict(bg0=sb("w_bg0", [1, D]), rowsum=sb("w_rowsum", [1, HN]), Wg0=sb("w_g0", [P, 2, D]),
                     Wg1=sb("w_g1", [P, 2, D]), bg1=sb("w_bg1", [P, D]), Wih=sb("w_ih", [P, MAX_SKIP, 2, 4 * D]),
                     Whh=sb("w_hh", [P, MAX_SKIP - 1, 2, 4 * D]), bias=sb("w_bias", [P, 32]),
                     bih=sb("w_bih", [P, 32]), W1=sb("w_1", [P, 2, 512]), W2=sb("w_2", [P, 4, 1024]),
                     W3=sb("w_3", [P, 8, D]))
            keep["w"] = w
            by_rows = "(c p) n -> p c n"
            loads = [(w["bg0"][:, :], bg0.rearrange("(o d) -> o d", o=1)),
                     (w["Wg0"][:, :, :], Wg0.rearrange(by_rows, p=P)),
                     (w["Wg1"][:, :, :], Wg1.rearrange(by_rows, p=P)),
                     (w["bg1"][:, :], bg1.rearrange("(o d) -> o d", o=1).to_broadcast([P, D])),
                     (w["bias"][:, :], bih), (w["bih"][:, :], bhh),
                     (w["W1"][:, :, :], L1_W1.rearrange(by_rows, p=P)),
                     (w["W2"][:, :, :], L1_W2.rearrange(by_rows, p=P)),
                     (w["W3"][:, :, :], L1_W3.rearrange(by_rows, p=P))]
            loads += [(w["Wih"][:, p, :, :], WihT[p].rearrange(by_rows, p=P)) for p in range(MAX_SKIP)]
            loads += [(w["Whh"][:, p - 1, :, :], WhhT[p].rearrange(by_rows, p=P)) for p in range(1, MAX_SKIP)]

            def load_weights(sp):
                for d, s in loads:
                    sp.dma_start(d, s).then_inc(weights_in, 16)

            keep["load_weights"] = load_weights
            keep["weights_wait"] = lambda eng: eng.wait_ge(weights_in, 16 * len(loads))
            keep["dve_links_a"] = LINKS_A
            prepare(nc, dram, keep)
            layers_0_1(nc, dram, keep)
        keep["dve_links_b"] = LINKS_B
        layers_2_3(nc, dram, keep)


LINKS_A = 24
LINKS_B = 21

_OUT = (BATCH, T, D)


def kernel(**inputs):
    import numpy as _np
    import concourse.bacc as _bacc
    from concourse import mybir as _mybir
    from concourse.bass_utils import run_bass_kernel_spmd as _run

    i = {k: _np.asarray(v) for k, v in inputs.items()}

    def by_chunk(b):
        return b.reshape(MAX_SKIP, 8, P).transpose(2, 0, 1).reshape(P, MAX_SKIP * 8)

    laid = dict(
        x=i["x"].reshape(BATCH * T, D), adj=i["adj"], adjT=i["adj"].T, Wg0=i["L0_gnn_Wg0"], bg0=i["L0_gnn_bg0"],
        Wg1=i["L0_gnn_Wg1"], bg1=i["L0_gnn_bg1"], WihT=i["L0_gnn_Wih"].transpose(0, 2, 1),
        WhhT=i["L0_gnn_Whh"].transpose(0, 2, 1), bih=by_chunk(i["L0_gnn_bih"]), bhh=by_chunk(i["L0_gnn_bhh"]),
        L1_W1=i["L1_gnn_W1"], L1_W2=i["L1_gnn_W2"], L1_W3=i["L1_gnn_W3"], L2_W1=i["L2_gnn_W1"],
        L2_b1=i["L2_gnn_b1"], L2_W2=i["L2_gnn_W2"], L2_b2=i["L2_gnn_b2"], W_linT=i["L3_gnn_W_lin"].T,
        W_valT=i["L3_gnn_W_val"].T, W_outT=i["L3_gnn_W_out"].T, a=i["L3_gnn_a"], src=i["L3_gnn_src"],
        dst=i["L3_gnn_dst"], src_col=i["L3_gnn_src"].reshape(-1, P).T, dst_col=i["L3_gnn_dst"].reshape(-1, P).T)
    nc = _bacc.Bacc("TRN2", target_bir_lowering=False, num_devices=1)
    arrays, args = {}, {}
    for name, a in laid.items():
        a = _np.ascontiguousarray(a)
        arrays[f"in_{name}"] = a
        args[name] = nc.dram_tensor(f"in_{name}", a.shape, _mybir.dt.from_np(a.dtype), kind="ExternalInput").ap()
    out = nc.dram_tensor("out_0", (BATCH * T, D), _mybir.dt.float32, kind="ExternalOutput").ap()
    build(nc, out=out, **args)
    r = _run(nc, [arrays], core_ids=[0])
    return r.results[0]["out_0"].reshape(_OUT)
```

```python
from contextlib import ExitStack

import concourse.bass as bass
from concourse import mybir

ALU = mybir.AluOpType
ACT = mybir.ActivationFunctionType
F32 = mybir.dt.float32
BF16 = mybir.dt.bfloat16
I32 = mybir.dt.int32
AX_X = mybir.AxisListType.X

BATCH, T, D = 128, 64, 256
P = 128
GB = 16
NGRP = BATCH // GB
GT = GB * T
TILES = GT // P
HALF = TILES // 2
HN = HALF * P
EDGES = 512
HEADS = 4
LN_EPS = 1e-5
TINY = 1e-30
MAX_SKIP = 4
SECTIONS = 32
MID = T // 2
PASSES = 5


class Laplacian:

    def __init__(self, sb, sem):
        N = T
        self.pidx = sb("pidx_f", [P, P], F32)
        self.iota = sb("iota", [P, P], F32)
        self.ones = sb("ones", [N, P], F32)
        self.neg_id = sb("neg_id", [P, N], F32)
        self.is_q = sb("is_q", [P, 1], F32)
        self.half_pow = sb("half_pow", [P, 1], F32)
        self.mhalf_pow = sb("mhalf_pow", [P, 1], F32)
        self.M = sb("M", [P, N], F32)
        self.V = sb("V", [P, N], F32)
        self.Vr = sb("Vr", [P, N], F32)
        self.Wr = sb("Wr", [P, N], F32)
        self.OH = sb("OH", [P, N], F32)
        self.MK = sb("MK", [P, N], F32)
        self.SEL = sb("SEL", [N, P], F32)
        self.DG = sb("DG", [N, N], F32)
        self.junk = sb("junk", [P, 6, N], F32)
        self.sc = sb("sc", [P, 32], F32)
        self.k1 = sb("k1", [P, 1], F32)
        self.sel_ok = sem("sel_ready")
        self.row_ok = sem("row_ready")
        self.n2_ok = sem("n2_ready")
        self.nrm_ok = sem("norm_ready")
        self.dg_ok = sem("diag_ready")
        self.w_ok = sem("w_ready")


STEPS_A_TURN = 8


def reflect(nc, dve, link, lap, row_ps, w_ps, k):
    N = T
    v = nc.vector
    M, V, Vr, Wr, OH, MK, sc, k1, junk = lap.M, lap.V, lap.Vr, lap.Wr, lap.OH, lap.MK, lap.sc, lap.k1, lap.junk
    link(v.tensor_scalar(OH[:, :], lap.iota[:, 0:N], k1[:, 0:1], None, ALU.is_equal), wait=False)
    link(v.tensor_scalar(MK[:, :], lap.iota[:, 0:N], k1[:, 0:1], None, ALU.is_gt))
    dve.wait_ge(lap.row_ok, k + 1)
    link(v.tensor_tensor(Vr[:, :], row_ps, MK[:, :], ALU.mult), wait=False)
    link(v.tensor_tensor_reduce(junk[:, 0, :], row_ps, OH[:, :], 1.0, 0.0, ALU.mult, ALU.add,
                                 sc[:, 11:12]))
    link(v.tensor_tensor_reduce(junk[:, 1, :], Vr[:, :], Vr[:, :], 1.0, TINY, ALU.mult, ALU.add,
                                 sc[:, 12:13]))
    link(v.scalar_tensor_tensor(sc[:, 3:4], sc[:, 11:12], sc[:, 11:12], sc[:, 12:13], ALU.mult,
                                 ALU.add))
    link(v.tensor_scalar(sc[:, 13:14], sc[:, 11:12], 0.0, 2.0, ALU.is_ge, ALU.mult))
    v.tensor_scalar(sc[:, 14:15], sc[:, 13:14], -1.0, None, ALU.add).then_inc(lap.n2_ok, 1)
    dve.wait_ge(lap.n2_ok, k + 1)
    dve.wait_ge(lap.nrm_ok, k + 1)
    link(v.scalar_tensor_tensor(sc[:, 15:16], sc[:, 4:5], sc[:, 14:15], sc[:, 11:12], ALU.mult,
                                 ALU.add))
    link(v.scalar_tensor_tensor(V[:, :], OH[:, :], sc[:, 15:16], Vr[:, :], ALU.mult, ALU.add))
    link(v.scalar_tensor_tensor(sc[:, 16:17], sc[:, 15:16], sc[:, 15:16], sc[:, 12:13], ALU.mult,
                                 ALU.add))
    link(v.reciprocal(sc[:, 17:18], sc[:, 16:17]), wait=False)
    link(v.tensor_scalar(sc[:, 18:19], sc[:, 12:13], 2.0 * TINY, 2.0, ALU.is_gt, ALU.mult))
    link(v.tensor_tensor(sc[:, 19:20], sc[:, 17:18], sc[:, 18:19], ALU.mult), wait=False)
    link(v.tensor_tensor_reduce(junk[:, 2, :], M[:, :], V[:, :], 1.0, 0.0, ALU.mult, ALU.add,
                                 sc[:, 20:21]))
    link(v.tensor_tensor(sc[:, 21:22], sc[:, 20:21], sc[:, 19:20], ALU.mult))
    v.tensor_scalar(lap.DG[:, :], lap.ident[0:N, 0:N], sc[0:N, 21:22], None, ALU.mult).then_inc(lap.dg_ok, 1)
    link(v.tensor_tensor_reduce(junk[:, 3, :], V[:, :], lap.neg_id[:, :], 1.0, 0.0, ALU.mult, ALU.add,
                                 sc[:, 22:23]), wait=False)
    link(v.tensor_tensor(sc[:, 23:24], sc[:, 21:22], lap.is_q[:, :], ALU.mult))
    dve.wait_ge(lap.w_ok, k + 1)
    link(v.tensor_tensor_reduce(junk[:, 4, :], w_ps, V[:, :], 1.0, 0.0, ALU.mult, ALU.add,
                                 sc[:, 24:25]))
    link(v.tensor_scalar(sc[:, 25:26], sc[:, 24:25], sc[:, 19:20], -0.5, ALU.mult, ALU.mult))
    link(v.scalar_tensor_tensor(Wr[:, :], V[:, :], sc[:, 25:26], w_ps, ALU.mult, ALU.add))
    link(v.tensor_tensor_reduce(junk[:, 5, :], Wr[:, :], lap.neg_id[:, :], 1.0, sc[:, 23:24], ALU.mult,
                                 ALU.add, sc[:, 26:27]), wait=False)
    link(v.scalar_tensor_tensor(M[:, :], Wr[:, :], sc[:, 22:23], M[:, :], ALU.mult, ALU.add))
    link(v.scalar_tensor_tensor(M[:, :], V[:, :], sc[:, 26:27], M[:, :], ALU.mult, ALU.add), wait=False)
    link(v.tensor_scalar(k1[:, :], k1[:, :], 1.0, None, ALU.add))
    v.tensor_scalar(lap.SEL[:, :], lap.pidx[0:N, :], k1[0:N, 0:1], -1.0, ALU.subtract, ALU.is_equal).then_inc(lap.sel_ok, 1)


def prepare(nc, dram, keep):
    N = T
    with ExitStack() as ctx:
        def sb(name, shape, dt=F32):
            return ctx.enter_context(nc.sbuf_tensor(name, shape, dt))

        def sem(name):
            return ctx.enter_context(nc.semaphore(name))

        ps = ctx.enter_context(nc.psum_tensor("ps_prep", [P, 8, 512], F32))
        adj = sb("adj_sb", [P, N])
        adjT = sb("adjT_sb", [P, N])
        pidx = sb("pidx", [P, P], I32)
        iota_i = sb("iota_i", [P, P], I32)
        ident, lap = keep["ident"], keep["lap"]
        pidx_f, iota, ones, neg_id, is_q = lap.pidx, lap.iota, lap.ones, lap.neg_id, lap.is_q
        M, V, Vr, Wr, OH, MK, SEL, DG = lap.M, lap.V, lap.Vr, lap.Wr, lap.OH, lap.MK, lap.SEL, lap.DG
        sc, k1, junk = lap.sc, lap.k1, lap.junk

        loaded = sem("adj_loaded")
        made = sem("consts_made")
        link_s = sem("dve_link")
        pw_in = sem("pow_in")
        pw_out = sem("pow_out")
        tr_in = sem("tr_in")
        tr_out = sem("tr_out")

        block = ctx.enter_context(nc.Block())

        @block.sync
        def _(sp):
            for half in range(2):
                rows = slice(half * N, half * N + N)
                sp.dma_start(adj[rows, :], dram["adj"]).then_inc(loaded, 16)
                sp.dma_start(adjT[rows, :], dram["adjT"]).then_inc(loaded, 16)
            keep["load_weights"](sp)

        @block.gpsimd
        def _(pool):
            nc.gpsimd.iota(pidx[:, :], pattern=[[0, P]], base=0, channel_multiplier=1).then_inc(made, 1)
            nc.gpsimd.iota(iota_i[:, :], pattern=[[1, P]], base=0, channel_multiplier=0).then_inc(made, 1)
            nc.gpsimd.memset(lap.half_pow[:, :], 0.5).then_inc(made, 1)
            nc.gpsimd.memset(lap.mhalf_pow[:, :], -0.5).then_inc(made, 1)
            nc.gpsimd.memset(ones[:, :], 1.0).then_inc(made, 1)
            pool.wait_ge(made, 5)
            pool.wait_ge(pw_in, 1)
            nc.gpsimd.tensor_tensor(sc[:, 1:2], sc[:, 0:1], lap.mhalf_pow[:, 0:1], ALU.pow).then_inc(pw_out, 1)

        @block.tensor
        def _(pe):
            pe.wait_ge(tr_in, 1)
            nc.tensor.matmul(ps[0:N, 7, 0:N], ones[:, 0:N], DG[:, :], start=True, stop=True)
            nc.tensor.matmul(ps[0:N, 7, N:2 * N], ones[:, 0:N], adjT[0:N, :], start=True, stop=True)\
                .then_inc(tr_out, 1)

        @block.vector
        def _(dve):
            done = [0]

            def link(ins):
                done[0] += 1
                ins.then_inc(link_s, 1)
                dve.wait_ge(link_s, done[0])

            v = nc.vector
            dve.wait_ge(made, 5)
            dve.wait_ge(loaded, 64)
            link(v.tensor_copy(pidx_f[:, :], pidx[:, :]))
            link(v.tensor_copy(iota[:, :], iota_i[:, :]))
            link(v.tensor_tensor(ident[:, :], pidx_f[:, :], iota[:, :], ALU.is_equal))
            link(v.tensor_scalar(is_q[:, :], pidx_f[:, 0:1], float(N), -1.0, ALU.is_ge, ALU.mult))
            link(v.memset(neg_id[:, :], 0.0))
            link(v.tensor_scalar(neg_id[0:N, :], ident[0:N, 0:N], -1.0, None, ALU.mult))
            bda, bdw = keep["bd_adjT"], keep["bd_wT"]
            link(v.memset(bda[:, :], 0.0))
            link(v.memset(bdw[:, :], 0.0))
            for half in range(2):
                r = slice(half * N, half * N + N)
                v.tensor_copy(bda[r, r], adjT[r, :])
                link(v.tensor_tensor(bdw[r, r], adjT[r, :], adjT[r, :], ALU.mult))
            link(v.tensor_reduce(sc[:, 5:6], adj[:, :], AX_X, ALU.add))
            link(v.tensor_reduce(sc[:, 6:7], adjT[:, :], AX_X, ALU.add))
            link(v.memset(OH[:, :], 0.0))
            for half in range(2):
                r = slice(half * N, half * N + N)
                link(v.tensor_copy(OH[r, :], ident[r, r]))
            link(v.tensor_tensor_reduce(junk[:, 0, :], adj[:, :], OH[:, :], 1.0, 0.0, ALU.mult, ALU.add, sc[:, 7:8]))
            link(v.tensor_tensor(sc[:, 8:9], sc[:, 5:6], sc[:, 6:7], ALU.add))
            link(v.tensor_tensor(sc[:, 9:10], sc[:, 8:9], sc[:, 7:8], ALU.subtract))
            link(v.tensor_scalar(sc[:, 10:11], sc[:, 9:10], 0.0, None, ALU.is_gt))
            v.tensor_scalar(sc[:, 0:1], sc[:, 9:10], 1e-37, None, ALU.max).then_inc(pw_in, 1)
            dve.wait_ge(pw_out, 1)
            link(v.tensor_tensor(sc[:, 2:3], sc[:, 1:2], sc[:, 10:11], ALU.mult))
            link(v.tensor_scalar(Vr[:, :], OH[:, :], sc[:, 9:10], None, ALU.mult))
            link(v.tensor_tensor(V[:, :], Vr[:, :], adj[:, :], ALU.subtract))
            link(v.tensor_tensor(Wr[:, :], Vr[:, :], adjT[:, :], ALU.subtract))
            link(v.tensor_tensor(MK[:, :], V[:, :], Wr[:, :], ALU.add))
            link(v.tensor_scalar(MK[:, :], MK[:, :], sc[:, 2:3], 0.5, ALU.mult, ALU.mult))
            link(v.tensor_scalar(DG[:, :], ident[0:N, 0:N], sc[0:N, 2:3], None, ALU.mult))
            v.memset(SEL[:, :], 0.0).then_inc(tr_in, 1)
            dve.wait_ge(tr_out, 1)
            link(v.tensor_tensor(M[0:N, :], MK[0:N, :], ps[0:N, 7, 0:N], ALU.mult))
            keep["weights_wait"](dve)
            w = keep["w"]
            link(v.tensor_copy(w["rowsum"][0:1, :].rearrange("p (b n) -> p b n", n=N),
                               ps[0:1, 7, N:2 * N].rearrange("p (o n) -> p o n", o=1).to_broadcast([1, HN // N, N])))
            link(v.tensor_tensor(w["bias"][:, :], w["bias"][:, :], w["bih"][:, :], ALU.add))
            link(v.tensor_copy(M[N:P, :], ident[N:P, N:P]))
            link(v.memset(k1[:, :], 1.0))
            link(v.tensor_scalar(SEL[:, :], pidx_f[0:N, :], 0.0, None, ALU.is_equal))
            v.memset(sc[:, 30:31], 0.0).then_inc(lap.sel_ok, 1)


def eigenvectors(nc, keep):
    N = T
    with ExitStack() as ctx:
        def sb(name, shape, dt=F32):
            return ctx.enter_context(nc.sbuf_tensor(name, shape, dt))

        def sem(name):
            return ctx.enter_context(nc.semaphore(name))

        ident, lap = keep["ident"], keep["lap"]
        pidx_f, iota, ones, neg_id, is_q = lap.pidx, lap.iota, lap.ones, lap.neg_id, lap.is_q
        M, V, Vr, Wr, OH, MK, SEL, DG = lap.M, lap.V, lap.Vr, lap.Wr, lap.OH, lap.MK, lap.SEL, lap.DG
        sc, k1, junk = lap.sc, lap.k1, lap.junk
        ps = ctx.enter_context(nc.psum_tensor("ps_e", [P, 8, 512], F32))
        D_ = sb("Drow", [P, N])
        E_all = sb("Erow", [P, N])
        nE2_all = sb("nE2", [P, N])
        D_end = sb("D_end", [P, MID])
        nE2_end = sb("nE2_end", [P, MID])
        pair_sum = sb("pair_sum", [P, P])
        DL = sb("DL", [P, MID, SECTIONS])
        neg = sb("neg", [P, MID, SECTIONS])
        halves = sb("halves", [P, 2, SECTIONS])
        lam = sb("lam", [P, SECTIONS])
        steps = sb("steps", [P, SECTIONS])
        rc = sb("rc", [P, SECTIONS])
        cnt = sb("cnt", [P, SECTIONS])
        st_lanes = sb("st", [P, 64])
        PD = sb("PD", [N, N, 8])
        QP = sb("QP", [N, N, 8])
        nE2P = sb("nE2P", [N, N, 8])
        nEP = sb("nEP", [N, N, 2])
        RP = sb("RP", [N, N, 2])
        ZP = sb("ZP", [N, N, 2])
        gam = sb("gam", [N, N])
        dlt = sb("dlt", [N, N])
        Z = sb("Z", [N, N])
        BE = sb("BEc", [N, 32, 6])
        BC = sb("BCc", [N, 32, 6])
        BZ = sb("BZc", [N, 32, 6])
        BM = sb("BMc", [N, 32, 6])
        QT2 = sb("QT2", [N, P])
        Z2 = sb("Z2", [N, P])
        Zs = sb("Zs", [N, N])

        link_s = sem("e_dve_link")
        ms = sem("ms_link")
        halves_in, halves_out = sem("halves_ready"), sem("pair_sums_ready")
        pw_in, pw_out = sem("e_pow_in"), sem("e_pow_out")
        tr_in, tr_out = sem("e_tr_in"), sem("e_tr_out")
        block = ctx.enter_context(nc.Block())

        @block.gpsimd
        def _(pool):
            pool.wait_ge(pw_in, 1)
            nc.gpsimd.tensor_tensor(st_lanes[0:N, 11:12], st_lanes[0:N, 10:11], lap.mhalf_pow[0:N, 0:1], ALU.pow).then_inc(pw_out, 1)

        @block.tensor
        def _(pe):
            pe.wait_ge(tr_in, 1)
            nc.tensor.matmul(ps[:, 2, 0:N], ones[:, :], DG[:, :], start=True, stop=True)
            nc.tensor.matmul(ps[:, 2, N:2 * N], ones[:, :], SEL[:, 0:N], start=True, stop=True)
            nc.tensor.transpose(ps[0:N, 3, 0:P], M[:, :], ident[:, :]).then_inc(tr_out, 1)
            with pe.Fori(0, PASSES) as it:
                pe.wait_ge(halves_in, it + 1)
                nc.tensor.matmul(ps[:, 7, 0:2 * SECTIONS], pair_sum[:, :], halves[:, :, :], start=True, stop=True)\
                    .then_inc(halves_out, 1)
            pe.wait_ge(tr_in, 2)
            nc.tensor.matmul(ps[0:N, 4, 0:N], ones[:, 0:N], DG[:, :], start=True, stop=True).then_inc(tr_out, 1)
            pe.wait_ge(tr_in, 3)
            nc.tensor.transpose(ps[0:N, 5, 0:N], Zs[:, :], ident[0:N, 0:N]).then_inc(tr_out, 1)
            pe.wait_ge(tr_in, 4)
            nc.tensor.matmul(ps[:, 6, 0:N], QT2[:, :], Z2[:, 0:N], start=True, stop=True)
            nc.tensor.matmul(ps[:, 6, N:2 * N], Z2[:, :], QT2[:, 0:N], start=True, stop=True).then_inc(tr_out, 1)

        @block.vector
        def _(dve):
            done = [0]
            st = st_lanes

            def link(ins, wait=True):
                done[0] += 1
                ins.then_inc(link_s, 1)
                if wait:
                    dve.wait_ge(link_s, done[0])

            v = nc.vector
            link(v.tensor_tensor(MK[0:N, :], iota[0:N, 0:N], pidx_f[0:N, 0:N], ALU.subtract))
            link(v.tensor_scalar(MK[0:N, :], MK[0:N, :], -1.0, None, ALU.is_equal))
            link(v.tensor_tensor(SEL[:, 0:N], M[0:N, :], MK[0:N, :], ALU.mult))
            v.tensor_tensor(DG[:, :], M[0:N, :], ident[0:N, 0:N], ALU.mult).then_inc(tr_in, 1)
            dve.wait_ge(tr_out, 1)
            link(v.tensor_copy(D_[:, :], ps[:, 2, 0:N]))
            link(v.tensor_copy(E_all[:, :], ps[:, 2, N:2 * N]))
            link(v.tensor_copy(QT2[:, 0:N], ps[0:N, 3, N:P]))
            link(v.tensor_copy(QT2[:, N:P], ps[0:N, 3, N:P]))
            for half in range(2):
                r = slice(half * N, half * N + N)
                link(v.tensor_copy(pair_sum[r, :].rearrange("p (b n) -> p b n", n=N),
                                   ident[r, r].rearrange("p (o n) -> p o n", o=1).to_broadcast([N, 2, N])))
            aE, G, t0 = Vr[:, :], V[:, :], Wr[:, :]
            link(v.scalar_tensor_tensor(aE, E_all[:, :], -1.0, E_all[:, :], ALU.mult, ALU.max))
            link(v.tensor_tensor(t0, E_all[:, :], E_all[:, :], ALU.mult))
            link(v.tensor_scalar(nE2_all[:, :], t0, TINY, -1.0, ALU.max, ALU.mult))
            link(v.tensor_copy(G, aE))
            link(v.tensor_tensor(G[:, 1:N], aE[:, 1:N], aE[:, 0:N - 1], ALU.add))
            link(v.tensor_tensor(t0, D_[:, :], G, ALU.subtract))
            link(v.tensor_reduce(st[:, 0:1], t0, AX_X, ALU.min))
            link(v.tensor_tensor(t0, D_[:, :], G, ALU.add))
            link(v.tensor_reduce(st[:, 1:2], t0, AX_X, ALU.max))
            link(v.tensor_tensor(st[:, 2:3], st[:, 1:2], st[:, 0:1], ALU.subtract))
            link(v.tensor_scalar(st[:, 3:4], st[:, 2:3], 1.002, 1e-6, ALU.mult, ALU.add))
            link(v.scalar_tensor_tensor(st[:, 0:1], st[:, 3:4], -1e-3, st[:, 0:1], ALU.mult, ALU.add))
            link(v.tensor_scalar(st[:, 4:5], st[:, 3:4], 1.0 / (SECTIONS + 1), None, ALU.mult))
            link(v.tensor_scalar(steps[:, :], iota[:, 0:SECTIONS], 1.0, None, ALU.add))
            v.tensor_copy(D_end[0:N, :], D_[0:N, 0:MID])
            v.tensor_copy(nE2_end[0:N, :], nE2_all[0:N, 0:MID])
            v.tensor_copy(D_end[N:P, :], D_[N:P, N - 1:MID - 1:-1])
            v.tensor_copy(nE2_end[N:P, :], nE2_all[N:P, N - 2:MID - 2:-1])
            lane = st[:, 8:9]
            link(v.tensor_scalar(lane, is_q[:, :], float(N), pidx_f[:, 0:1], ALU.mult, ALU.add))

            PER = 2 * (MID - 1) + 15
            with dve.Fori(0, PASSES) as it:
                base = dve.snap(it * PER)
                n = [0]

                def mlink(ins, wait=True):
                    n[0] += 1
                    ins.then_inc(ms, 1)
                    if wait:
                        dve.wait_ge(ms, base + n[0])

                mlink(v.tensor_scalar(lam[:, :], steps[:, :], st[:, 4:5], st[:, 0:1], ALU.mult, ALU.add))
                mlink(v.tensor_tensor(DL[:, :, :], col(D_end[:, :]).to_broadcast([P, MID, SECTIONS]),
                                      lam[:, :].rearrange("p (o f) -> p o f", o=1).to_broadcast([P, MID, SECTIONS]),
                                      ALU.subtract))
                for j in range(1, MID):
                    mlink(v.reciprocal(rc[:, :], DL[:, j - 1, :]))
                    mlink(v.scalar_tensor_tensor(DL[:, j, :], rc[:, :], nE2_end[:, j - 1:j], DL[:, j, :], ALU.mult,
                                                 ALU.add))
                mlink(v.tensor_copy(halves[0:N, 0, :], DL[0:N, MID - 1, :]), wait=False)
                mlink(v.reciprocal(halves[N:P, 0, :], DL[N:P, MID - 1, :]))
                mlink(v.tensor_scalar(halves[N:P, 0, :], halves[N:P, 0, :], nE2_end[N:P, MID - 1:MID], None, ALU.mult))
                mlink(v.tensor_scalar(halves[:, 0, :], halves[:, 0, :], 1e30, -1e30, ALU.min, ALU.max), wait=False)
                mlink(v.tensor_scalar(neg[:, :, :], DL[:, :, :], 0.0, None, ALU.is_lt))
                mlink(v.tensor_reduce(halves[0:N, 1, :], neg[0:N, 0:MID - 1, :].rearrange("p k f -> p f k"), AX_X,
                                      ALU.add), wait=False)
                mlink(v.tensor_reduce(halves[N:P, 1, :], neg[N:P, :, :].rearrange("p k f -> p f k"), AX_X, ALU.add))
                dve.sem_inc(halves_in, 1)
                dve.wait_ge(halves_out, it + 1)
                mlink(v.tensor_scalar(rc[:, :], ps[:, 7, 0:SECTIONS], 0.0, None, ALU.is_lt))
                mlink(v.tensor_tensor(cnt[:, :], rc[:, :], ps[:, 7, SECTIONS:2 * SECTIONS], ALU.add))
                mlink(v.tensor_scalar(lam[:, :], cnt[:, :], lane, None, ALU.is_le))
                mlink(v.tensor_reduce(st[:, 5:6], lam[:, :], AX_X, ALU.add))
                mlink(v.scalar_tensor_tensor(st[:, 0:1], st[:, 5:6], st[:, 4:5], st[:, 0:1], ALU.mult, ALU.add))
                mlink(v.tensor_scalar(st[:, 4:5], st[:, 4:5], 1.0 / (SECTIONS + 1), None, ALU.mult))
                assert n[0] == PER, n[0]
            lamc = st[:, 6:7]
            link(v.scalar_tensor_tensor(lamc, st[:, 4:5], 0.5 * (SECTIONS + 1), st[:, 0:1], ALU.mult, ALU.add))
            v.tensor_scalar(DG[:, :], ident[0:N, 0:N], lamc[0:N], None, ALU.mult).then_inc(tr_in, 1)

            K = N - 1
            aE, E_, nE2, st = aE[0:N], E_all[0:N], nE2_all[0:N], st_lanes[0:N]
            link(v.memset(PD[:, :, :], 1.0))
            link(v.memset(nE2P[:, :, :], 0.0))
            link(v.memset(nEP[:, :, :], 0.0))
            link(v.memset(BE[:, :, :], 0.0))
            link(v.tensor_scalar(PD[:, :, 0], D_[0:N, :], st[:, 6:7], None, ALU.subtract))
            v.tensor_copy(PD[:, :, 1], PD[:, ::-1, 0])
            v.tensor_copy(nE2P[:, 0:K, 0], nE2[:, 0:K])
            v.tensor_copy(nE2P[:, 0:K, 1], nE2[:, K - 1::-1])
            link(v.tensor_scalar(nEP[:, 0:K, 0], E_[:, 0:K], -1.0, None, ALU.mult))
            v.tensor_copy(nEP[:, 0:K, 1], nEP[:, K - 1::-1, 0])
            chains = [(15, -1, 16, 15), (16, 1, 16, 15), (31, -1, 32, 31), (32, 1, 32, 31), (47, -1, 16, 47),
                      (48, 1, 16, 47)]

            def part(c):
                start, way, size, seam = chains[c]
                last = start + way * (size - 1)
                if way > 0:
                    return slice(start, start + size), slice(start, start + size - 1), size, seam
                stop = last - 1 if last else None
                return slice(start, stop, -1), slice(start - 1, stop, -1), size, seam

            for c in range(6):
                rows, between, size, seam = part(c)
                v.tensor_copy(PD[:, 0:size, 2 + c], PD[:, rows, 0])
                link(v.tensor_copy(BE[:, 0:size - 1, c], E_[:, between]))
                link(v.tensor_tensor(PD[:, 0, 2 + c:3 + c], PD[:, 0, 2 + c:3 + c], aE[:, seam:seam + 1],
                                     ALU.subtract))
            link(v.tensor_tensor(nE2P[:, 0:MID, 2:8], BE[:, :, :], BE[:, :, :], ALU.mult))
            link(v.tensor_scalar(nE2P[:, 0:MID, 2:8], nE2P[:, 0:MID, 2:8], TINY, -1.0, ALU.max, ALU.mult))
            link(v.tensor_copy(QP[:, 0, :], PD[:, 0, :]))
            for k in range(1, N):
                w = 8 if k < MID else 2
                link(v.reciprocal(rc[0:N, 0:w], QP[:, k - 1, 0:w]))
                link(v.tensor_tensor(rc[0:N, 8:8 + w], rc[0:N, 0:w], nE2P[:, k - 1, 0:w], ALU.mult))
                link(v.tensor_tensor(QP[:, k, 0:w], rc[0:N, 8:8 + w], PD[:, k, 0:w], ALU.add))
            link(v.tensor_scalar(QP[:, :, 0:2], QP[:, :, 0:2], 1e30, -1e30, ALU.min, ALU.max))
            v.reciprocal(BM[:, :, :], QP[:, 0:MID, 2:8])
            link(v.reciprocal(RP[:, :, :], QP[:, :, 0:2]))
            v.tensor_scalar(BM[:, :, :], BM[:, :, :], 1e30, -1e30, ALU.min, ALU.max)
            link(v.tensor_scalar(RP[:, :, :], RP[:, :, :], 1e30, -1e30, ALU.min, ALU.max))
            v.tensor_tensor(BM[:, :, :], BM[:, :, :], BE[:, :, :], ALU.mult)
            link(v.tensor_tensor(RP[:, :, :], RP[:, :, :], nEP[:, :, :], ALU.mult))
            link(v.tensor_tensor(gam[:, :], QP[:, :, 0], QP[:, ::-1, 1], ALU.add))
            link(v.tensor_tensor(gam[:, :], gam[:, :], PD[:, :, 0], ALU.subtract))
            link(v.scalar_tensor_tensor(gam[:, :], gam[:, :], -1.0, gam[:, :], ALU.mult, ALU.max))
            link(v.tensor_reduce(st[:, 7:8], gam[:, :], AX_X, ALU.min))
            link(v.tensor_scalar(dlt[:, :], gam[:, :], st[:, 7:8], None, ALU.is_le))
            link(v.tensor_copy(ZP[:, :, 0], dlt[:, :]))
            link(v.tensor_copy(ZP[:, :, 1], dlt[:, ::-1]))
            link(v.memset(BC[:, 0, :], 1.0))
            for j in range(K - 1, -1, -1):
                link(v.tensor_tensor(rc[0:N, 0:2], RP[:, j, :], ZP[:, j + 1, :], ALU.mult))
                up = K - j
                if up < MID:
                    link(v.tensor_tensor(BC[:, up, :], BC[:, up - 1, :], BM[:, up - 1, :], ALU.mult), wait=False)
                link(v.tensor_tensor(ZP[:, j, :], rc[0:N, 0:2], ZP[:, j, :], ALU.add))
            link(v.tensor_tensor(Z[:, :], ZP[:, :, 0], ZP[:, ::-1, 1], ALU.add))
            link(v.tensor_tensor(Z[:, :], Z[:, :], dlt[:, :], ALU.subtract))
            v.tensor_tensor_reduce(gam[:, :], Z[:, :], Z[:, :], 1.0, 0.0, ALU.mult, ALU.add,
                                   st[:, 10:11]).then_inc(pw_in, 1)
            dve.wait_ge(pw_out, 1)
            link(v.tensor_scalar(Z[:, :], Z[:, :], st[:, 11:12], None, ALU.mult))

            link(v.memset(BZ[:, :, :], 0.0))
            link(v.tensor_tensor(gam[:, :], Z[:, :], Z[:, :], ALU.mult))
            for c in range(6):
                rows, _, size, _ = part(c)
                link(v.tensor_copy(BZ[:, 0:size, c], gam[:, rows]), wait=False)
            link(v.tensor_scalar(BC[:, :, :], BC[:, :, :], 1e18, -1e18, ALU.min, ALU.max))
            link(v.tensor_tensor(BC[:, :, :], BC[:, :, :], BC[:, :, :], ALU.mult))
            link(v.tensor_reduce(st[:, 20:26], BZ[:, :, :].rearrange("p j c -> p c j"), AX_X, ALU.max))
            link(v.tensor_tensor(BM[:, :, :], BZ[:, :, :],
                                 st[:, 20:26].rearrange("p (o c) -> p o c", o=1).to_broadcast([N, 32, 6]),
                                 ALU.is_ge))
            link(v.tensor_tensor(BM[:, :, :], BM[:, :, :], BZ[:, :, :], ALU.mult))
            link(v.tensor_tensor(BM[:, :, :], BM[:, :, :], BC[:, :, :], ALU.mult))
            link(v.tensor_reduce(st[:, 26:32], BM[:, :, :].rearrange("p j c -> p c j"), AX_X, ALU.add))
            mx = st[:, 20:26].rearrange("p (b s) -> p b s", s=2)
            q2 = st[:, 26:32].rearrange("p (b s) -> p b s", s=2)
            low_side, q_at = st[:, 32:35], st[:, 35:38]
            link(v.tensor_tensor(low_side, mx[:, :, 0], mx[:, :, 1], ALU.is_ge))
            link(v.tensor_tensor(q_at, q2[:, :, 0], q2[:, :, 1], ALU.subtract))
            link(v.tensor_tensor(q_at, q_at, low_side, ALU.mult))
            link(v.tensor_tensor(q_at, q_at, q2[:, :, 1], ALU.add))
            eb = E_[:, 15:48:16]
            r_at, r2 = st[:, 38:41], st[:, 42:45]
            link(v.tensor_scalar(st[:, 45:48], eb, 0.0, 2.0, ALU.is_ge, ALU.mult))
            link(v.tensor_scalar(st[:, 45:48], st[:, 45:48], -1.0, None, ALU.add))
            link(v.tensor_tensor(r2, st[:, 45:48], Z[:, 16:49:16], ALU.mult))
            link(v.tensor_tensor(r_at, r2, Z[:, 15:48:16], ALU.add))
            link(v.tensor_reduce(st[:, 48:49], Z[:, 0:N:16], AX_X, ALU.add))
            link(v.tensor_scalar(st[:, 41:42], st[:, 48:49], -1.0, None, ALU.mult))
            dve.wait_ge(tr_out, 2)
            link(v.tensor_copy(dlt[:, :], ps[0:N, 4, 0:N]))
            link(v.tensor_tensor(dlt[:, :], dlt[:, :], dlt[:, :], ALU.mult))
            link(v.tensor_reduce(st[:, 49:50], dlt[:, :], AX_X, ALU.max))
            link(v.tensor_scalar(st[:, 50:51], st[:, 49:50], (8 * 2.0 ** -24) ** 2, None, ALU.mult))
            link(v.tensor_tensor(r2, r_at, r_at, ALU.mult))
            link(v.tensor_scalar(r2, r2, 1e-8, None, ALU.is_gt))
            link(v.tensor_tensor(st[:, 51:54], eb, eb, ALU.mult))
            link(v.tensor_tensor(st[:, 51:54], st[:, 51:54], q_at, ALU.mult))
            link(v.tensor_scalar(st[:, 51:54], st[:, 51:54], 2.0, st[:, 50:51], ALU.mult, ALU.is_gt))
            link(v.tensor_tensor(r2, r2, st[:, 51:54], ALU.max))
            sg = st[:, 54:58]
            link(v.tensor_scalar(sg, st[:, 38:42], 0.0, -2.0, ALU.is_ge, ALU.mult))
            link(v.tensor_scalar(sg, sg, 1.0, None, ALU.add))
            leaf, s15, s31, s47 = sg[:, 3:4], sg[:, 0:1], sg[:, 1:2], sg[:, 2:3]
            k15, k31, k47 = r2[:, 0:1], r2[:, 1:2], r2[:, 2:3]

            def choose(out, flag, yes, no):
                link(v.tensor_tensor(st[:, 62:63], yes, no, ALU.subtract))
                link(v.scalar_tensor_tensor(out, st[:, 62:63], flag, no, ALU.mult, ALU.add))

            choose(st[:, 58:59], k15, s15, leaf)
            choose(st[:, 59:60], k47, s47, leaf)
            choose(st[:, 60:61], low_side[:, 1:2], st[:, 58:59], st[:, 59:60])
            choose(st[:, 61:62], k31, s31, st[:, 60:61])
            v.tensor_scalar(Zs[:, :], Z[:, :], st[:, 61:62], None, ALU.mult).then_inc(tr_in, 1)
            dve.wait_ge(tr_out, 3)
            link(v.tensor_copy(Z2[:, 0:N], ps[0:N, 5, 0:N]))
            v.tensor_copy(Z2[:, N:P], ps[0:N, 5, 0:N]).then_inc(tr_in, 1)
            dve.wait_ge(tr_out, 4)
            bdu, bdut = keep["bd_U"], keep["bd_UT"]
            link(v.memset(bdu[:, :], 0.0))
            link(v.memset(bdut[:, :], 0.0))
            for half in range(2):
                r = slice(half * N, half * N + N)
                link(v.tensor_copy(bdu[r, r], ps[r, 6, 0:N]))
                link(v.tensor_copy(bdut[r, r], ps[r, 6, N:2 * N]))


def col(ap):
    return ap.rearrange("p (n o) -> p n o", o=1)


def settle(eng, passed):
    eng.sem_inc(passed, 1)


FIRST = (0, 0)


def at(turn, per, n):
    j, k = turn
    return add(j * (2 * per), k * per + n)


def add(base, n):
    return base + n


def layer_norm(nc, eng, link, ln_value, rows, stats, mv, var, rstd, var_ready, rstd_ready, passed):
    v = nc.vector
    for t in range(HALF):
        ins = v.bn_stats(stats[:, t, :], rows[:, t, :])
    link(ins)
    settle(eng, passed)
    for t in range(HALF):
        ins = v.bn_aggr(mv[:, t, :], stats[:, t, :])
    link(ins)
    v.tensor_scalar(var[:, :], mv[:, :, 1], LN_EPS, None, ALU.add).then_inc(var_ready, 1)
    eng.wait_ge(rstd_ready, ln_value[0] + 1)
    for t in range(HALF):
        ins = v.tensor_scalar(rows[:, t, :], rows[:, t, :], mv[:, t, 0:1], rstd[:, t:t + 1], ALU.subtract, ALU.mult)
    return ins


def lstm_units():
    units = [(1, tile, 0, fc) for tile in range(2) for fc in range(2)]
    for p in range(2, MAX_SKIP + 1):
        units += [(p, 0, step, fc) for step in range(p) for fc in range(2)]
    return units


UNITS = lstm_units()
FIRST_UNIT = {p: min(u for u, x in enumerate(UNITS) if x[0] == p) for p in range(1, MAX_SKIP + 1)}


def gates_of(step):
    return (0, 2, 3) if step == 0 else (0, 2, 1, 3)


def f_count(u):
    return sum(1 for x in UNITS[:u] if x[2] > 0)


def windows(buf, kc, p, tile, step):
    if p == 1:
        return buf[:, kc, tile * 512:(tile + 1) * 512]
    nw = T // p
    return buf[:, kc, :].rearrange("q (b t) -> q b t", t=T)[:, :, step:step + (nw - 1) * p + 1:p]


def width(p):
    return 512 if p == 1 else GB * (T // p)


def cells(ap, p):
    w = ap[:, 0:width(p)]
    return w if p == 1 else w.rearrange("q (b w) -> q b w", b=GB)


def layers_0_1(nc, dram, keep):
    with ExitStack() as ctx:
        def sb(name, shape, dt=F32):
            return ctx.enter_context(nc.sbuf_tensor(name, shape, dt))

        def sem(name):
            return ctx.enter_context(nc.semaphore(name))

        w = keep["w"]
        ps = ctx.enter_context(nc.psum_tensor("ps_a", [P, 8, 512], F32))
        X = sb("a_x", [P, TILES, D])
        XR = sb("a_xr", [P, TILES, D])
        AXT = sb("a_axt", [P, 2, GT])
        Y = sb("a_y", [P, TILES, D])
        arena = sb("a_arena", [P, 16384])
        H1T = arena[:, 0:2048].rearrange("p (c n) -> p c n", c=2)
        HT = arena[:, 2048:4096].rearrange("p (c n) -> p c n", c=2)
        HB = arena[:, 4096:6144].rearrange("p (c n) -> p c n", c=2)
        GATE = arena[:, 6144:10240].rearrange("p (f g n) -> p f g n", f=2, g=4)
        C = arena[:, 10240:11264].rearrange("p (f n) -> p f n", f=2)
        HS = arena[:, 11264:13312].rearrange("p (s f n) -> p s f n", s=2, f=2)
        TMP = arena[:, 13312:13824]
        S1 = arena[:, 0:4096].rearrange("p (t n) -> p t n", t=TILES)
        WS = arena[:, 4096:8192].rearrange("p (h c n) -> p h c n", h=2, c=4)
        S2 = arena[:, 8192:16384].rearrange("p (h c n) -> p h c n", h=2, c=8)
        stats = sb("a_stats", [P, HALF, 6])
        mv = sb("a_mv", [P, HALF, 2])
        var = sb("a_var", [P, HALF])
        rstd = sb("a_rstd", [P, HALF])
        mhalf = sb("a_mhalf", [P, HALF])
        ident, bda, bdw = keep["ident"], keep["bd_adjT"], keep["bd_wT"]
        lap = keep["lap"]
        HH = STEPS_A_TURN
        HH_EARLY = 3
        ROW_AT = [4, 8, 12, 17, 23, 29, 35, 40]
        W_AT = [6, 10, 14, 20, 26, 32, 38, 43]
        row_ps = [ps[:, 7, 0:T], ps[:, 3, 0:T], ps[:, 3, 0:T]]
        w_ps = [ps[:, 6, 0:T], ps[:, 2, 0:T], ps[:, 2, 0:T]]

        x_in = sem("x_loaded")
        ax_ps, ax_sb = sem("ax_ps"), sem("ax_sb")
        h1_ps, h1_sb = sem("h1_ps"), sem("h1_sb")
        y_ps, y_sb = sem("y_ps"), sem("y_sb")
        h2_ps, h2_sb = sem("h2_ps"), sem("h2_sb")
        xpart = sem("lstm_x_read")
        gates_ps = sem("gates_ps")
        ig_sb, f_sb, o_sb = sem("ig_sb"), sem("f_sb"), sem("o_sb")
        c_sb = sem("c_sb")
        tc_sb = sem("tanh_c_sb")
        h_sb = sem("h_sb")
        ht_ps = sem("h_tokens_ps")
        x1_sb = sem("x1_sb")
        wx_ps, wx_sb = sem("wx_ps"), sem("wx_sb")
        s1_ps, s1_sb = sem("s1_ps"), sem("s1_sb")
        ws_ps, ws_sb = sem("ws_ps"), sem("ws_sb")
        s2_ps, s2_sb = sem("s2_ps"), sem("s2_sb")
        y3_ps, y3_sb = sem("y3_ps"), sem("y3_sb")
        x2_ps, x2_sb = sem("x2_ps"), sem("x2_sb")
        x2_read = sem("x2_ps_read")
        var_ready, rstd_ready = sem("var_ready"), sem("rstd_ready")
        stored = sem("x2_stored")
        dve_passed = sem("a_dve_passed")
        own = sem("dve_own")
        const = sem("a_const")
        NU = len(UNITS)
        NF = f_count(NU)
        LN_CALLS = 4

        block = ctx.enter_context(nc.Block())

        @block.sync
        def _(sp):
            src = dram["x"].rearrange("(g t p) d -> g p t d", p=P, t=TILES)
            dst = dram["x2"].rearrange("(g t p) d -> g p t d", p=P, t=TILES)
            sp.sem_inc(stored, 16)
            sp.dma_start(X[:, :, :], src[0]).then_inc(x_in, 16)
            for g in range(NGRP):
                if g + 1 < NGRP:
                    sp.wait_ge(x1_sb, 2 * (g + 1))
                    sp.dma_start(X[:, :, :], src[g + 1]).then_inc(x_in, 16)
                sp.wait_ge(x2_sb, 2 * (g + 2))
                sp.dma_start(dst[g], XR[:, :, :]).then_inc(stored, 16)
            sp.wait_ge(stored, 16 * (NGRP + 1))

        @block.gpsimd
        def _(pool):
            nc.gpsimd.memset(mhalf[:, :], -0.5).then_inc(const, 1)
            pool.wait_ge(const, 1)
            with pool.Fori(0, NGRP) as i:
                for n in range(LN_CALLS):
                    pool.wait_ge(var_ready, i * LN_CALLS + (n + 1))
                    nc.gpsimd.tensor_tensor(rstd[:, :], var[:, :], mhalf[:, :], ALU.pow).then_inc(rstd_ready, 1)
                    if n == 1:
                        for q in range(HH):
                            pool.wait_ge(lap.n2_ok, i * HH + (q + 1))
                            nc.gpsimd.tensor_tensor(lap.sc[:, 4:5], lap.sc[:, 3:4], lap.half_pow[:, :], ALU.pow)\
                                .then_inc(lap.nrm_ok, 1)

        @block.tensor
        def _(pe):
            mm = nc.tensor.matmul

            def reflect_row(i, q):
                pe.wait_ge(lap.sel_ok, i * HH + (q + 1))
                mm(row_ps[q // HH_EARLY], lap.SEL[:, :], lap.M[0:T, :], start=True, stop=True).then_inc(lap.row_ok, 1)

            def reflect_w(i, q):
                pe.wait_ge(lap.dg_ok, i * HH + (q + 1))
                mm(w_ps[q // HH_EARLY], lap.ones[:, :], lap.DG[:, :], start=True, stop=True).then_inc(lap.w_ok, 1)

            def reflection_slot(i, n):
                if n in ROW_AT:
                    reflect_row(i, ROW_AT.index(n))
                if n in W_AT:
                    reflect_w(i, W_AT.index(n))

            def mix_nodes(h, src, fcs, banks, mat, tok):
                for c in range(fcs):
                    for t in range(HALF):
                        last = mm(ps[:, banks + c, t * P:(t + 1) * P], src[:, tok + t, c * P:(c + 1) * P], mat[:, :],
                                  start=True, stop=True)
                return last

            keep["weights_wait"](pe)
            with pe.Fori(0, NGRP) as i:
                pe.wait_ge(x_in, i * 16 + 16)
                for h in range(2):
                    mix_nodes(h, X, 2, 4 * h, bda, 4 * h).then_inc(ax_ps, 1)
                pe.wait_ge(x2_read, i * 2 + 2)
                for h in range(2):
                    pe.wait_ge(ax_sb, i * 2 + (h + 1))
                    for oc in range(2):
                        o = ps[:, 4 * h + 2 + oc, :]
                        mm(o, w["bg0"][0:1, oc * P:(oc + 1) * P], w["rowsum"][0:1, :], start=True, stop=False)
                        for kc in range(2):
                            last = mm(o, w["Wg0"][:, kc, oc * P:(oc + 1) * P], AXT[:, kc, h * HN:(h + 1) * HN],
                                      start=False, stop=(kc == 1))
                    last.then_inc(h1_ps, 1)
                for h in range(2):
                    pe.wait_ge(h1_sb, i * 2 + (h + 1))
                    for t in range(HALF):
                        for kc in range(2):
                            last = mm(ps[:, 4 * h + t // 2, (t % 2) * D:(t % 2 + 1) * D],
                                      H1T[:, kc, (4 * h + t) * P:(4 * h + t + 1) * P], w["Wg1"][:, kc, :],
                                      start=(kc == 0), stop=(kc == 1))
                    last.then_inc(y_ps, 1)
                for h in range(2):
                    pe.wait_ge(y_sb, i * 2 + (h + 1))
                    mix_nodes(h, Y, 2, 4 * h + 2, bda, 4 * h).then_inc(h2_ps, 1)
                pe.wait_ge(h2_sb, i * 2 + 1)
                for u, (p, tile, step, _) in enumerate(UNITS):
                    if u % 2:
                        continue
                    src = HT if p == 1 else HB
                    n = width(p)

                    def gates(fc, weights, kcs, rhs, first, final):
                        for g in gates_of(step):
                            for kc in kcs:
                                last = mm(ps[:, 4 * fc + g, 0:n], weights[:, kc, g * D + fc * P:g * D + (fc + 1) * P],
                                          rhs(kc), start=(first and kc == kcs[0]), stop=(final and kc == kcs[-1]))
                        return last

                    def x_part(fc, kcs):
                        return gates(fc, w["Wih"][:, p - 1], kcs, lambda kc: windows(src, kc, p, tile, step),
                                     kcs[0] == 0, step == 0 and kcs[-1] == 1)

                    if p == 1 and u > 0:
                        pe.wait_ge(o_sb, i * NU + (u - 1))
                    if p > 1:
                        pe.wait_ge(h_sb, i * NU + (u - 1))
                    if step == 0:
                        x_part(0, [0])
                        if u > 0:
                            pe.wait_ge(o_sb, i * NU + u)
                        else:
                            pe.wait_ge(h2_sb, i * 2 + 2)
                        x_part(1, [0])
                        if p > 1:
                            pe.wait_ge(h_sb, i * NU + u)
                        for fc in range(2):
                            x_part(fc, [1]).then_inc(gates_ps, 1)
                    else:
                        x_part(0, [0, 1]).then_inc(xpart, 1)
                        pe.wait_ge(o_sb, i * NU + u)
                        x_part(1, [0, 1]).then_inc(xpart, 1)
                        pe.wait_ge(h_sb, i * NU + u)
                        for fc in range(2):
                            gates(fc, w["Whh"][:, p - 2], [0, 1], lambda kc: HS[:, (step - 1) % 2, kc, 0:n], False,
                                  True).then_inc(gates_ps, 1)
                def to_tokens(h, fc):
                    for t in range(HALF):
                        last = nc.tensor.transpose(
                            ps[:, 4 * h + t // 2, (t % 2) * D + fc * P:(t % 2) * D + (fc + 1) * P],
                            HB[:, fc, (4 * h + t) * P:(4 * h + t + 1) * P], ident[:, :])
                    return last

                pe.wait_ge(h_sb, i * NU + (NU - 1))
                to_tokens(0, 0)
                pe.wait_ge(o_sb, i * NU + NU)
                to_tokens(1, 0)
                pe.wait_ge(h_sb, i * NU + NU)
                for h in range(2):
                    to_tokens(h, 1).then_inc(ht_ps, 1)

                def wx(h):
                    pe.wait_ge(x1_sb, i * 2 + (h + 1))
                    mix_nodes(h, XR, 2, 4 * h + 2, bdw, 4 * h).then_inc(wx_ps, 1)

                def s1(h):
                    pe.wait_ge(wx_sb, i * 2 + (h + 1))
                    for t in range(HALF):
                        for kc in range(2):
                            last = mm(ps[:, 4 * h + t, :], AXT[:, kc, (4 * h + t) * P:(4 * h + t + 1) * P],
                                      w["W1"][:, kc, :], start=(kc == 0), stop=(kc == 1))
                    last.then_inc(s1_ps, 1)

                def ws(h):
                    pe.wait_ge(s1_sb, i * 2 + (h + 1))
                    mix_nodes(h, S1, 4, 4 * h, bdw, 4 * h).then_inc(ws_ps, 1)

                wx(0)
                s1(0)
                wx(1)
                ws(0)
                s1(1)
                for h in range(2):
                    pe.wait_ge(ws_sb, i * 2 + (h + 1))
                    if h == 1:
                        pe.wait_ge(s2_sb, i * 16 + 8)
                    for oc in range(8):
                        if oc >= 4:
                            pe.wait_ge(s2_sb, i * 16 + (8 * h + oc - 3))
                        if h == 0 and oc == 1:
                            ws(1)
                        for kc in range(4):
                            if kc % 2 == 0:
                                n = 16 * h + 2 * oc + kc // 2
                                if n == ROW_AT[0]:
                                    pe.wait_ge(ws_sb, i * 2 + 2)
                                reflection_slot(i, n)
                            last = mm(ps[:, 4 * h + oc % 4, :], w["W2"][:, kc, oc * P:(oc + 1) * P],
                                      WS[:, h, kc, :], start=(kc == 0), stop=(kc == 3))
                        last.then_inc(s2_ps, 1)
                for h in range(2):
                    pe.wait_ge(s2_sb, i * 16 + (8 * h + 8))
                    for t in range(HALF):
                        for kc in range(8):
                            if kc % 4 == 0:
                                reflection_slot(i, 32 + 8 * h + 2 * t + kc // 4)
                            last = mm(ps[:, 4 * h + t // 2, (t % 2) * D:(t % 2 + 1) * D],
                                      S2[:, h, kc, t * P:(t + 1) * P], w["W3"][:, kc, :], start=(kc == 0),
                                      stop=(kc == 7))
                    last.then_inc(y3_ps, 1)
                pe.wait_ge(lap.sel_ok, i * HH + (HH + 1))
                for h in range(2):
                    pe.wait_ge(y3_sb, i * 2 + (h + 1))
                    for u in range(2):
                        last = mm(ps[:, 4 * h + 2 + u, :], bdw[:, :], Y[:, 4 * h + 2 * u:4 * h + 2 * u + 2, :],
                                  start=True, stop=True)
                    last.then_inc(x2_ps, 1)

        @block.scalar
        def _(act):
            a = nc.scalar.activation
            keep["weights_wait"](act)
            with act.Fori(0, NGRP) as i:
                for h in range(2):
                    act.wait_ge(ax_ps, i * 2 + (h + 1))
                    a(AXT[:, :, h * HN:(h + 1) * HN], ps[:, 4 * h:4 * h + 2, :], ACT.Copy).then_inc(ax_sb, 1)
                for h in range(2):
                    act.wait_ge(h1_ps, i * 2 + (h + 1))
                    a(H1T[:, :, h * HN:(h + 1) * HN], ps[:, 4 * h + 2:4 * h + 4, :], ACT.Relu).then_inc(h1_sb, 1)
                for h in range(2):
                    act.wait_ge(h2_ps, i * 2 + (h + 1))
                    a(HT[:, :, h * HN:(h + 1) * HN], ps[:, 4 * h + 2:4 * h + 4, :], ACT.Relu).then_inc(h2_sb, 1)
                for u, (p, tile, step, fc) in enumerate(UNITS):
                    n = width(p)
                    act.wait_ge(gates_ps, i * NU + (u + 1))
                    if u >= 2:
                        act.wait_ge(h_sb, i * NU + (u - 1))

                    def gate(g, func):
                        b = (p - 1) * 8 + 2 * g + fc
                        return a(GATE[:, fc, g, 0:n], ps[:, 4 * fc + g, 0:n], func, bias=w["bias"][:, b:b + 1])

                    gate(0, ACT.Sigmoid)
                    gate(2, ACT.Tanh).then_inc(ig_sb, 1)
                    if step > 0:
                        gate(1, ACT.Sigmoid).then_inc(f_sb, 1)
                    gate(3, ACT.Sigmoid).then_inc(o_sb, 1)
                    act.wait_ge(c_sb, i * NU + (u + 1))
                    a(GATE[:, fc, 2, 0:n], C[:, fc, 0:n], ACT.Tanh).then_inc(tc_sb, 1)
                def wx(h):
                    act.wait_ge(wx_ps, i * 2 + (h + 1))
                    a(AXT[:, :, h * HN:(h + 1) * HN], ps[:, 4 * h + 2:4 * h + 4, :], ACT.Copy).then_inc(wx_sb, 1)

                def s1(h):
                    act.wait_ge(s1_ps, i * 2 + (h + 1))
                    a(S1[:, 4 * h:4 * h + 4, :], ps[:, 4 * h:4 * h + 4, :], ACT.Relu).then_inc(s1_sb, 1)

                def ws(h):
                    act.wait_ge(ws_ps, i * 2 + (h + 1))
                    a(WS[:, h, :, :], ps[:, 4 * h:4 * h + 4, :], ACT.Copy).then_inc(ws_sb, 1)

                wx(0)
                s1(0)
                wx(1)
                ws(0)
                s1(1)
                for h in range(2):
                    for oc in range(8):
                        if h == 0 and oc == 1:
                            ws(1)
                        act.wait_ge(s2_ps, i * 16 + (8 * h + oc + 1))
                        a(S2[:, h, oc, :], ps[:, 4 * h + oc % 4, :], ACT.Relu).then_inc(s2_sb, 1)
                for h in range(2):
                    act.wait_ge(y3_ps, i * 2 + (h + 1))
                    a(Y[:, 4 * h:4 * h + 4, :], ps[:, 4 * h:4 * h + 2, :], ACT.Copy).then_inc(y3_sb, 1)

        @block.vector
        def _(dve):
            v = nc.vector
            keep["weights_wait"](dve)
            per = keep["dve_links_a"]
            v.memset(var[:, :], 0.0).then_inc(x2_sb, 2)
            dve.sem_inc(x2_read, 2)
            with dve.Fori(0, NGRP) as i:
                turn = dve.snap(i * per)
                n_own = [0]

                def link(ins, wait=True):
                    n_own[0] += 1
                    ins.then_inc(own, 1)
                    if wait:
                        dve.wait_ge(own, turn + n_own[0])

                for h in range(2):
                    dve.wait_ge(y_ps, i * 2 + (h + 1))
                    v.tensor_tensor(Y[:, 4 * h:4 * h + 4, :],
                                    ps[:, 4 * h:4 * h + 2, :].rearrange("p b (t n) -> p (b t) n", n=D),
                                    across(w["bg1"], HALF), ALU.add).then_inc(y_sb, 1)
                for u, (p, tile, step, fc) in enumerate(UNITS):
                    n = width(p)
                    g = [GATE[:, fc, q, 0:n] for q in range(4)]
                    c = C[:, fc, 0:n]
                    dve.wait_ge(ig_sb, i * NU + (u + 1))
                    if step == 0:
                        v.tensor_tensor(c, g[0], g[2], ALU.mult).then_inc(c_sb, 1)
                    else:
                        v.tensor_tensor(TMP[:, 0:n], g[0], g[2], ALU.mult)
                        dve.wait_ge(f_sb, i * NF + (f_count(u) + 1))
                        link(v.tensor_tensor(c, g[1], c, ALU.mult))
                        v.tensor_tensor(c, c, TMP[:, 0:n], ALU.add).then_inc(c_sb, 1)
                    last_step = step == p - 1
                    if last_step:
                        out = windows(HB, fc, p, tile, step)
                        if step > 0 and fc == 0:
                            dve.wait_ge(xpart, i * NF + (f_count(u) + 2))
                    else:
                        out = cells(HS[:, step % 2, fc, :], p)
                    dve.wait_ge(tc_sb, i * NU + (u + 1))
                    v.tensor_tensor(out, cells(g[3], p), cells(g[2], p), ALU.mult).then_inc(h_sb, 1)
                for h in range(2):
                    dve.wait_ge(ht_ps, i * 2 + (h + 1))
                    if h == 0:
                        keep["wait_stored"](dve, stored, i)
                    ins = v.tensor_tensor(XR[:, 4 * h:4 * h + 4, :], X[:, 4 * h:4 * h + 4, :],
                                          ps[:, 4 * h:4 * h + 2, :].rearrange("p b (t n) -> p (b t) n", n=D),
                                          ALU.add)
                    link(ins)
                    layer_norm(nc, dve, link, [i * LN_CALLS + (0 + h)], XR[:, 4 * h:4 * h + 4, :], stats, mv, var,
                               rstd, var_ready, rstd_ready, dve_passed).then_inc(x1_sb, 1)
                for q in range(HH):
                    reflect(nc, dve, link, lap, row_ps[q // HH_EARLY], w_ps[q // HH_EARLY], i * HH + q)
                for h in range(2):
                    dve.wait_ge(x2_ps, i * 2 + (h + 1))
                    link(v.tensor_tensor(XR[:, 4 * h:4 * h + 4, :], XR[:, 4 * h:4 * h + 4, :],
                                         ps[:, 4 * h + 2:4 * h + 4, :].rearrange("p b (t n) -> p (b t) n", n=D),
                                         ALU.add))
                    dve.sem_inc(x2_read, 1)
                for h in range(2):
                    layer_norm(nc, dve, link, [i * LN_CALLS + (2 + h)], XR[:, 4 * h:4 * h + 4, :], stats, mv, var,
                               rstd, var_ready, rstd_ready, dve_passed).then_inc(x2_sb, 1)
                assert n_own[0] == per, n_own[0]


def across(row, n):
    return row[:, :].rearrange("p (o d) -> p o d", o=1).to_broadcast([P, n, D])


def layers_2_3(nc, dram, keep):
    N = T
    CH = EDGES // P
    ROWS = GB * HEADS
    NH = N // 2
    with ExitStack() as ctx:
        def sb(name, shape, dt=F32):
            return ctx.enter_context(nc.sbuf_tensor(name, shape, dt))

        def sem(name):
            return ctx.enter_context(nc.semaphore(name))

        ps = ctx.enter_context(nc.psum_tensor("ps_b", [P, 8, 512], F32))
        ident, bdu, bdut = keep["ident"], keep["bd_U"], keep["bd_UT"]
        W1 = sb("b_W1", [P, 2, 128])
        b1 = sb("b_b1", [P, 1])
        W2 = sb("b_W2", [P, D])
        b2 = sb("b_b2", [P, D])
        Wlv = sb("b_Wlv", [P, 2, 2 * D])
        Wout = sb("b_Wout", [P, 2, D])
        APAD = sb("b_apad", [P, 2, ROWS - HEADS + P])
        adjT = sb("b_adjT", [N, N])
        src_i = sb("b_src_i", [P, EDGES], I32)
        dst_i = sb("b_dst_i", [P, EDGES], I32)
        src_f = sb("b_src_f", [P, EDGES])
        dst_f = sb("b_dst_f", [P, EDGES])
        ecol_i = sb("b_ecol_i", [P, 2, CH], I32)
        ecol = sb("b_ecol", [P, 2, CH])
        node_i = sb("b_node_i", [P, 1], I32)
        node = sb("b_node", [P, 1])
        col_i = sb("b_col_i", [P, P], I32)
        colm = sb("b_colm", [P, P])
        SRC = sb("b_src1h", [P, EDGES])
        DST = sb("b_dst1h", [P, EDGES])
        GS = sb("b_gs", [P, EDGES])
        SRCT = sb("b_srcT", [P, CH, N])
        DSTT = sb("b_dstT", [P, CH, P])
        SRClo = SRC[0:NH, :]
        SRChi = sb("b_src1h_hi", [NH, EDGES])
        NEG = sb("b_neg", [P, NH, EDGES], BF16)
        LOGA = sb("b_loga", [P, EDGES])
        ones = sb("b_ones", [N, P])
        eps = sb("b_eps", [P, 1])
        X = sb("b_x", [P, TILES, D])
        XR2 = sb("b_xr", [P, 2, TILES, D])
        FT = sb("b_ft", [P, 2, GT])
        HT = sb("b_ht", [P, GT])
        Y = sb("b_y", [P, TILES, D])
        QV2 = sb("b_qv", [P, 2, TILES, 2 * D])
        ABS = sb("b_abs", [P, 2, EDGES])
        LR = sb("b_lrelu", [P, 2, 2, EDGES])
        ES = sb("b_es", [P, EDGES])
        EX = sb("b_ex", [ROWS, EDGES])
        JUNK = 8
        mjunk = sb("b_mjunk", [P, JUNK, EDGES], BF16)
        m = sb("b_m", [P, NH])
        mT = sb("b_mT", [NH, P])
        EXT = sb("b_ext", [P, CH, ROWS])
        RD = sb("b_rd", [N, ROWS])
        AT = sb("b_at", [P, CH, ROWS])
        PRO = sb("b_pro", [P, 2, CH, 8, N])
        PT = sb("b_pt", [P, 2, HEADS, N])
        YT = sb("b_yt", [P, 2, GT])
        stats = sb("b_stats", [P, HALF, 6])
        mv = sb("b_mv", [P, HALF, 2])
        var = sb("b_var", [P, HALF])
        rstd = sb("b_rstd", [P, HALF])
        mhalf = sb("b_mhalf", [P, HALF])

        w_in = sem("b_weights")
        const = sem("b_const")
        prep = sem("b_prep")
        aa_in, aa_ps, z_in, z_ps, loga_sb = sem("aa_in"), sem("aa_ps"), sem("z_in"), sem("z_ps"), sem("loga_sb")
        x_in = sem("b_x_loaded")
        ux_ps, ux_sb = sem("ux_ps"), sem("ux_sb")
        hid_ps, hid_sb = sem("hid_ps"), sem("hid_sb")
        o2_ps, o2_sb = sem("o2_ps"), sem("o2_sb")
        x3_ps, x3_sb = sem("x3_ps"), sem("x3_sb")
        xt_ps, xt_sb = sem("xt_ps"), sem("xt_sb")
        qv_ps, qv_sb = sem("qv_ps"), sem("qv_sb")
        pair_ps, abs_sb, lr_sb = sem("pair_ps"), sem("abs_sb"), sem("lr_sb")
        score_ps, es_sb = sem("score_ps"), sem("es_sb")
        m_sb, mT_ps, mT_sb, mg_ps, d_sb, ex_sb = (sem("m_sb"), sem("mT_ps"), sem("mT_sb"), sem("mg_ps"), sem("d_sb"),
                                                  sem("ex_sb"))
        ext_ps, ext_sb, den_ps, rd_sb, rg_ps, at_sb = (sem("ext_ps"), sem("ext_sb"), sem("den_ps"), sem("rd_sb"),
                                                       sem("rg_ps"), sem("at_sb"))
        pro_sb, pt_ps, pt_sb, yt_ps, yt_sb = sem("pro_sb"), sem("pt_ps"), sem("pt_sb"), sem("yt_ps"), sem("yt_sb")
        fin_ps, fin_sb = sem("fin_ps"), sem("fin_sb")
        var_ready, rstd_ready = sem("b_var_ready"), sem("b_rstd_ready")
        stored = sem("out_stored")
        dve_passed, pe_passed = sem("b_dve_passed"), sem("b_pe_passed")
        own = sem("b_dve_own")
        LN_CALLS = 4
        block = ctx.enter_context(nc.Block())

        @block.sync
        def _(sp):
            src = dram["x2"].rearrange("(g t p) d -> g p t d", p=P, t=TILES)
            dst = dram["out"].rearrange("(g t p) d -> g p t d", p=P, t=TILES)
            sp.sem_inc(stored, 32)
            two = [(src_i, "src"), (dst_i, "dst")]
            for tile, name in two:
                sp.dma_start(tile[:, :], dram[name].rearrange("(o e) -> o e", o=1).to_broadcast([P, EDGES]))\
                    .then_inc(w_in, 16)
            for q, name in enumerate(("src", "dst")):
                sp.dma_start(ecol_i[:, q, :], dram[name + "_col"]).then_inc(w_in, 16)
            sp.dma_start(adjT[:, :], dram["adjT"]).then_inc(w_in, 16)
            sp.dma_start(W1[:, :, :], dram["L2_W1"].rearrange("(c p) n -> p c n", p=P)).then_inc(w_in, 16)
            sp.dma_start(b1[:, :], dram["L2_b1"].rearrange("(p o) -> p o", o=1)).then_inc(w_in, 16)
            sp.dma_start(W2[:, :], dram["L2_W2"]).then_inc(w_in, 16)
            sp.dma_start(b2[:, :], dram["L2_b2"].rearrange("(o d) -> o d", o=1).to_broadcast([P, D])).then_inc(w_in, 16)
            for q, name in enumerate(("W_linT", "W_valT")):
                sp.dma_start(Wlv[:, :, q * D:(q + 1) * D], dram[name].rearrange("(c p) n -> p c n", p=P))\
                    .then_inc(w_in, 16)
            sp.dma_start(Wout[:, :, :], dram["W_outT"].rearrange("(c p) n -> p c n", p=P)).then_inc(w_in, 16)
            sp.wait_ge(const, 6)
            for head in range(HEADS):
                c, s = head // 2, head % 2
                for at in (ROWS - HEADS + head, 2 * ROWS - HEADS + head):
                    sp.dma_start(APAD[s * N:(s + 1) * N, c, at:at + 1],
                                 dram["a"][head, :].rearrange("(f o) -> f o", o=1)).then_inc(w_in, 16)
            sp.dma_start(X[:, :, :], src[0]).then_inc(x_in, 16)
            for g in range(NGRP):
                if g + 1 < NGRP:
                    sp.wait_ge(x3_sb, 2 * (g + 1))
                    sp.dma_start(X[:, :, :], src[g + 1]).then_inc(x_in, 16)
                if g >= 1:
                    sp.wait_ge(fin_sb, 2 * (g + 1))
                    sp.dma_start(dst[g - 1], XR2[:, (g - 1) % 2, :, :]).then_inc(stored, 16)
            sp.wait_ge(fin_sb, 2 * (NGRP + 1))
            sp.dma_start(dst[NGRP - 1], XR2[:, (NGRP - 1) % 2, :, :]).then_inc(stored, 16)
            sp.wait_ge(stored, 16 * (NGRP + 2))

        @block.gpsimd
        def _(pool):
            g = nc.gpsimd
            g.memset(mhalf[:, :], -0.5).then_inc(const, 1)
            g.memset(ones[:, :], 1.0).then_inc(const, 1)
            g.memset(eps[:, :], 1e-8).then_inc(const, 1)
            g.memset(APAD[:, :, :], 0.0).then_inc(const, 1)
            g.iota(node_i[:, :], pattern=[[0, 1]], base=0, channel_multiplier=1).then_inc(const, 1)
            g.iota(col_i[:, :], pattern=[[0, 2], [1, N]], base=0, channel_multiplier=0).then_inc(const, 1)
            pool.wait_ge(const, 6)
            with pool.Fori(0, NGRP * LN_CALLS) as n:
                pool.wait_ge(var_ready, n + 1)
                g.tensor_tensor(rstd[:, :], var[:, :], mhalf[:, :], ALU.pow).then_inc(rstd_ready, 1)

        @block.tensor
        def _(pe):
            mm = nc.tensor.matmul
            pe.wait_ge(aa_in, 1)
            mm(ps[0:N, 0, :], adjT[:, :], DST[0:N, :], start=True, stop=True).then_inc(aa_ps, 1)
            pe.wait_ge(z_in, 1)
            mm(ps[:, 1, :], ones[:, :], ES[0:N, :], start=True, stop=True).then_inc(z_ps, 1)
            pe.wait_ge(loga_sb, 1)

            def spectral(turn, h, step):
                if step == 0:
                    pe.wait_ge(x_in, at(turn, 16, 16))
                    if h == 0:
                        pe.wait_ge(fin_sb, at(turn, 2, 0))
                    else:
                        pe.wait_ge(x3_sb, at(turn, 2, 1))
                    for c in range(2):
                        for t in range(HALF):
                            last = mm(ps[:, 5 + c, t * P:(t + 1) * P], X[:, 4 * h + t, c * P:(c + 1) * P],
                                      bdu[:, :], start=True, stop=True)
                    last.then_inc(ux_ps, 1)
                elif step == 1:
                    pe.wait_ge(ux_sb, at(turn, 2, h + 1))
                    for kc in range(2):
                        last = mm(ps[:, 7, :], W1[:, kc, :], FT[:, kc, h * HN:(h + 1) * HN],
                                  start=(kc == 0), stop=(kc == 1))
                    last.then_inc(hid_ps, 1)
                elif step == 2:
                    pe.wait_ge(hid_sb, at(turn, 2, h + 1))
                    for t in range(HALF):
                        last = mm(ps[:, 5 + t // 2, (t % 2) * D:(t % 2 + 1) * D],
                                  HT[:, (4 * h + t) * P:(4 * h + t + 1) * P], W2[:, :], start=True, stop=True)
                    last.then_inc(o2_ps, 1)
                else:
                    pe.wait_ge(o2_sb, at(turn, 2, h + 1))
                    for u in range(2):
                        last = mm(ps[:, 5 + u, :], bdut[:, :], Y[:, 4 * h + 2 * u:4 * h + 2 * u + 2, :],
                                  start=True, stop=True)
                    last.then_inc(x3_ps, 1)

            def queries(turn, par):
                for h in range(2):
                    pe.wait_ge(x3_sb, at(turn, 2, h + 1))
                    for c in range(2):
                        for t in range(HALF):
                            last = nc.tensor.transpose(ps[:, 2 * h + c, t * P:(t + 1) * P],
                                                       XR2[:, par, 4 * h + t, c * P:(c + 1) * P], ident[:, :])
                    last.then_inc(xt_ps, 1)
                pe.wait_ge(es_sb, at(turn, 1, 1))
                for h in range(2):
                    pe.wait_ge(xt_sb, at(turn, 2, 1 if h == 0 else 2))
                    for t in range(HALF):
                        for kc in range(2):
                            last = mm(ps[:, 4 * (1 - h) + t, :], FT[:, kc, (4 * h + t) * P:(4 * h + t + 1) * P],
                                      Wlv[:, kc, :], start=(kc == 0), stop=(kc == 1))
                    last.then_inc(qv_ps, 1)

            def pairs(turn, par, b):
                r = slice((b % 2) * N, (b % 2 + 1) * N)
                if b >= 2:
                    pe.wait_ge(lr_sb, at(turn, GB, b - 1))
                for c in range(2):
                    last = mm(ps[:, 2 * (b % 2) + c, :], QV2[r, par, b // 2, c * P:(c + 1) * P], GS[r, :],
                              start=True, stop=True)
                last.then_inc(pair_ps, 1)

            def scores(turn, b):
                pe.wait_ge(lr_sb, at(turn, GB, b + 1))
                if b == 0:
                    pe.wait_ge(fin_sb, at(turn, 2, 2))
                for c in range(2):
                    col0 = ROWS - HEADS - HEADS * b
                    last = mm(ps[:, 4, :], APAD[:, c, col0:col0 + P], LR[:, b % 2, c, :],
                              start=(b == 0 and c == 0), stop=(b == GB - 1 and c == 1))
                last.then_inc(score_ps, 1)

            def softmax(turn):
                pe.wait_ge(m_sb, at(turn, 1, 1))
                nc.tensor.transpose(ps[0:NH, 5, 0:P], m[:, :], ident[:, :]).then_inc(mT_ps, 1)
                pe.wait_ge(mT_sb, at(turn, 1, 1))
                mm(ps[0:ROWS, 6, :], mT[:, 0:ROWS], SRClo, start=True, stop=False)
                mm(ps[0:ROWS, 6, :], mT[:, ROWS:P], SRChi[:, :], start=False, stop=True).then_inc(mg_ps, 1)
                pe.wait_ge(ex_sb, at(turn, 1, 1))
                settle(pe, pe_passed)
                for c in range(CH):
                    last = nc.tensor.transpose(ps[:, 7, c * ROWS:(c + 1) * ROWS], EX[:, c * P:(c + 1) * P],
                                               ident[0:ROWS, 0:ROWS])
                last.then_inc(ext_ps, 1)
                pe.wait_ge(ext_sb, at(turn, 1, 1))
                for c in range(CH):
                    last = mm(ps[0:N, 5, 0:ROWS], SRCT[:, c, :], EXT[:, c, :], start=(c == 0), stop=(c == CH - 1))
                last.then_inc(den_ps, 1)
                pe.wait_ge(rd_sb, at(turn, 1, 1))
                for c in range(CH):
                    last = mm(ps[:, 6, c * ROWS:(c + 1) * ROWS], SRC[0:N, c * P:(c + 1) * P], RD[:, :], start=True,
                              stop=True)
                last.then_inc(rg_ps, 1)

            def node_matrices(turn, t):
                pe.wait_ge(pro_sb, at(turn, TILES, t + 1))
                if t >= 2:
                    pe.wait_ge(pt_sb, at(turn, TILES, t - 1))
                for c in range(CH):
                    last = mm(ps[:, t % 2, :], DSTT[:, c, :], PRO[:, t % 2, c, :, :], start=(c == 0),
                              stop=(c == CH - 1))
                last.then_inc(pt_ps, 1)

            def values(turn, par, t):
                pe.wait_ge(pt_sb, at(turn, TILES, t + 1))
                if t >= 2:
                    pe.wait_ge(yt_sb, at(turn, TILES, t - 1))
                for b in range(2):
                    r = slice(b * N, (b + 1) * N)
                    for c in range(2):
                        last = mm(ps[:, 2 + 2 * (t % 2) + b, c * P:(c + 1) * P],
                                  QV2[r, par, t, D + c * P:D + (c + 1) * P], PT[r, t % 2, 2 * c:2 * c + 2, :],
                                  start=True, stop=True)
                last.then_inc(yt_ps, 1)

            def one_turn(turn, nxt, par):
                pairs(turn, par, 0)
                for b in range(1, GB + 1):
                    if b < GB:
                        pairs(turn, par, b)
                    scores(turn, b - 1)
                    if nxt and b % 2 == 0:
                        spectral(nxt, (b // 2 - 1) // 4, (b // 2 - 1) % 4)
                if nxt:
                    queries(nxt, 1 - par)
                    pe.wait_ge(qv_sb, at(nxt, 2, 2))
                softmax(turn)
                node_matrices(turn, 0)
                for t in range(1, TILES + 1):
                    if t < TILES:
                        node_matrices(turn, t)
                    values(turn, par, t - 1)
                pe.wait_ge(yt_sb, at(turn, TILES, TILES))
                for h in range(2):
                    for t in range(HALF):
                        for kc in range(2):
                            last = mm(ps[:, 4 + 2 * h + t // 2, (t % 2) * D:(t % 2 + 1) * D],
                                      YT[:, kc, (4 * h + t) * P:(4 * h + t + 1) * P], Wout[:, kc, :],
                                      start=(kc == 0), stop=(kc == 1))
                    last.then_inc(fin_ps, 1)

            for h in range(2):
                for step in range(4):
                    spectral((0, 0), h, step)
            queries((0, 0), 0)
            pe.wait_ge(qv_sb, 2)
            with pe.Fori(0, NGRP // 2 - 1) as j:
                one_turn((j, 0), (j, 1), 0)
                one_turn((j, 1), (j, 2), 1)
            j = NGRP // 2 - 1
            one_turn((j, 0), (j, 1), 0)
            one_turn((j, 1), None, 1)

        @block.scalar
        def _(act):
            a = nc.scalar.activation
            act.wait_ge(z_ps, 1)
            act.wait_ge(w_in, B_DMAS * 16)
            act.wait_ge(const, 6)
            a(LOGA[:, :], ps[:, 1, :], ACT.Ln, bias=eps[:, 0:1]).then_inc(loga_sb, 1)

            def spectral(turn, h, step):
                if step == 0:
                    act.wait_ge(ux_ps, at(turn, 2, h + 1))
                    a(FT[:, :, h * HN:(h + 1) * HN], ps[:, 5:7, :], ACT.Copy).then_inc(ux_sb, 1)
                elif step == 1:
                    act.wait_ge(hid_ps, at(turn, 2, h + 1))
                    a(HT[:, h * HN:(h + 1) * HN], ps[:, 7, :], ACT.Relu, bias=b1[:, 0:1]).then_inc(hid_sb, 1)

            def queries(turn, par):
                for h in range(2):
                    act.wait_ge(xt_ps, at(turn, 2, h + 1))
                    a(FT[:, :, h * HN:(h + 1) * HN], ps[:, 2 * h:2 * h + 2, :], ACT.Copy).then_inc(xt_sb, 1)
                for h in range(2):
                    act.wait_ge(qv_ps, at(turn, 2, h + 1))
                    b = 4 * (1 - h)
                    a(QV2[:, par, 4 * h:4 * h + 4, :], ps[:, b:b + 4, :], ACT.Copy).then_inc(qv_sb, 1)

            def one_turn(turn, nxt, par):
                for b in range(GB):
                    act.wait_ge(pair_ps, at(turn, GB, b + 1))
                    if b >= 1:
                        act.wait_ge(lr_sb, at(turn, GB, b))
                    a(ABS[:, :, :], ps[:, 2 * (b % 2):2 * (b % 2) + 2, :], ACT.Abs, scale=0.4).then_inc(abs_sb, 1)
                    if nxt and b % 2 == 0 and b > 0:
                        spectral(nxt, (b // 2 - 1) // 4, (b // 2 - 1) % 4)
                if nxt:
                    queries(nxt, 1 - par)
                act.wait_ge(mT_ps, at(turn, 1, 1))
                a(mT[:, :], ps[0:NH, 5, 0:P], ACT.Copy).then_inc(mT_sb, 1)
                act.wait_ge(d_sb, at(turn, 1, 1))
                a(EX[:, :], ES[0:ROWS, :], ACT.Exp).then_inc(ex_sb, 1)
                act.wait_ge(ext_ps, at(turn, 1, 1))
                a(EXT[:, :, :], ps[:, 7, 0:CH * ROWS].rearrange("p (c r) -> p c r", c=CH), ACT.Copy)\
                    .then_inc(ext_sb, 1)
                for t in range(TILES + 1):
                    if t < TILES:
                        act.wait_ge(pt_ps, at(turn, TILES, t + 1))
                        for b in range(2):
                            r = slice(b * N, (b + 1) * N)
                            last = a(PT[r, t % 2, :, :],
                                     ps[r, t % 2, b * HEADS * N:(b + 1) * HEADS * N]
                                     .rearrange("p (h n) -> p h n", n=N), ACT.Copy)
                        last.then_inc(pt_sb, 1)
                    if t > 0:
                        q = t - 1
                        act.wait_ge(yt_ps, at(turn, TILES, q + 1))
                        o = ps[:, 2 + 2 * (q % 2):4 + 2 * (q % 2), 0:D].rearrange("p b (c s n) -> p b c s n", c=2, s=2)
                        y = YT[:, :, q * P:(q + 1) * P].rearrange("p c (b n) -> p b c n", b=2)
                        for s in range(2):
                            r = slice(s * N, (s + 1) * N)
                            last = a(y[r, :, :, :], o[r, :, :, s, :], ACT.Copy)
                        last.then_inc(yt_sb, 1)

            for h in range(2):
                for step in range(2):
                    spectral((0, 0), h, step)
            queries((0, 0), 0)
            with act.Fori(0, NGRP // 2 - 1) as j:
                one_turn((j, 0), (j, 1), 0)
                one_turn((j, 1), (j, 2), 1)
            j = NGRP // 2 - 1
            one_turn((j, 0), (j, 1), 0)
            one_turn((j, 1), None, 1)

        @block.vector
        def _(dve):
            v = nc.vector
            done = [0]

            def made(ins):
                done[0] += 1
                ins.then_inc(prep, 1)
                dve.wait_ge(prep, done[0])

            dve.wait_ge(const, 6)
            dve.wait_ge(w_in, B_DMAS * 16)
            made(v.tensor_copy(node[:, :], node_i[:, :]))
            made(v.tensor_scalar(EXT[:, 0, 0:1], node[:, :], float(N), -float(N), ALU.is_ge, ALU.mult))
            made(v.tensor_scalar(EXT[:, 0, 1:2], EXT[:, 0, 0:1], 0.5, None, ALU.mult))
            made(v.tensor_tensor(node[:, :], node[:, :], EXT[:, 0, 0:1], ALU.add))
            made(v.tensor_scalar(RD[0:NH, 0:1], node[0:NH, :], float(NH), None, ALU.add))
            made(v.tensor_copy(colm[:, :], col_i[:, :]))
            made(v.tensor_copy(src_f[:, :], src_i[:, :]))
            made(v.tensor_copy(dst_f[:, :], dst_i[:, :]))
            made(v.tensor_copy(ecol[:, :, :], ecol_i[:, :, :]))
            made(v.tensor_scalar(SRC[:, :], src_f[:, :], node[:, 0:1], None, ALU.is_equal))
            v.tensor_scalar(DST[:, :], dst_f[:, :], node[:, 0:1], None, ALU.is_equal).then_inc(aa_in, 1)
            dve.wait_ge(aa_in, 1)
            made(v.tensor_scalar(SRChi[:, :], src_f[0:NH, :], RD[0:NH, 0:1], None, ALU.is_equal))
            made(v.tensor_tensor(GS[:, :], SRC[:, :], DST[:, :], ALU.add))
            for c in range(CH):
                made(v.tensor_scalar(SRCT[:, c, :], colm[:, 0:N], ecol[:, 0, c:c + 1], None, ALU.is_equal))
                made(v.tensor_scalar(DSTT[:, c, :], colm[:, :], ecol[:, 1, c:c + 1], None, ALU.is_equal))
            dve.wait_ge(aa_ps, 1)
            v.tensor_tensor(ES[0:N, :], ps[0:N, 0, :], SRC[0:N, :], ALU.mult).then_inc(z_in, 1)
            made(v.tensor_scalar(src_f[:, :], src_f[:, :], EXT[:, 0, 1:2], None, ALU.add))
            for n in range(NH):
                made(v.tensor_scalar(NEG[:, n, :], src_f[:, :], float(n), -1e30, ALU.not_equal, ALU.mult))
            v.memset(var[:, :], 0.0).then_inc(fin_sb, 2)
            dve.wait_ge(loga_sb, 1)
            v.memset(m[:, :], 0.0).then_inc(es_sb, 1)

            def link(ins):
                n_own[0] += 1
                ins.then_inc(own, 1)
                dve.wait_ge(own, add(link_base[0], n_own[0]))

            def finish_rows(turn, h, ln_at, dst, banks, x, done_sem):
                rows = dst[:, 4 * h:4 * h + 4, :]
                link(v.tensor_tensor(rows, x[:, 4 * h:4 * h + 4, :],
                                     ps[:, banks:banks + 2, :].rearrange("p b (t n) -> p (b t) n", n=D), ALU.add))
                ln_value[0] = ln_at
                layer_norm(nc, dve, link, ln_value, rows, stats, mv, var, rstd, var_ready, rstd_ready, dve_passed)\
                    .then_inc(done_sem, 1)

            def spectral(turn, par, h, step):
                if step == 2:
                    dve.wait_ge(o2_ps, at(turn, 2, h + 1))
                    v.tensor_tensor(Y[:, 4 * h:4 * h + 4, :],
                                    ps[:, 5:7, :].rearrange("p b (t n) -> p (b t) n", n=D), across(b2, HALF),
                                    ALU.add).then_inc(o2_sb, 1)
                elif step == 3:
                    dve.wait_ge(x3_ps, at(turn, 2, h + 1))
                    if h == 0:
                        dve.wait_ge(stored, at(turn, 16, 16))
                    finish_rows(turn, h, h if turn is FIRST else at(turn, LN_CALLS, h - 2), XR2[:, par, :, :], 5, X, x3_sb)

            def one_turn(turn, nxt, par):
                XR = XR2[:, par, :, :]
                for b in range(GB):
                    dve.wait_ge(abs_sb, at(turn, GB, b + 1))
                    if b >= 2:
                        dve.wait_ge(score_ps, at(turn, GB, b - 1))
                    v.scalar_tensor_tensor(LR[:, b % 2, :, :], ps[:, 2 * (b % 2):2 * (b % 2) + 2, :], 0.6,
                                           ABS[:, :, :], ALU.mult, ALU.add).then_inc(lr_sb, 1)
                    if nxt and b % 2 == 0 and b > 0:
                        spectral(nxt, 1 - par, (b // 2 - 1) // 4, (b // 2 - 1) % 4)
                if nxt:
                    spectral(nxt, 1 - par, 1, 3)
                dve.wait_ge(score_ps, at(turn, GB, GB))
                v.tensor_tensor(ES[:, :], ps[:, 4, :], LOGA[:, :], ALU.add).then_inc(es_sb, 1)
                dve.wait_ge(es_sb, at(turn, 1, 2))
                settle(dve, dve_passed)
                for n in range(NH):
                    last = v.tensor_tensor_reduce(mjunk[:, n % JUNK, :], ES[:, :], NEG[:, n, :], 1.0, -3e38, ALU.add,
                                                  ALU.max, m[:, n:n + 1])
                    if n % JUNK == JUNK - 1 and n < NH - 1:
                        link(last)
                        settle(dve, dve_passed)
                last.then_inc(m_sb, 1)
                dve.wait_ge(mg_ps, at(turn, 1, 1))
                v.tensor_tensor(ES[0:ROWS, :], ES[0:ROWS, :], ps[0:ROWS, 6, :], ALU.subtract).then_inc(d_sb, 1)
                dve.wait_ge(den_ps, at(turn, 1, 1))
                link(v.tensor_scalar(RD[:, :], ps[0:N, 5, 0:ROWS], TINY, None, ALU.max))
                v.reciprocal(RD[:, :], RD[:, :]).then_inc(rd_sb, 1)
                dve.wait_ge(rg_ps, at(turn, 1, 1))
                v.tensor_tensor(AT[:, :, :], EXT[:, :, :],
                                ps[:, 6, 0:CH * ROWS].rearrange("p (c r) -> p c r", c=CH), ALU.mult).then_inc(at_sb, 1)
                dve.wait_ge(at_sb, at(turn, 1, 1))
                for t in range(TILES):
                    if t >= 2:
                        dve.wait_ge(pt_ps, at(turn, TILES, t - 1))
                    for c in range(CH):
                        last = v.tensor_tensor(
                            PRO[:, t % 2, c, :, :],
                            SRCT[:, c, :].rearrange("p (o n) -> p o n", o=1).to_broadcast([P, 8, N]),
                            col(AT[:, c, 8 * t:8 * t + 8]).to_broadcast([P, 8, N]), ALU.mult)
                    last.then_inc(pro_sb, 1)
                for h in range(2):
                    dve.wait_ge(fin_ps, at(turn, 2, h + 1))
                    finish_rows(turn, h, at(turn, LN_CALLS, (4 if nxt else 2) + h), XR, 4 + 2 * h, XR, fin_sb)

            n_own, link_base, ln_value = [0], [0], [0]
            for h in range(2):
                spectral(FIRST, 0, h, 2)
                spectral(FIRST, 0, h, 3)
            first, per = n_own[0], keep["dve_links_b"]
            with dve.Fori(0, NGRP // 2 - 1) as j:
                n_own[0], link_base[0] = first, dve.snap(j * (2 * per))
                one_turn((j, 0), (j, 1), 0)
                one_turn((j, 1), (j, 2), 1)
                assert n_own[0] == first + 2 * per, n_own[0] - first
            j = NGRP // 2 - 1
            link_base[0] = (j - 1) * 2 * per
            one_turn((j, 0), (j, 1), 0)
            one_turn((j, 1), None, 1)


B_DMAS = 20


def build(nc, x, adj, adjT, Wg0, bg0, Wg1, bg1, WihT, WhhT, bih, bhh, L1_W1, L1_W2, L1_W3, L2_W1, L2_b1, L2_W2, L2_b2,
          W_linT, W_valT, W_outT, a, src, dst, src_col,
          dst_col, out):
    dram = dict(x=x, adj=adj, adjT=adjT, L2_W1=L2_W1, L2_b1=L2_b1, L2_W2=L2_W2, L2_b2=L2_b2, W_linT=W_linT,
                W_valT=W_valT, W_outT=W_outT, a=a, src=src, dst=dst, src_col=src_col,
                dst_col=dst_col, out=out)
    dram["x2"] = nc.dram_tensor("x2_scratch", (BATCH * T, D), F32).ap()
    with ExitStack() as ctx:
        keep = {n: ctx.enter_context(nc.sbuf_tensor(n, [P, P], F32))
                for n in ("ident", "bd_adjT", "bd_wT", "bd_U", "bd_UT")}
        keep["lap"] = Laplacian(lambda n, sh, dt: ctx.enter_context(nc.sbuf_tensor(n, sh, dt)),
                                lambda n: ctx.enter_context(nc.semaphore(n)))
        keep["lap"].ident = keep["ident"]
        weights_in = ctx.enter_context(nc.semaphore("weights_in"))
        stored_credit = 0

        def wait_stored(eng, stored, i):
            eng.wait_ge(stored, i * 16 + 16)

        keep["wait_stored"] = wait_stored
        with ExitStack() as ctx_w:
            def sb(name, shape):
                return ctx_w.enter_context(nc.sbuf_tensor(name, shape, F32))

            w = dict(bg0=sb("w_bg0", [1, D]), rowsum=sb("w_rowsum", [1, HN]), Wg0=sb("w_g0", [P, 2, D]),
                     Wg1=sb("w_g1", [P, 2, D]), bg1=sb("w_bg1", [P, D]), Wih=sb("w_ih", [P, MAX_SKIP, 2, 4 * D]),
                     Whh=sb("w_hh", [P, MAX_SKIP - 1, 2, 4 * D]), bias=sb("w_bias", [P, 32]),
                     bih=sb("w_bih", [P, 32]), W1=sb("w_1", [P, 2, 512]), W2=sb("w_2", [P, 4, 1024]),
                     W3=sb("w_3", [P, 8, D]))
            keep["w"] = w
            by_rows = "(c p) n -> p c n"
            loads = [(w["bg0"][:, :], bg0.rearrange("(o d) -> o d", o=1)),
                     (w["Wg0"][:, :, :], Wg0.rearrange(by_rows, p=P)),
                     (w["Wg1"][:, :, :], Wg1.rearrange(by_rows, p=P)),
                     (w["bg1"][:, :], bg1.rearrange("(o d) -> o d", o=1).to_broadcast([P, D])),
                     (w["bias"][:, :], bih), (w["bih"][:, :], bhh),
                     (w["W1"][:, :, :], L1_W1.rearrange(by_rows, p=P)),
                     (w["W2"][:, :, :], L1_W2.rearrange(by_rows, p=P)),
                     (w["W3"][:, :, :], L1_W3.rearrange(by_rows, p=P))]
            loads += [(w["Wih"][:, p, :, :], WihT[p].rearrange(by_rows, p=P)) for p in range(MAX_SKIP)]
            loads += [(w["Whh"][:, p - 1, :, :], WhhT[p].rearrange(by_rows, p=P)) for p in range(1, MAX_SKIP)]

            def load_weights(sp):
                for d, s in loads:
                    sp.dma_start(d, s).then_inc(weights_in, 16)

            keep["load_weights"] = load_weights
            keep["weights_wait"] = lambda eng: eng.wait_ge(weights_in, 16 * len(loads))
            keep["dve_links_a"] = LINKS_A
            prepare(nc, dram, keep)
            layers_0_1(nc, dram, keep)
        keep["dve_links_b"] = LINKS_B
        eigenvectors(nc, keep)
        layers_2_3(nc, dram, keep)


LINKS_A = 24 + 24 * STEPS_A_TURN
LINKS_B = 16

_OUT = (BATCH, T, D)


def kernel(**inputs):
    import numpy as _np
    import concourse.bacc as _bacc
    from concourse import mybir as _mybir
    from concourse.bass_utils import run_bass_kernel_spmd as _run

    i = {k: _np.asarray(v) for k, v in inputs.items()}

    def by_chunk(b):
        return b.reshape(MAX_SKIP, 8, P).transpose(2, 0, 1).reshape(P, MAX_SKIP * 8)

    laid = dict(
        x=i["x"].reshape(BATCH * T, D), adj=i["adj"], adjT=i["adj"].T, Wg0=i["L0_gnn_Wg0"], bg0=i["L0_gnn_bg0"],
        Wg1=i["L0_gnn_Wg1"], bg1=i["L0_gnn_bg1"], WihT=i["L0_gnn_Wih"].transpose(0, 2, 1),
        WhhT=i["L0_gnn_Whh"].transpose(0, 2, 1), bih=by_chunk(i["L0_gnn_bih"]), bhh=by_chunk(i["L0_gnn_bhh"]),
        L1_W1=i["L1_gnn_W1"], L1_W2=i["L1_gnn_W2"], L1_W3=i["L1_gnn_W3"], L2_W1=i["L2_gnn_W1"],
        L2_b1=i["L2_gnn_b1"], L2_W2=i["L2_gnn_W2"], L2_b2=i["L2_gnn_b2"], W_linT=i["L3_gnn_W_lin"].T,
        W_valT=i["L3_gnn_W_val"].T, W_outT=i["L3_gnn_W_out"].T, a=i["L3_gnn_a"], src=i["L3_gnn_src"],
        dst=i["L3_gnn_dst"], src_col=i["L3_gnn_src"].reshape(-1, P).T, dst_col=i["L3_gnn_dst"].reshape(-1, P).T)
    nc = _bacc.Bacc("TRN2", target_bir_lowering=False, num_devices=1)
    arrays, args = {}, {}
    for name, a in laid.items():
        a = _np.ascontiguousarray(a)
        arrays[f"in_{name}"] = a
        args[name] = nc.dram_tensor(f"in_{name}", a.shape, _mybir.dt.from_np(a.dtype), kind="ExternalInput").ap()
    out = nc.dram_tensor("out_0", (BATCH * T, D), _mybir.dt.float32, kind="ExternalOutput").ap()
    build(nc, out=out, **args)
    r = _run(nc, [arrays], core_ids=[0])
    return r.results[0]["out_0"].reshape(_OUT)
```

```python
from contextlib import ExitStack

import concourse.bass as bass
from concourse import mybir

ALU = mybir.AluOpType
ACT = mybir.ActivationFunctionType
F32 = mybir.dt.float32
BF16 = mybir.dt.bfloat16
F32R = mybir.dt.float32r
I32 = mybir.dt.int32
AX_X = mybir.AxisListType.X

BATCH, T, D = 128, 64, 256
P = 128
GB = 16
NGRP = BATCH // GB
GT = GB * T
TILES = GT // P
HALF = TILES // 2
HN = HALF * P
EDGES = 512
HEADS = 4
CH = EDGES // P
ROWS = GB * HEADS
NH = T // 2
LN_EPS = 1e-5
TINY = 1e-30
MAX_SKIP = 4
SECTIONS = 32
MID = T // 2
PASSES = 5


class Laplacian:

    def __init__(self, sb, sem):
        N = T
        self.pidx = sb("pidx_f", [P, P], F32)
        self.iota = sb("iota", [P, P], F32)
        self.ones = sb("ones", [N, P], F32)
        self.neg_id = sb("neg_id", [P, N], F32)
        self.is_q = sb("is_q", [P, 1], F32)
        self.half_pow = sb("half_pow", [P, 1], F32)
        self.mhalf_pow = sb("mhalf_pow", [P, 1], F32)
        self.M = sb("M", [P, N], F32)
        self.V = sb("V", [P, N], F32)
        self.Vr = sb("Vr", [P, N], F32)
        self.Wr = sb("Wr", [P, N], F32)
        self.OH = sb("OH", [P, N], F32)
        self.MK = sb("MK", [P, N], F32)
        self.SEL = sb("SEL", [N, P], F32)
        self.DG = sb("DG", [N, N], F32)
        self.junk = sb("junk", [P, 6, N], F32)
        self.sc = sb("sc", [P, 32], F32)
        self.k1 = sb("k1", [P, 1], F32)
        self.sel_ok = sem("sel_ready")
        self.row_ok = sem("row_ready")
        self.n2_ok = sem("n2_ready")
        self.nrm_ok = sem("norm_ready")
        self.dg_ok = sem("diag_ready")
        self.w_ok = sem("w_ready")


STEPS_A_TURN = 8


def reflect(nc, dve, link, lap, row_ps, w_ps, k):
    N = T
    v = nc.vector
    M, V, Vr, Wr, OH, MK, sc, k1, junk = lap.M, lap.V, lap.Vr, lap.Wr, lap.OH, lap.MK, lap.sc, lap.k1, lap.junk
    link(v.tensor_scalar(OH[:, :], lap.iota[:, 0:N], k1[:, 0:1], None, ALU.is_equal), wait=False)
    link(v.tensor_scalar(MK[:, :], lap.iota[:, 0:N], k1[:, 0:1], None, ALU.is_gt))
    dve.wait_ge(lap.row_ok, k + 1)
    link(v.tensor_tensor(Vr[:, :], row_ps, MK[:, :], ALU.mult), wait=False)
    link(v.tensor_tensor_reduce(junk[:, 0, :], row_ps, OH[:, :], 1.0, 0.0, ALU.mult, ALU.add,
                                 sc[:, 11:12]))
    link(v.tensor_tensor_reduce(junk[:, 1, :], Vr[:, :], Vr[:, :], 1.0, TINY, ALU.mult, ALU.add,
                                 sc[:, 12:13]))
    link(v.scalar_tensor_tensor(sc[:, 3:4], sc[:, 11:12], sc[:, 11:12], sc[:, 12:13], ALU.mult,
                                 ALU.add))
    link(v.tensor_scalar(sc[:, 13:14], sc[:, 11:12], 0.0, 2.0, ALU.is_ge, ALU.mult))
    v.tensor_scalar(sc[:, 14:15], sc[:, 13:14], -1.0, None, ALU.add).then_inc(lap.n2_ok, 1)
    dve.wait_ge(lap.n2_ok, k + 1)
    dve.wait_ge(lap.nrm_ok, k + 1)
    link(v.scalar_tensor_tensor(sc[:, 15:16], sc[:, 4:5], sc[:, 14:15], sc[:, 11:12], ALU.mult,
                                 ALU.add))
    link(v.scalar_tensor_tensor(V[:, :], OH[:, :], sc[:, 15:16], Vr[:, :], ALU.mult, ALU.add))
    link(v.scalar_tensor_tensor(sc[:, 16:17], sc[:, 15:16], sc[:, 15:16], sc[:, 12:13], ALU.mult,
                                 ALU.add))
    link(v.reciprocal(sc[:, 17:18], sc[:, 16:17]), wait=False)
    link(v.tensor_scalar(sc[:, 18:19], sc[:, 12:13], 2.0 * TINY, 2.0, ALU.is_gt, ALU.mult))
    link(v.tensor_tensor(sc[:, 19:20], sc[:, 17:18], sc[:, 18:19], ALU.mult), wait=False)
    link(v.tensor_tensor_reduce(junk[:, 2, :], M[:, :], V[:, :], 1.0, 0.0, ALU.mult, ALU.add,
                                 sc[:, 20:21]))
    link(v.tensor_tensor(sc[:, 21:22], sc[:, 20:21], sc[:, 19:20], ALU.mult))
    v.tensor_scalar(lap.DG[:, :], lap.ident[0:N, 0:N], sc[0:N, 21:22], None, ALU.mult).then_inc(lap.dg_ok, 1)
    link(v.tensor_tensor_reduce(junk[:, 3, :], V[:, :], lap.neg_id[:, :], 1.0, 0.0, ALU.mult, ALU.add,
                                 sc[:, 22:23]), wait=False)
    link(v.tensor_tensor(sc[:, 23:24], sc[:, 21:22], lap.is_q[:, :], ALU.mult))
    dve.wait_ge(lap.w_ok, k + 1)
    link(v.tensor_tensor_reduce(junk[:, 4, :], w_ps, V[:, :], 1.0, 0.0, ALU.mult, ALU.add,
                                 sc[:, 24:25]))
    link(v.tensor_scalar(sc[:, 25:26], sc[:, 24:25], sc[:, 19:20], -0.5, ALU.mult, ALU.mult))
    link(v.scalar_tensor_tensor(Wr[:, :], V[:, :], sc[:, 25:26], w_ps, ALU.mult, ALU.add))
    link(v.tensor_tensor_reduce(junk[:, 5, :], Wr[:, :], lap.neg_id[:, :], 1.0, sc[:, 23:24], ALU.mult,
                                 ALU.add, sc[:, 26:27]), wait=False)
    link(v.scalar_tensor_tensor(M[:, :], Wr[:, :], sc[:, 22:23], M[:, :], ALU.mult, ALU.add))
    link(v.scalar_tensor_tensor(M[:, :], V[:, :], sc[:, 26:27], M[:, :], ALU.mult, ALU.add), wait=False)
    link(v.tensor_scalar(k1[:, :], k1[:, :], 1.0, None, ALU.add))
    v.tensor_scalar(lap.SEL[:, :], lap.pidx[0:N, :], k1[0:N, 0:1], -1.0, ALU.subtract, ALU.is_equal).then_inc(lap.sel_ok, 1)


def prepare(nc, dram, keep):
    N = T
    with ExitStack() as ctx:
        def sb(name, shape, dt=F32):
            return ctx.enter_context(nc.sbuf_tensor(name, shape, dt))

        def sem(name):
            return ctx.enter_context(nc.semaphore(name))

        ps = ctx.enter_context(nc.psum_tensor("ps_prep", [P, 8, 512], F32))
        adj = sb("adj_sb", [P, N])
        adjT = sb("adjT_sb", [P, N])
        pidx = sb("pidx", [P, P], I32)
        iota_i = sb("iota_i", [P, P], I32)
        ident, lap = keep["ident"], keep["lap"]
        pidx_f, iota, ones, neg_id, is_q = lap.pidx, lap.iota, lap.ones, lap.neg_id, lap.is_q
        M, V, Vr, Wr, OH, MK, SEL, DG = lap.M, lap.V, lap.Vr, lap.Wr, lap.OH, lap.MK, lap.SEL, lap.DG
        sc, k1, junk = lap.sc, lap.k1, lap.junk

        loaded = sem("adj_loaded")
        made = sem("consts_made")
        link_s = sem("dve_link")
        pw_in = sem("pow_in")
        pw_out = sem("pow_out")
        tr_in = sem("tr_in")
        tr_out = sem("tr_out")

        block = ctx.enter_context(nc.Block())

        @block.sync
        def _(sp):
            for half in range(2):
                rows = slice(half * N, half * N + N)
                sp.dma_start(adj[rows, :], dram["adj"]).then_inc(loaded, 16)
                sp.dma_start(adjT[rows, :], dram["adjT"]).then_inc(loaded, 16)
            keep["load_weights"](sp, "layer 0")

        @block.gpsimd
        def _(pool):
            nc.gpsimd.iota(pidx[:, :], pattern=[[0, P]], base=0, channel_multiplier=1).then_inc(made, 1)
            nc.gpsimd.iota(iota_i[:, :], pattern=[[1, P]], base=0, channel_multiplier=0).then_inc(made, 1)
            nc.gpsimd.memset(lap.half_pow[:, :], 0.5).then_inc(made, 1)
            nc.gpsimd.memset(lap.mhalf_pow[:, :], -0.5).then_inc(made, 1)
            nc.gpsimd.memset(ones[:, :], 1.0).then_inc(made, 1)
            pool.wait_ge(made, 5)
            pool.wait_ge(pw_in, 1)
            nc.gpsimd.tensor_tensor(sc[:, 1:2], sc[:, 0:1], lap.mhalf_pow[:, 0:1], ALU.pow).then_inc(pw_out, 1)

        @block.tensor
        def _(pe):
            pe.wait_ge(tr_in, 1)
            nc.tensor.matmul(ps[0:N, 7, 0:N], ones[:, 0:N], DG[:, :], start=True, stop=True)
            nc.tensor.matmul(ps[0:N, 7, N:2 * N], ones[:, 0:N], adjT[0:N, :], start=True, stop=True)\
                .then_inc(tr_out, 1)

        @block.vector
        def _(dve):
            done = [0]

            def link(ins):
                done[0] += 1
                ins.then_inc(link_s, 1)
                dve.wait_ge(link_s, done[0])

            v = nc.vector
            dve.wait_ge(made, 5)
            dve.wait_ge(loaded, 64)
            link(v.tensor_copy(pidx_f[:, :], pidx[:, :]))
            link(v.tensor_copy(iota[:, :], iota_i[:, :]))
            link(v.tensor_tensor(ident[:, :], pidx_f[:, :], iota[:, :], ALU.is_equal))
            link(v.tensor_scalar(is_q[:, :], pidx_f[:, 0:1], float(N), -1.0, ALU.is_ge, ALU.mult))
            link(v.memset(neg_id[:, :], 0.0))
            link(v.tensor_scalar(neg_id[0:N, :], ident[0:N, 0:N], -1.0, None, ALU.mult))
            bda, bdw = keep["bd_adjT"], keep["bd_wT"]
            link(v.memset(bda[:, :], 0.0))
            link(v.memset(bdw[:, :], 0.0))
            for half in range(2):
                r = slice(half * N, half * N + N)
                v.tensor_copy(bda[r, r], adjT[r, :])
                link(v.tensor_tensor(bdw[r, r], adjT[r, :], adjT[r, :], ALU.mult))
            link(v.tensor_reduce(sc[:, 5:6], adj[:, :], AX_X, ALU.add))
            link(v.tensor_reduce(sc[:, 6:7], adjT[:, :], AX_X, ALU.add))
            link(v.memset(OH[:, :], 0.0))
            for half in range(2):
                r = slice(half * N, half * N + N)
                link(v.tensor_copy(OH[r, :], ident[r, r]))
            link(v.tensor_tensor_reduce(junk[:, 0, :], adj[:, :], OH[:, :], 1.0, 0.0, ALU.mult, ALU.add, sc[:, 7:8]))
            link(v.tensor_tensor(sc[:, 8:9], sc[:, 5:6], sc[:, 6:7], ALU.add))
            link(v.tensor_tensor(sc[:, 9:10], sc[:, 8:9], sc[:, 7:8], ALU.subtract))
            link(v.tensor_scalar(sc[:, 10:11], sc[:, 9:10], 0.0, None, ALU.is_gt))
            v.tensor_scalar(sc[:, 0:1], sc[:, 9:10], 1e-37, None, ALU.max).then_inc(pw_in, 1)
            dve.wait_ge(pw_out, 1)
            link(v.tensor_tensor(sc[:, 2:3], sc[:, 1:2], sc[:, 10:11], ALU.mult))
            link(v.tensor_scalar(Vr[:, :], OH[:, :], sc[:, 9:10], None, ALU.mult))
            link(v.tensor_tensor(V[:, :], Vr[:, :], adj[:, :], ALU.subtract))
            link(v.tensor_tensor(Wr[:, :], Vr[:, :], adjT[:, :], ALU.subtract))
            link(v.tensor_tensor(MK[:, :], V[:, :], Wr[:, :], ALU.add))
            link(v.tensor_scalar(MK[:, :], MK[:, :], sc[:, 2:3], 0.5, ALU.mult, ALU.mult))
            link(v.tensor_scalar(DG[:, :], ident[0:N, 0:N], sc[0:N, 2:3], None, ALU.mult))
            v.memset(SEL[:, :], 0.0).then_inc(tr_in, 1)
            dve.wait_ge(tr_out, 1)
            link(v.tensor_tensor(M[0:N, :], MK[0:N, :], ps[0:N, 7, 0:N], ALU.mult))
            keep["weights_wait"](dve, "layer 0")
            w = keep["w"]
            link(v.tensor_copy(w["rowsum"][0:1, :].rearrange("p (b n) -> p b n", n=N),
                               ps[0:1, 7, N:2 * N].rearrange("p (o n) -> p o n", o=1).to_broadcast([1, HN // N, N])))
            link(v.tensor_tensor(w["bias"][:, :], w["bias"][:, :], w["bih"][:, :], ALU.add))
            link(v.tensor_copy(M[N:P, :], ident[N:P, N:P]))
            link(v.memset(k1[:, :], 1.0))
            link(v.tensor_scalar(SEL[:, :], pidx_f[0:N, :], 0.0, None, ALU.is_equal))
            v.memset(sc[:, 30:31], 0.0).then_inc(lap.sel_ok, 1)


class EdgeData:

    def __init__(self, sb, sem):
        N = T
        self.W1 = sb("b_W1", [P, 2, 128])
        self.b1 = sb("b_b1", [P, 1])
        self.W2 = sb("b_W2", [P, D])
        self.b2 = sb("b_b2", [P, D])
        self.Wlv = sb("b_Wlv", [P, 2, 2 * D])
        self.Wout = sb("b_Wout", [P, 2, D])
        self.APAD = sb("b_apad", [P, 2, ROWS - HEADS + P])
        self.adjT = sb("b_adjT", [N, N])
        self.YT = sb("b_yt", [P, 2, GT])
        self.src_i, self.dst_i = (self.YT[:, 0, q * EDGES:(q + 1) * EDGES].bitcast(I32) for q in range(2))
        self.src_f, self.dst_f = (self.YT[:, 1, q * EDGES:(q + 1) * EDGES] for q in range(2))
        self.ecol_i = sb("b_ecol_i", [P, 2, CH], I32)
        self.ecol = sb("b_ecol", [P, 2, CH])
        self.node_i = sb("b_node_i", [P, 1], I32)
        self.node = sb("b_node", [P, 1])
        self.col_i = sb("b_col_i", [P, P], I32)
        self.colm = sb("b_colm", [P, P])
        self.SRC = sb("b_src1h", [P, EDGES])
        self.DST = sb("b_dst1h", [P, EDGES])
        self.GS = sb("b_gs", [P, EDGES], F32R)
        self.SRCT = sb("b_srcT", [P, CH, N])
        self.DSTT = sb("b_dstT", [P, CH, P], F32R)
        self.SRClo = self.SRC[0:NH, :]
        self.SRChi = sb("b_src1h_hi", [NH, EDGES])
        self.NEG = sb("b_neg", [P, NH, EDGES], BF16)
        self.LOGA = sb("b_loga", [P, EDGES])
        self.eps = sb("b_eps", [P, 1])
        self.X = sb("b_x", [P, TILES, D])
        self.ES = sb("b_es", [P, EDGES])
        self.mhalf = sb("b_mhalf", [P, HALF])
        self.tmp = sb("b_tmp", [P, 3])
        self.w_in = sem("b_weights")
        self.const = sem("b_const")
        self.prep = sem("b_prep")
        self.aa_in, self.aa_ps, self.aa_sb = sem("aa_in"), sem("aa_ps"), sem("aa_sb")
        self.z_in, self.z_ps = sem("z_in"), sem("z_ps")
        self.x_in = sem("b_x_loaded")


def eigenvectors(nc, dram, keep):
    N = T
    with ExitStack() as ctx:
        def sb(name, shape, dt=F32):
            return ctx.enter_context(nc.sbuf_tensor(name, shape, dt))

        def sem(name):
            return ctx.enter_context(nc.semaphore(name))

        ident, lap = keep["ident"], keep["lap"]
        pidx_f, iota, ones, neg_id, is_q = lap.pidx, lap.iota, lap.ones, lap.neg_id, lap.is_q
        M, V, Vr, Wr, OH, MK, SEL, DG = lap.M, lap.V, lap.Vr, lap.Wr, lap.OH, lap.MK, lap.SEL, lap.DG
        sc, k1, junk = lap.sc, lap.k1, lap.junk
        ps = ctx.enter_context(nc.psum_tensor("ps_e", [P, 8, 512], F32))
        D_ = sb("Drow", [P, N])
        E_all = sb("Erow", [P, N])
        nE2_all = sb("nE2", [P, N])
        D_end = sb("D_end", [P, MID])
        nE2_end = sb("nE2_end", [P, MID])
        pair_sum = sb("pair_sum", [P, P])
        DL = sb("DL", [P, MID, SECTIONS])
        neg = sb("neg", [P, MID, SECTIONS])
        halves = sb("halves", [P, 2, SECTIONS])
        lam = sb("lam", [P, SECTIONS])
        steps = sb("steps", [P, SECTIONS])
        rc = sb("rc", [P, SECTIONS])
        cnt = sb("cnt", [P, SECTIONS])
        st_lanes = sb("st", [P, 64])
        PD = sb("PD", [N, N, 8])
        QP = sb("QP", [N, N, 8])
        nE2P = sb("nE2P", [N, N, 8])
        nEP = sb("nEP", [N, N, 2])
        RP = sb("RP", [N, N, 2])
        ZP = sb("ZP", [N, N, 2])
        gam = sb("gam", [N, N])
        dlt = sb("dlt", [N, N])
        Z = sb("Z", [N, N])
        BE = sb("BEc", [N, 32, 6])
        BC = sb("BCc", [N, 32, 6])
        BZ = sb("BZc", [N, 32, 6])
        BM = sb("BMc", [N, 32, 6])
        QT2 = sb("QT2", [N, P])
        Z2 = sb("Z2", [N, P])
        Zs = sb("Zs", [N, N])

        link_s = sem("e_dve_link")
        ms = sem("ms_link")
        halves_in, halves_out = sem("halves_ready"), sem("pair_sums_ready")
        pw_in, pw_out = sem("e_pow_in"), sem("e_pow_out")
        tr_in, tr_out = sem("e_tr_in"), sem("e_tr_out")
        E = keep["edges"]
        W1, b1, W2, b2, Wlv, Wout, APAD, adjT = \
            E.W1, E.b1, E.W2, E.b2, E.Wlv, E.Wout, E.APAD, E.adjT
        src_i, dst_i, src_f, dst_f, ecol_i, ecol, node_i, node = \
            E.src_i, E.dst_i, E.src_f, E.dst_f, E.ecol_i, E.ecol, E.node_i, E.node
        col_i, colm, SRC, DST, GS, SRCT, DSTT, SRChi = \
            E.col_i, E.colm, E.SRC, E.DST, E.GS, E.SRCT, E.DSTT, E.SRChi
        NEG, LOGA, eps, X, ES, mhalf, tmp = E.NEG, E.LOGA, E.eps, E.X, E.ES, E.mhalf, E.tmp
        w_in, const, prep, aa_in, aa_ps, aa_sb, z_in, z_ps = \
            E.w_in, E.const, E.prep, E.aa_in, E.aa_ps, E.aa_sb, E.z_in, E.z_ps
        x_in = E.x_in

        def load(sp):
            src = dram["x2"].rearrange("(g t p) d -> g p t d", p=P, t=TILES)
            two = [(src_i, "src"), (dst_i, "dst")]
            for tile, name in two:
                sp.dma_start(tile[:, :], dram[name].rearrange("(o e) -> o e", o=1).to_broadcast([P, EDGES]))\
                    .then_inc(w_in, 16)
            for q, name in enumerate(("src", "dst")):
                sp.dma_start(ecol_i[:, q, :], dram[name + "_col"]).then_inc(w_in, 16)
            sp.dma_start(adjT[:, :], dram["adjT"]).then_inc(w_in, 16)
            sp.dma_start(W1[:, :, :], dram["L2_W1"].rearrange("(c p) n -> p c n", p=P)).then_inc(w_in, 16)
            sp.dma_start(b1[:, :], dram["L2_b1"].rearrange("(p o) -> p o", o=1)).then_inc(w_in, 16)
            sp.dma_start(W2[:, :], dram["L2_W2"]).then_inc(w_in, 16)
            sp.dma_start(b2[:, :], dram["L2_b2"].rearrange("(o d) -> o d", o=1).to_broadcast([P, D])).then_inc(w_in, 16)
            for q, name in enumerate(("W_linT", "W_valT")):
                sp.dma_start(Wlv[:, :, q * D:(q + 1) * D], dram[name].rearrange("(c p) n -> p c n", p=P))\
                    .then_inc(w_in, 16)
            sp.dma_start(Wout[:, :, :], dram["W_outT"].rearrange("(c p) n -> p c n", p=P)).then_inc(w_in, 16)
            sp.wait_ge(const, 5)
            for head in range(HEADS):
                c, s = head // 2, head % 2
                for at in (ROWS - HEADS + head, 2 * ROWS - HEADS + head):
                    sp.dma_start(APAD[s * N:(s + 1) * N, c, at:at + 1],
                                 dram["a"][head, :].rearrange("(f o) -> f o", o=1)).then_inc(w_in, 16)
            sp.dma_start(X[:, :, :], src[0]).then_inc(x_in, 16)

        def constants(pool):
            g = nc.gpsimd
            g.memset(mhalf[:, :], -0.5).then_inc(const, 1)
            g.memset(eps[:, :], 1e-8).then_inc(const, 1)
            g.memset(APAD[:, :, :], 0.0).then_inc(const, 1)
            g.iota(node_i[:, :], pattern=[[0, 1]], base=0, channel_multiplier=1).then_inc(const, 1)
            g.iota(col_i[:, :], pattern=[[0, 2], [1, N]], base=0, channel_multiplier=0).then_inc(const, 1)
            pool.wait_ge(const, 5)
            done = [0]

            def made(ins):
                done[0] += 1
                ins.then_inc(prep, 1)
                pool.wait_ge(prep, done[0])

            pool.wait_ge(w_in, B_DMAS * 16)
            made(g.tensor_copy(node[:, :], node_i[:, :]))
            made(g.tensor_scalar(tmp[:, 0:1], node[:, :], float(N), -float(N), ALU.is_ge, ALU.mult))
            made(g.tensor_scalar(tmp[:, 1:2], tmp[:, 0:1], 0.5, None, ALU.mult))
            made(g.tensor_tensor(node[:, :], node[:, :], tmp[:, 0:1], ALU.add))
            made(g.tensor_scalar(tmp[0:NH, 2:3], node[0:NH, :], float(NH), None, ALU.add))
            made(g.tensor_copy(colm[:, :], col_i[:, :]))
            made(g.tensor_copy(src_f[:, :], src_i[:, :]))
            made(g.tensor_copy(dst_f[:, :], dst_i[:, :]))
            made(g.tensor_copy(ecol[:, :, :], ecol_i[:, :, :]))
            made(g.tensor_scalar(SRC[:, :], src_f[:, :], node[:, 0:1], None, ALU.is_equal))
            g.tensor_scalar(DST[:, :], dst_f[:, :], node[:, 0:1], None, ALU.is_equal).then_inc(aa_in, 1)
            pool.wait_ge(aa_in, 1)
            made(g.tensor_scalar(SRChi[:, :], src_f[0:NH, :], tmp[0:NH, 2:3], None, ALU.is_equal))
            made(g.tensor_tensor(GS[:, :], SRC[:, :], DST[:, :], ALU.add))
            for c in range(CH):
                made(g.tensor_scalar(SRCT[:, c, :], colm[:, 0:N], ecol[:, 0, c:c + 1], None, ALU.is_equal))
                made(g.tensor_scalar(DSTT[:, c, :], colm[:, :], ecol[:, 1, c:c + 1], None, ALU.is_equal))
            pool.wait_ge(aa_sb, 1)
            g.tensor_tensor(ES[0:N, :], ES[0:N, :], SRC[0:N, :], ALU.mult).then_inc(z_in, 1)
            made(g.tensor_scalar(src_f[:, :], src_f[:, :], tmp[:, 1:2], None, ALU.add))
            for n in range(NH):
                made(g.tensor_scalar(dst_f[:, :], src_f[:, :], float(n), None, ALU.is_equal))
                made(g.tensor_scalar(NEG[:, n, :], dst_f[:, :], -1.0, 1e30, ALU.add, ALU.mult))

        def edge_products(pe):
            mm = nc.tensor.matmul
            pe.wait_ge(aa_in, 1)
            mm(ps[0:N, 0, :], adjT[:, :], DST[0:N, :], start=True, stop=True).then_inc(aa_ps, 1)
            pe.wait_ge(z_in, 1)
            mm(ps[:, 1, :], ones[:, :], ES[0:N, :], start=True, stop=True).then_inc(z_ps, 1)

        def edge_logarithms(act):
            a = nc.scalar.activation
            act.wait_ge(aa_ps, 1)
            a(ES[0:N, :], ps[0:N, 0, :], ACT.Copy).then_inc(aa_sb, 1)
            act.wait_ge(z_ps, 1)
            act.wait_ge(w_in, B_DMAS * 16)
            act.wait_ge(const, 5)
            a(LOGA[:, :], ps[:, 1, :], ACT.Ln, bias=eps[:, 0:1])

        block = ctx.enter_context(nc.Block())

        @block.sync
        def _(sp):
            load(sp)

        @block.scalar
        def _(act):
            edge_logarithms(act)

        @block.gpsimd
        def _(pool):
            constants(pool)
            pool.wait_ge(pw_in, 1)
            nc.gpsimd.tensor_tensor(st_lanes[0:N, 11:12], st_lanes[0:N, 10:11], lap.mhalf_pow[0:N, 0:1], ALU.pow).then_inc(pw_out, 1)

        @block.tensor
        def _(pe):
            pe.wait_ge(tr_in, 1)
            nc.tensor.matmul(ps[:, 2, 0:N], ones[:, :], DG[:, :], start=True, stop=True)
            nc.tensor.matmul(ps[:, 2, N:2 * N], ones[:, :], SEL[:, 0:N], start=True, stop=True)
            nc.tensor.transpose(ps[0:N, 3, 0:P], M[:, :], ident[:, :]).then_inc(tr_out, 1)
            with pe.Fori(0, PASSES) as it:
                pe.wait_ge(halves_in, it + 1)
                nc.tensor.matmul(ps[:, 7, 0:2 * SECTIONS], pair_sum[:, :], halves[:, :, :], start=True, stop=True)\
                    .then_inc(halves_out, 1)
            edge_products(pe)
            pe.wait_ge(tr_in, 2)
            nc.tensor.matmul(ps[0:N, 4, 0:N], ones[:, 0:N], DG[:, :], start=True, stop=True).then_inc(tr_out, 1)
            pe.wait_ge(tr_in, 3)
            nc.tensor.transpose(ps[0:N, 5, 0:N], Zs[:, :], ident[0:N, 0:N]).then_inc(tr_out, 1)
            pe.wait_ge(tr_in, 4)
            nc.tensor.matmul(ps[:, 6, 0:N], QT2[:, :], Z2[:, 0:N], start=True, stop=True)
            nc.tensor.matmul(ps[:, 6, N:2 * N], Z2[:, :], QT2[:, 0:N], start=True, stop=True).then_inc(tr_out, 1)

        @block.vector
        def _(dve):
            done = [0]
            st = st_lanes

            def link(ins, wait=True):
                done[0] += 1
                ins.then_inc(link_s, 1)
                if wait:
                    dve.wait_ge(link_s, done[0])

            v = nc.vector
            link(v.tensor_tensor(MK[0:N, :], iota[0:N, 0:N], pidx_f[0:N, 0:N], ALU.subtract))
            link(v.tensor_scalar(MK[0:N, :], MK[0:N, :], -1.0, None, ALU.is_equal))
            link(v.tensor_tensor(SEL[:, 0:N], M[0:N, :], MK[0:N, :], ALU.mult))
            v.tensor_tensor(DG[:, :], M[0:N, :], ident[0:N, 0:N], ALU.mult).then_inc(tr_in, 1)
            dve.wait_ge(tr_out, 1)
            link(v.tensor_copy(D_[:, :], ps[:, 2, 0:N]))
            link(v.tensor_copy(E_all[:, :], ps[:, 2, N:2 * N]))
            link(v.tensor_copy(QT2[:, 0:N], ps[0:N, 3, N:P]))
            link(v.tensor_copy(QT2[:, N:P], ps[0:N, 3, N:P]))
            for half in range(2):
                r = slice(half * N, half * N + N)
                link(v.tensor_copy(pair_sum[r, :].rearrange("p (b n) -> p b n", n=N),
                                   ident[r, r].rearrange("p (o n) -> p o n", o=1).to_broadcast([N, 2, N])))
            aE, G, t0 = Vr[:, :], V[:, :], Wr[:, :]
            link(v.scalar_tensor_tensor(aE, E_all[:, :], -1.0, E_all[:, :], ALU.mult, ALU.max))
            link(v.tensor_tensor(t0, E_all[:, :], E_all[:, :], ALU.mult))
            link(v.tensor_scalar(nE2_all[:, :], t0, TINY, -1.0, ALU.max, ALU.mult))
            link(v.tensor_copy(G, aE))
            link(v.tensor_tensor(G[:, 1:N], aE[:, 1:N], aE[:, 0:N - 1], ALU.add))
            link(v.tensor_tensor(t0, D_[:, :], G, ALU.subtract))
            link(v.tensor_reduce(st[:, 0:1], t0, AX_X, ALU.min))
            link(v.tensor_tensor(t0, D_[:, :], G, ALU.add))
            link(v.tensor_reduce(st[:, 1:2], t0, AX_X, ALU.max))
            link(v.tensor_tensor(st[:, 2:3], st[:, 1:2], st[:, 0:1], ALU.subtract))
            link(v.tensor_scalar(st[:, 3:4], st[:, 2:3], 1.002, 1e-6, ALU.mult, ALU.add))
            link(v.scalar_tensor_tensor(st[:, 0:1], st[:, 3:4], -1e-3, st[:, 0:1], ALU.mult, ALU.add))
            link(v.tensor_scalar(st[:, 4:5], st[:, 3:4], 1.0 / (SECTIONS + 1), None, ALU.mult))
            link(v.tensor_scalar(steps[:, :], iota[:, 0:SECTIONS], 1.0, None, ALU.add))
            v.tensor_copy(D_end[0:N, :], D_[0:N, 0:MID])
            v.tensor_copy(nE2_end[0:N, :], nE2_all[0:N, 0:MID])
            v.tensor_copy(D_end[N:P, :], D_[N:P, N - 1:MID - 1:-1])
            v.tensor_copy(nE2_end[N:P, :], nE2_all[N:P, N - 2:MID - 2:-1])
            lane = st[:, 8:9]
            link(v.tensor_scalar(lane, is_q[:, :], float(N), pidx_f[:, 0:1], ALU.mult, ALU.add))

            PER = 2 * (MID - 1) + 15
            with dve.Fori(0, PASSES) as it:
                base = dve.snap(it * PER)
                n = [0]

                def mlink(ins, wait=True):
                    n[0] += 1
                    ins.then_inc(ms, 1)
                    if wait:
                        dve.wait_ge(ms, base + n[0])

                mlink(v.tensor_scalar(lam[:, :], steps[:, :], st[:, 4:5], st[:, 0:1], ALU.mult, ALU.add))
                mlink(v.tensor_tensor(DL[:, :, :], col(D_end[:, :]).to_broadcast([P, MID, SECTIONS]),
                                      lam[:, :].rearrange("p (o f) -> p o f", o=1).to_broadcast([P, MID, SECTIONS]),
                                      ALU.subtract))
                for j in range(1, MID):
                    mlink(v.reciprocal(rc[:, :], DL[:, j - 1, :]))
                    mlink(v.scalar_tensor_tensor(DL[:, j, :], rc[:, :], nE2_end[:, j - 1:j], DL[:, j, :], ALU.mult,
                                                 ALU.add))
                mlink(v.tensor_copy(halves[0:N, 0, :], DL[0:N, MID - 1, :]), wait=False)
                mlink(v.reciprocal(halves[N:P, 0, :], DL[N:P, MID - 1, :]))
                mlink(v.memset(DL[0:N, MID - 1, :], 1.0), wait=False)
                mlink(v.tensor_scalar(halves[N:P, 0, :], halves[N:P, 0, :], nE2_end[N:P, MID - 1:MID], None, ALU.mult))
                mlink(v.tensor_scalar(halves[:, 0, :], halves[:, 0, :], 1e30, -1e30, ALU.min, ALU.max), wait=False)
                mlink(v.tensor_scalar(neg[:, :, :], DL[:, :, :], 0.0, None, ALU.is_lt))
                mlink(v.tensor_reduce(halves[:, 1, :], neg[:, :, :].rearrange("p k f -> p f k"), AX_X, ALU.add))
                dve.sem_inc(halves_in, 1)
                dve.wait_ge(halves_out, it + 1)
                mlink(v.tensor_scalar(rc[:, :], ps[:, 7, 0:SECTIONS], 0.0, None, ALU.is_lt))
                mlink(v.tensor_tensor(cnt[:, :], rc[:, :], ps[:, 7, SECTIONS:2 * SECTIONS], ALU.add))
                mlink(v.tensor_scalar(lam[:, :], cnt[:, :], lane, None, ALU.is_le))
                mlink(v.tensor_reduce(st[:, 5:6], lam[:, :], AX_X, ALU.add))
                mlink(v.scalar_tensor_tensor(st[:, 0:1], st[:, 5:6], st[:, 4:5], st[:, 0:1], ALU.mult, ALU.add))
                mlink(v.tensor_scalar(st[:, 4:5], st[:, 4:5], 1.0 / (SECTIONS + 1), None, ALU.mult))
                assert n[0] == PER, n[0]
            lamc = st[:, 6:7]
            link(v.scalar_tensor_tensor(lamc, st[:, 4:5], 0.5 * (SECTIONS + 1), st[:, 0:1], ALU.mult, ALU.add))
            v.tensor_scalar(DG[:, :], ident[0:N, 0:N], lamc[0:N], None, ALU.mult).then_inc(tr_in, 1)

            K = N - 1
            aE, E_, nE2, st = aE[0:N], E_all[0:N], nE2_all[0:N], st_lanes[0:N]
            link(v.memset(PD[:, :, :], 1.0))
            link(v.memset(nE2P[:, :, :], 0.0))
            link(v.memset(nEP[:, :, :], 0.0))
            link(v.memset(BE[:, :, :], 0.0))
            link(v.tensor_scalar(PD[:, :, 0], D_[0:N, :], st[:, 6:7], None, ALU.subtract))
            v.tensor_copy(PD[:, :, 1], PD[:, ::-1, 0])
            v.tensor_copy(nE2P[:, 0:K, 0], nE2[:, 0:K])
            v.tensor_copy(nE2P[:, 0:K, 1], nE2[:, K - 1::-1])
            link(v.tensor_scalar(nEP[:, 0:K, 0], E_[:, 0:K], -1.0, None, ALU.mult))
            v.tensor_copy(nEP[:, 0:K, 1], nEP[:, K - 1::-1, 0])
            chains = [(15, -1, 16, 15), (16, 1, 16, 15), (31, -1, 32, 31), (32, 1, 32, 31), (47, -1, 16, 47),
                      (48, 1, 16, 47)]

            def part(c):
                start, way, size, seam = chains[c]
                last = start + way * (size - 1)
                if way > 0:
                    return slice(start, start + size), slice(start, start + size - 1), size, seam
                stop = last - 1 if last else None
                return slice(start, stop, -1), slice(start - 1, stop, -1), size, seam

            for c in range(6):
                rows, between, size, seam = part(c)
                v.tensor_copy(PD[:, 0:size, 2 + c], PD[:, rows, 0])
                link(v.tensor_copy(BE[:, 0:size - 1, c], E_[:, between]))
                link(v.tensor_tensor(PD[:, 0, 2 + c:3 + c], PD[:, 0, 2 + c:3 + c], aE[:, seam:seam + 1],
                                     ALU.subtract))
            link(v.tensor_tensor(nE2P[:, 0:MID, 2:8], BE[:, :, :], BE[:, :, :], ALU.mult))
            link(v.tensor_scalar(nE2P[:, 0:MID, 2:8], nE2P[:, 0:MID, 2:8], TINY, -1.0, ALU.max, ALU.mult))
            link(v.tensor_copy(QP[:, 0, :], PD[:, 0, :]))
            for k in range(1, N):
                w = 8 if k < MID else 2
                link(v.reciprocal(rc[0:N, 0:w], QP[:, k - 1, 0:w]))
                link(v.tensor_tensor(rc[0:N, 8:8 + w], rc[0:N, 0:w], nE2P[:, k - 1, 0:w], ALU.mult))
                link(v.tensor_tensor(QP[:, k, 0:w], rc[0:N, 8:8 + w], PD[:, k, 0:w], ALU.add))
            link(v.tensor_scalar(QP[:, :, 0:2], QP[:, :, 0:2], 1e30, -1e30, ALU.min, ALU.max))
            v.reciprocal(BM[:, :, :], QP[:, 0:MID, 2:8])
            link(v.reciprocal(RP[:, :, :], QP[:, :, 0:2]))
            v.tensor_scalar(BM[:, :, :], BM[:, :, :], 1e30, -1e30, ALU.min, ALU.max)
            link(v.tensor_scalar(RP[:, :, :], RP[:, :, :], 1e30, -1e30, ALU.min, ALU.max))
            v.tensor_tensor(BM[:, :, :], BM[:, :, :], BE[:, :, :], ALU.mult)
            link(v.tensor_tensor(RP[:, :, :], RP[:, :, :], nEP[:, :, :], ALU.mult))
            link(v.tensor_tensor(gam[:, :], QP[:, :, 0], QP[:, ::-1, 1], ALU.add))
            link(v.tensor_tensor(gam[:, :], gam[:, :], PD[:, :, 0], ALU.subtract))
            link(v.scalar_tensor_tensor(gam[:, :], gam[:, :], -1.0, gam[:, :], ALU.mult, ALU.max))
            link(v.tensor_reduce(st[:, 7:8], gam[:, :], AX_X, ALU.min))
            link(v.tensor_scalar(dlt[:, :], gam[:, :], st[:, 7:8], None, ALU.is_le))
            link(v.tensor_copy(ZP[:, :, 0], dlt[:, :]))
            link(v.tensor_copy(ZP[:, :, 1], dlt[:, ::-1]))
            link(v.memset(BC[:, 0, :], 1.0))
            for j in range(K - 1, -1, -1):
                link(v.tensor_tensor(rc[0:N, 0:2], RP[:, j, :], ZP[:, j + 1, :], ALU.mult))
                up = K - j
                if up < MID:
                    link(v.tensor_tensor(BC[:, up, :], BC[:, up - 1, :], BM[:, up - 1, :], ALU.mult), wait=False)
                link(v.tensor_tensor(ZP[:, j, :], rc[0:N, 0:2], ZP[:, j, :], ALU.add))
            link(v.tensor_tensor(Z[:, :], ZP[:, :, 0], ZP[:, ::-1, 1], ALU.add))
            link(v.tensor_tensor(Z[:, :], Z[:, :], dlt[:, :], ALU.subtract))
            v.tensor_tensor_reduce(gam[:, :], Z[:, :], Z[:, :], 1.0, 0.0, ALU.mult, ALU.add,
                                   st[:, 10:11]).then_inc(pw_in, 1)
            dve.wait_ge(pw_out, 1)
            link(v.tensor_scalar(Z[:, :], Z[:, :], st[:, 11:12], None, ALU.mult))

            link(v.memset(BZ[:, :, :], 0.0))
            link(v.tensor_tensor(gam[:, :], Z[:, :], Z[:, :], ALU.mult))
            for c in range(6):
                rows, _, size, _ = part(c)
                link(v.tensor_copy(BZ[:, 0:size, c], gam[:, rows]), wait=False)
            link(v.tensor_scalar(BC[:, :, :], BC[:, :, :], 1e18, -1e18, ALU.min, ALU.max))
            link(v.tensor_tensor(BC[:, :, :], BC[:, :, :], BC[:, :, :], ALU.mult))
            link(v.tensor_reduce(st[:, 20:26], BZ[:, :, :].rearrange("p j c -> p c j"), AX_X, ALU.max))
            link(v.tensor_tensor(BM[:, :, :], BZ[:, :, :],
                                 st[:, 20:26].rearrange("p (o c) -> p o c", o=1).to_broadcast([N, 32, 6]),
                                 ALU.is_ge))
            link(v.tensor_tensor(BM[:, :, :], BM[:, :, :], BZ[:, :, :], ALU.mult))
            link(v.tensor_tensor(BM[:, :, :], BM[:, :, :], BC[:, :, :], ALU.mult))
            link(v.tensor_reduce(st[:, 26:32], BM[:, :, :].rearrange("p j c -> p c j"), AX_X, ALU.add))
            mx = st[:, 20:26].rearrange("p (b s) -> p b s", s=2)
            q2 = st[:, 26:32].rearrange("p (b s) -> p b s", s=2)
            low_side, q_at = st[:, 32:35], st[:, 35:38]
            link(v.tensor_tensor(low_side, mx[:, :, 0], mx[:, :, 1], ALU.is_ge))
            link(v.tensor_tensor(q_at, q2[:, :, 0], q2[:, :, 1], ALU.subtract))
            link(v.tensor_tensor(q_at, q_at, low_side, ALU.mult))
            link(v.tensor_tensor(q_at, q_at, q2[:, :, 1], ALU.add))
            eb = E_[:, 15:48:16]
            r_at, r2 = st[:, 38:41], st[:, 42:45]
            link(v.tensor_scalar(st[:, 45:48], eb, 0.0, 2.0, ALU.is_ge, ALU.mult))
            link(v.tensor_scalar(st[:, 45:48], st[:, 45:48], -1.0, None, ALU.add))
            link(v.tensor_tensor(r2, st[:, 45:48], Z[:, 16:49:16], ALU.mult))
            link(v.tensor_tensor(r_at, r2, Z[:, 15:48:16], ALU.add))
            link(v.tensor_reduce(st[:, 48:49], Z[:, 0:N:16], AX_X, ALU.add))
            link(v.tensor_scalar(st[:, 41:42], st[:, 48:49], -1.0, None, ALU.mult))
            dve.wait_ge(tr_out, 2)
            link(v.tensor_copy(dlt[:, :], ps[0:N, 4, 0:N]))
            link(v.tensor_tensor(dlt[:, :], dlt[:, :], dlt[:, :], ALU.mult))
            link(v.tensor_reduce(st[:, 49:50], dlt[:, :], AX_X, ALU.max))
            link(v.tensor_scalar(st[:, 50:51], st[:, 49:50], (8 * 2.0 ** -24) ** 2, None, ALU.mult))
            link(v.tensor_tensor(r2, r_at, r_at, ALU.mult))
            link(v.tensor_scalar(r2, r2, 1e-8, None, ALU.is_gt))
            link(v.tensor_tensor(st[:, 51:54], eb, eb, ALU.mult))
            link(v.tensor_tensor(st[:, 51:54], st[:, 51:54], q_at, ALU.mult))
            link(v.tensor_scalar(st[:, 51:54], st[:, 51:54], 2.0, st[:, 50:51], ALU.mult, ALU.is_gt))
            link(v.tensor_tensor(r2, r2, st[:, 51:54], ALU.max))
            sg = st[:, 54:58]
            link(v.tensor_scalar(sg, st[:, 38:42], 0.0, -2.0, ALU.is_ge, ALU.mult))
            link(v.tensor_scalar(sg, sg, 1.0, None, ALU.add))
            leaf, s15, s31, s47 = sg[:, 3:4], sg[:, 0:1], sg[:, 1:2], sg[:, 2:3]
            k15, k31, k47 = r2[:, 0:1], r2[:, 1:2], r2[:, 2:3]

            def choose(out, flag, yes, no):
                link(v.tensor_tensor(st[:, 62:63], yes, no, ALU.subtract))
                link(v.scalar_tensor_tensor(out, st[:, 62:63], flag, no, ALU.mult, ALU.add))

            choose(st[:, 58:59], k15, s15, leaf)
            choose(st[:, 59:60], k47, s47, leaf)
            choose(st[:, 60:61], low_side[:, 1:2], st[:, 58:59], st[:, 59:60])
            choose(st[:, 61:62], k31, s31, st[:, 60:61])
            v.tensor_scalar(Zs[:, :], Z[:, :], st[:, 61:62], None, ALU.mult).then_inc(tr_in, 1)
            dve.wait_ge(tr_out, 3)
            link(v.tensor_copy(Z2[:, 0:N], ps[0:N, 5, 0:N]))
            v.tensor_copy(Z2[:, N:P], ps[0:N, 5, 0:N]).then_inc(tr_in, 1)
            dve.wait_ge(tr_out, 4)
            bdu, bdut = keep["bd_U"], keep["bd_UT"]
            link(v.memset(bdu[:, :], 0.0))
            link(v.memset(bdut[:, :], 0.0))
            for half in range(2):
                r = slice(half * N, half * N + N)
                link(v.tensor_copy(bdu[r, r], ps[r, 6, 0:N]))
                link(v.tensor_copy(bdut[r, r], ps[r, 6, N:2 * N]))


def col(ap):
    return ap.rearrange("p (n o) -> p n o", o=1)


def settle(eng, passed):
    eng.sem_inc(passed, 1)


FIRST = (0, 0)


def at(turn, per, n):
    j, k = turn
    return add(j * (2 * per), k * per + n)


def add(base, n):
    return base + n


def layer_norm(nc, eng, link, ln_value, rows, stats, mv, var, rstd, var_ready, rstd_ready, passed):
    row_statistics(nc, eng, link, rows, stats, mv, var, var_ready, passed)
    return scale_rows(nc, eng, ln_value, rows, mv, rstd, rstd_ready)


def row_statistics(nc, eng, link, rows, stats, mv, var, var_ready, passed):
    v = nc.vector
    for t in range(HALF):
        ins = v.bn_stats(stats[:, t, :], rows[:, t, :])
    link(ins)
    settle(eng, passed)
    for t in range(HALF):
        ins = v.bn_aggr(mv[:, t, :], stats[:, t, :])
    link(ins)
    v.tensor_scalar(var[:, :], mv[:, :, 1], LN_EPS, None, ALU.add).then_inc(var_ready, 1)


def scale_rows(nc, eng, ln_value, rows, mv, rstd, rstd_ready):
    v = nc.vector
    eng.wait_ge(rstd_ready, ln_value[0] + 1)
    for t in range(HALF):
        ins = v.tensor_scalar(rows[:, t, :], rows[:, t, :], mv[:, t, 0:1], rstd[:, t:t + 1], ALU.subtract, ALU.mult)
    return ins


def lstm_units():
    units = [(1, tile, 0, fc) for tile in range(2) for fc in range(2)]
    for p in range(2, MAX_SKIP + 1):
        units += [(p, 0, step, fc) for step in range(p) for fc in range(2)]
    return units


UNITS = lstm_units()
FIRST_UNIT = {p: min(u for u, x in enumerate(UNITS) if x[0] == p) for p in range(1, MAX_SKIP + 1)}


def gates_of(step):
    return (0, 2, 3) if step == 0 else (0, 2, 1, 3)


def f_count(u):
    return sum(1 for x in UNITS[:u] if x[2] > 0)


def windows(buf, kc, p, tile, step):
    if p == 1:
        return buf[:, kc, tile * 512:(tile + 1) * 512]
    nw = T // p
    return buf[:, kc, :].rearrange("q (b t) -> q b t", t=T)[:, :, step:step + (nw - 1) * p + 1:p]


def width(p):
    return 512 if p == 1 else GB * (T // p)


def cells(ap, p):
    w = ap[:, 0:width(p)]
    return w if p == 1 else w.rearrange("q (b w) -> q b w", b=GB)


def layers_0_1(nc, dram, keep):
    with ExitStack() as ctx:
        def sb(name, shape, dt=F32):
            return ctx.enter_context(nc.sbuf_tensor(name, shape, dt))

        def sem(name):
            return ctx.enter_context(nc.semaphore(name))

        w = keep["w"]
        ps = ctx.enter_context(nc.psum_tensor("ps_a", [P, 8, 512], F32))
        X = sb("a_x", [P, TILES, D])
        XR = sb("a_xr", [P, TILES, D])
        AXT = sb("a_axt", [P, 2, GT])
        Y = sb("a_y", [P, TILES, D])
        arena = sb("a_arena", [P, 16384])
        H1T = arena[:, 0:2048].rearrange("p (c n) -> p c n", c=2)
        HT = arena[:, 2048:4096].rearrange("p (c n) -> p c n", c=2)
        HB = arena[:, 4096:6144].rearrange("p (c n) -> p c n", c=2)
        GATE = arena[:, 6144:10240].rearrange("p (f g n) -> p f g n", f=2, g=4)
        C = arena[:, 10240:11264].rearrange("p (f n) -> p f n", f=2)
        HS = arena[:, 11264:13312].rearrange("p (s f n) -> p s f n", s=2, f=2)
        TMP = arena[:, 13312:13824]
        S1 = arena[:, 0:4096].rearrange("p (t n) -> p t n", t=TILES)
        WS = arena[:, 4096:8192].rearrange("p (h c n) -> p h c n", h=2, c=4)
        S2 = arena[:, 8192:16384].rearrange("p (h c n) -> p h c n", h=2, c=8)
        stats = sb("a_stats", [P, HALF, 6])
        mv = sb("a_mv", [P, HALF, 2])
        var = sb("a_var", [P, HALF])
        rstd = sb("a_rstd", [P, HALF])
        mhalf = sb("a_mhalf", [P, HALF])
        ident, bda, bdw = keep["ident"], keep["bd_adjT"], keep["bd_wT"]
        lap = keep["lap"]
        HH = STEPS_A_TURN
        HH_EARLY = 2
        ROW_AT = [4, 9, 16, 21, 26, 31, 36, 41]
        W_AT = [7, 12, 19, 24, 29, 34, 39, 44]
        row_ps = [ps[:, 7 if q < HH_EARLY else 3, 0:T] for q in range(HH)]
        w_ps = [ps[:, 6 if q < HH_EARLY else 2, 0:T] for q in range(HH)]

        x_in = sem("x_loaded")
        ax_ps, ax_sb = sem("ax_ps"), sem("ax_sb")
        h1_ps, h1_sb = sem("h1_ps"), sem("h1_sb")
        y_ps, y_sb = sem("y_ps"), sem("y_sb")
        h2_ps, h2_sb = sem("h2_ps"), sem("h2_sb")
        xpart = sem("lstm_x_read")
        gates_ps = sem("gates_ps")
        ig_sb, f_sb, o_sb = sem("ig_sb"), sem("f_sb"), sem("o_sb")
        c_sb = sem("c_sb")
        tc_sb = sem("tanh_c_sb")
        h_sb = sem("h_sb")
        ht_ps = sem("h_tokens_ps")
        x1_sb = sem("x1_sb")
        wx_ps, wx_sb = sem("wx_ps"), sem("wx_sb")
        s1_ps, s1_sb = sem("s1_ps"), sem("s1_sb")
        ws_ps, ws_sb = sem("ws_ps"), sem("ws_sb")
        s2_ps, s2_sb = sem("s2_ps"), sem("s2_sb")
        y3_ps, y3_sb = sem("y3_ps"), sem("y3_sb")
        x2_ps, x2_sb = sem("x2_ps"), sem("x2_sb")
        x2_read = sem("x2_ps_read")
        var_ready, rstd_ready = sem("var_ready"), sem("rstd_ready")
        stored = sem("x2_stored")
        dve_passed = sem("a_dve_passed")
        own = sem("dve_own")
        const = sem("a_const")
        NU = len(UNITS)
        NF = f_count(NU)
        LN_CALLS = 4

        block = ctx.enter_context(nc.Block())

        @block.sync
        def _(sp):
            src = dram["x"].rearrange("(g t p) d -> g p t d", p=P, t=TILES)
            dst = dram["x2"].rearrange("(g t p) d -> g p t d", p=P, t=TILES)
            sp.sem_inc(stored, 16)
            sp.dma_start(X[:, :, :], src[0]).then_inc(x_in, 16)
            keep["load_weights"](sp, "lstm")
            keep["load_weights"](sp, "layer 1")
            for g in range(NGRP):
                if g + 1 < NGRP:
                    sp.wait_ge(x1_sb, 2 * (g + 1))
                    sp.dma_start(X[:, :, :], src[g + 1]).then_inc(x_in, 16)
                sp.wait_ge(x2_sb, 2 * (g + 2))
                sp.dma_start(dst[g], XR[:, :, :]).then_inc(stored, 16)
            sp.wait_ge(stored, 16 * (NGRP + 1))

        @block.gpsimd
        def _(pool):
            nc.gpsimd.memset(mhalf[:, :], -0.5).then_inc(const, 1)
            pool.wait_ge(const, 1)
            with pool.Fori(0, NGRP) as i:
                for n in range(LN_CALLS):
                    pool.wait_ge(var_ready, i * LN_CALLS + (n + 1))
                    nc.gpsimd.tensor_tensor(rstd[:, :], var[:, :], mhalf[:, :], ALU.pow).then_inc(rstd_ready, 1)
                    if n == 1:
                        for q in range(HH):
                            pool.wait_ge(lap.n2_ok, i * HH + (q + 1))
                            nc.gpsimd.tensor_tensor(lap.sc[:, 4:5], lap.sc[:, 3:4], lap.half_pow[:, :], ALU.pow)\
                                .then_inc(lap.nrm_ok, 1)

        @block.tensor
        def _(pe):
            mm = nc.tensor.matmul

            def reflect_row(i, q):
                pe.wait_ge(lap.sel_ok, i * HH + (q + 1))
                mm(row_ps[q], lap.SEL[:, :], lap.M[0:T, :], start=True, stop=True).then_inc(lap.row_ok, 1)

            def reflect_w(i, q):
                pe.wait_ge(lap.dg_ok, i * HH + (q + 1))
                mm(w_ps[q], lap.ones[:, :], lap.DG[:, :], start=True, stop=True).then_inc(lap.w_ok, 1)

            def reflection_slot(i, n):
                if n in ROW_AT:
                    reflect_row(i, ROW_AT.index(n))
                if n in W_AT:
                    reflect_w(i, W_AT.index(n))

            def mix_nodes(h, src, fcs, banks, mat, tok):
                for c in range(fcs):
                    for t in range(HALF):
                        last = mm(ps[:, banks + c, t * P:(t + 1) * P], src[:, tok + t, c * P:(c + 1) * P], mat[:, :],
                                  start=True, stop=True)
                return last

            keep["weights_wait"](pe, "layer 0")
            with pe.Fori(0, NGRP) as i:
                pe.wait_ge(x_in, i * 16 + 16)
                for h in range(2):
                    mix_nodes(h, X, 2, 4 * h, bda, 4 * h).then_inc(ax_ps, 1)
                pe.wait_ge(x2_read, i * 2 + 2)
                for h in range(2):
                    pe.wait_ge(ax_sb, i * 2 + (h + 1))
                    for oc in range(2):
                        o = ps[:, 4 * h + 2 + oc, :]
                        mm(o, w["bg0"][0:1, oc * P:(oc + 1) * P], w["rowsum"][0:1, :], start=True, stop=False)
                        for kc in range(2):
                            last = mm(o, w["Wg0"][:, kc, oc * P:(oc + 1) * P], AXT[:, kc, h * HN:(h + 1) * HN],
                                      start=False, stop=(kc == 1))
                    last.then_inc(h1_ps, 1)
                for h in range(2):
                    pe.wait_ge(h1_sb, i * 2 + (h + 1))
                    for t in range(HALF):
                        for kc in range(2):
                            last = mm(ps[:, 4 * h + t // 2, (t % 2) * D:(t % 2 + 1) * D],
                                      H1T[:, kc, (4 * h + t) * P:(4 * h + t + 1) * P], w["Wg1"][:, kc, :],
                                      start=(kc == 0), stop=(kc == 1))
                    last.then_inc(y_ps, 1)
                for h in range(2):
                    pe.wait_ge(y_sb, i * 2 + (h + 1))
                    mix_nodes(h, Y, 2, 4 * h + 2, bda, 4 * h).then_inc(h2_ps, 1)
                keep["weights_wait"](pe, "lstm")
                pe.wait_ge(h2_sb, i * 2 + 1)
                for u, (p, tile, step, _) in enumerate(UNITS):
                    if u % 2:
                        continue
                    src = HT if p == 1 else HB
                    n = width(p)

                    def gates(fc, weights, kcs, rhs, first, final):
                        for g in gates_of(step):
                            for kc in kcs:
                                last = mm(ps[:, 4 * fc + g, 0:n], weights[:, kc, g * D + fc * P:g * D + (fc + 1) * P],
                                          rhs(kc), start=(first and kc == kcs[0]), stop=(final and kc == kcs[-1]))
                        return last

                    def x_part(fc, kcs):
                        return gates(fc, w["Wih"][:, p - 1], kcs, lambda kc: windows(src, kc, p, tile, step),
                                     kcs[0] == 0, step == 0 and kcs[-1] == 1)

                    if p == 1 and u > 0:
                        pe.wait_ge(o_sb, i * NU + (u - 1))
                    if p > 1:
                        pe.wait_ge(h_sb, i * NU + (u - 1))
                    if step == 0:
                        x_part(0, [0])
                        if u > 0:
                            pe.wait_ge(o_sb, i * NU + u)
                        else:
                            pe.wait_ge(h2_sb, i * 2 + 2)
                        x_part(1, [0])
                        if p > 1:
                            pe.wait_ge(h_sb, i * NU + u)
                        for fc in range(2):
                            x_part(fc, [1]).then_inc(gates_ps, 1)
                    else:
                        x_part(0, [0, 1]).then_inc(xpart, 1)
                        pe.wait_ge(o_sb, i * NU + u)
                        x_part(1, [0, 1]).then_inc(xpart, 1)
                        pe.wait_ge(h_sb, i * NU + u)
                        for fc in range(2):
                            gates(fc, w["Whh"][:, p - 2], [0, 1], lambda kc: HS[:, (step - 1) % 2, kc, 0:n], False,
                                  True).then_inc(gates_ps, 1)
                def to_tokens(h, fc):
                    for t in range(HALF):
                        last = nc.tensor.transpose(
                            ps[:, 4 * h + t // 2, (t % 2) * D + fc * P:(t % 2) * D + (fc + 1) * P],
                            HB[:, fc, (4 * h + t) * P:(4 * h + t + 1) * P], ident[:, :])
                    return last

                pe.wait_ge(h_sb, i * NU + (NU - 1))
                to_tokens(0, 0)
                pe.wait_ge(o_sb, i * NU + NU)
                to_tokens(1, 0)
                pe.wait_ge(h_sb, i * NU + NU)
                for h in range(2):
                    to_tokens(h, 1).then_inc(ht_ps, 1)

                def wx(h):
                    pe.wait_ge(x1_sb, i * 2 + (h + 1))
                    mix_nodes(h, XR, 2, 4 * h + 2, bdw, 4 * h).then_inc(wx_ps, 1)

                def s1(h):
                    pe.wait_ge(wx_sb, i * 2 + (h + 1))
                    for t in range(HALF):
                        for kc in range(2):
                            last = mm(ps[:, 4 * h + t, :], AXT[:, kc, (4 * h + t) * P:(4 * h + t + 1) * P],
                                      w["W1"][:, kc, :], start=(kc == 0), stop=(kc == 1))
                    last.then_inc(s1_ps, 1)

                def ws(h):
                    pe.wait_ge(s1_sb, i * 2 + (h + 1))
                    mix_nodes(h, S1, 4, 4 * h, bdw, 4 * h).then_inc(ws_ps, 1)

                keep["weights_wait"](pe, "layer 1")
                wx(0)
                s1(0)
                wx(1)
                ws(0)
                s1(1)
                for h in range(2):
                    pe.wait_ge(ws_sb, i * 2 + (h + 1))
                    if h == 1:
                        pe.wait_ge(s2_sb, i * 16 + 8)
                    for oc in range(8):
                        if oc >= 4:
                            pe.wait_ge(s2_sb, i * 16 + (8 * h + oc - 3))
                        if h == 0 and oc == 1:
                            ws(1)
                        for kc in range(4):
                            if kc % 2 == 0:
                                n = 16 * h + 2 * oc + kc // 2
                                if n == ROW_AT[0]:
                                    pe.wait_ge(ws_sb, i * 2 + 2)
                                reflection_slot(i, n)
                            last = mm(ps[:, 4 * h + oc % 4, :], w["W2"][:, kc, oc * P:(oc + 1) * P],
                                      WS[:, h, kc, :], start=(kc == 0), stop=(kc == 3))
                        last.then_inc(s2_ps, 1)
                for h in range(2):
                    pe.wait_ge(s2_sb, i * 16 + (8 * h + 8))
                    for t in range(HALF):
                        for kc in range(8):
                            if kc % 4 == 0:
                                reflection_slot(i, 32 + 8 * h + 2 * t + kc // 4)
                            last = mm(ps[:, 4 * h + t // 2, (t % 2) * D:(t % 2 + 1) * D],
                                      S2[:, h, kc, t * P:(t + 1) * P], w["W3"][:, kc, :], start=(kc == 0),
                                      stop=(kc == 7))
                    last.then_inc(y3_ps, 1)
                pe.wait_ge(lap.sel_ok, i * HH + (HH + 1))
                for h in range(2):
                    pe.wait_ge(y3_sb, i * 2 + (h + 1))
                    for u in range(2):
                        last = mm(ps[:, 4 * h + 2 + u, :], bdw[:, :], Y[:, 4 * h + 2 * u:4 * h + 2 * u + 2, :],
                                  start=True, stop=True)
                    last.then_inc(x2_ps, 1)

        @block.scalar
        def _(act):
            a = nc.scalar.activation
            keep["weights_wait"](act, "layer 0")
            with act.Fori(0, NGRP) as i:
                for h in range(2):
                    act.wait_ge(ax_ps, i * 2 + (h + 1))
                    a(AXT[:, :, h * HN:(h + 1) * HN], ps[:, 4 * h:4 * h + 2, :], ACT.Copy).then_inc(ax_sb, 1)
                for h in range(2):
                    act.wait_ge(h1_ps, i * 2 + (h + 1))
                    a(H1T[:, :, h * HN:(h + 1) * HN], ps[:, 4 * h + 2:4 * h + 4, :], ACT.Relu).then_inc(h1_sb, 1)
                for h in range(2):
                    act.wait_ge(h2_ps, i * 2 + (h + 1))
                    a(HT[:, :, h * HN:(h + 1) * HN], ps[:, 4 * h + 2:4 * h + 4, :], ACT.Relu).then_inc(h2_sb, 1)
                for u, (p, tile, step, fc) in enumerate(UNITS):
                    n = width(p)
                    act.wait_ge(gates_ps, i * NU + (u + 1))
                    if u >= 2:
                        act.wait_ge(h_sb, i * NU + (u - 1))

                    def gate(g, func):
                        b = (p - 1) * 8 + 2 * g + fc
                        return a(GATE[:, fc, g, 0:n], ps[:, 4 * fc + g, 0:n], func, bias=w["bias"][:, b:b + 1])

                    gate(0, ACT.Sigmoid)
                    gate(2, ACT.Tanh).then_inc(ig_sb, 1)
                    if step > 0:
                        gate(1, ACT.Sigmoid).then_inc(f_sb, 1)
                    gate(3, ACT.Sigmoid).then_inc(o_sb, 1)
                    act.wait_ge(c_sb, i * NU + (u + 1))
                    a(GATE[:, fc, 2, 0:n], C[:, fc, 0:n], ACT.Tanh).then_inc(tc_sb, 1)
                def wx(h):
                    act.wait_ge(wx_ps, i * 2 + (h + 1))
                    a(AXT[:, :, h * HN:(h + 1) * HN], ps[:, 4 * h + 2:4 * h + 4, :], ACT.Copy).then_inc(wx_sb, 1)

                def s1(h):
                    act.wait_ge(s1_ps, i * 2 + (h + 1))
                    a(S1[:, 4 * h:4 * h + 4, :], ps[:, 4 * h:4 * h + 4, :], ACT.Relu).then_inc(s1_sb, 1)

                def ws(h):
                    act.wait_ge(ws_ps, i * 2 + (h + 1))
                    a(WS[:, h, :, :], ps[:, 4 * h:4 * h + 4, :], ACT.Copy).then_inc(ws_sb, 1)

                wx(0)
                s1(0)
                wx(1)
                ws(0)
                s1(1)
                for h in range(2):
                    for oc in range(8):
                        if h == 0 and oc == 1:
                            ws(1)
                        act.wait_ge(s2_ps, i * 16 + (8 * h + oc + 1))
                        a(S2[:, h, oc, :], ps[:, 4 * h + oc % 4, :], ACT.Relu).then_inc(s2_sb, 1)
                for h in range(2):
                    act.wait_ge(y3_ps, i * 2 + (h + 1))
                    a(Y[:, 4 * h:4 * h + 4, :], ps[:, 4 * h:4 * h + 2, :], ACT.Copy).then_inc(y3_sb, 1)

        @block.vector
        def _(dve):
            v = nc.vector
            keep["weights_wait"](dve, "layer 0")
            per = keep["dve_links_a"]
            v.memset(var[:, :], 0.0).then_inc(x2_sb, 2)
            dve.sem_inc(x2_read, 2)
            with dve.Fori(0, NGRP) as i:
                turn = dve.snap(i * per)
                n_own = [0]

                def link(ins, wait=True):
                    n_own[0] += 1
                    ins.then_inc(own, 1)
                    if wait:
                        dve.wait_ge(own, turn + n_own[0])

                for h in range(2):
                    dve.wait_ge(y_ps, i * 2 + (h + 1))
                    v.tensor_tensor(Y[:, 4 * h:4 * h + 4, :],
                                    ps[:, 4 * h:4 * h + 2, :].rearrange("p b (t n) -> p (b t) n", n=D),
                                    across(w["bg1"], HALF), ALU.add).then_inc(y_sb, 1)
                for u, (p, tile, step, fc) in enumerate(UNITS):
                    n = width(p)
                    g = [GATE[:, fc, q, 0:n] for q in range(4)]
                    c = C[:, fc, 0:n]
                    dve.wait_ge(ig_sb, i * NU + (u + 1))
                    if step == 0:
                        v.tensor_tensor(c, g[0], g[2], ALU.mult).then_inc(c_sb, 1)
                    else:
                        v.tensor_tensor(TMP[:, 0:n], g[0], g[2], ALU.mult)
                        dve.wait_ge(f_sb, i * NF + (f_count(u) + 1))
                        link(v.tensor_tensor(c, g[1], c, ALU.mult))
                        v.tensor_tensor(c, c, TMP[:, 0:n], ALU.add).then_inc(c_sb, 1)
                    last_step = step == p - 1
                    if last_step:
                        out = windows(HB, fc, p, tile, step)
                        if step > 0 and fc == 0:
                            dve.wait_ge(xpart, i * NF + (f_count(u) + 2))
                    else:
                        out = cells(HS[:, step % 2, fc, :], p)
                    dve.wait_ge(tc_sb, i * NU + (u + 1))
                    v.tensor_tensor(out, cells(g[3], p), cells(g[2], p), ALU.mult).then_inc(h_sb, 1)
                for h in range(2):
                    dve.wait_ge(ht_ps, i * 2 + (h + 1))
                    if h == 0:
                        keep["wait_stored"](dve, stored, i)
                    ins = v.tensor_tensor(XR[:, 4 * h:4 * h + 4, :], X[:, 4 * h:4 * h + 4, :],
                                          ps[:, 4 * h:4 * h + 2, :].rearrange("p b (t n) -> p (b t) n", n=D),
                                          ALU.add)
                    link(ins)
                    layer_norm(nc, dve, link, [i * LN_CALLS + (0 + h)], XR[:, 4 * h:4 * h + 4, :], stats, mv, var,
                               rstd, var_ready, rstd_ready, dve_passed).then_inc(x1_sb, 1)
                for q in range(HH):
                    reflect(nc, dve, link, lap, row_ps[q], w_ps[q], i * HH + q)
                for h in range(2):
                    dve.wait_ge(x2_ps, i * 2 + (h + 1))
                    link(v.tensor_tensor(XR[:, 4 * h:4 * h + 4, :], XR[:, 4 * h:4 * h + 4, :],
                                         ps[:, 4 * h + 2:4 * h + 4, :].rearrange("p b (t n) -> p (b t) n", n=D),
                                         ALU.add))
                    dve.sem_inc(x2_read, 1)
                for h in range(2):
                    layer_norm(nc, dve, link, [i * LN_CALLS + (2 + h)], XR[:, 4 * h:4 * h + 4, :], stats, mv, var,
                               rstd, var_ready, rstd_ready, dve_passed).then_inc(x2_sb, 1)
                assert n_own[0] == per, n_own[0]


def across(row, n):
    return row[:, :].rearrange("p (o d) -> p o d", o=1).to_broadcast([P, n, D])


def layers_2_3(nc, dram, keep):
    N = T
    RING = 4
    with ExitStack() as ctx:
        def sb(name, shape, dt=F32):
            return ctx.enter_context(nc.sbuf_tensor(name, shape, dt))

        def sem(name):
            return ctx.enter_context(nc.semaphore(name))

        ps = ctx.enter_context(nc.psum_tensor("ps_b", [P, 8, 512], F32))
        ident, bdu, bdut = keep["ident"], keep["bd_U"], keep["bd_UT"]
        E = keep["edges"]
        W1, b1, W2, b2, Wlv, Wout, APAD, YT = \
            E.W1, E.b1, E.W2, E.b2, E.Wlv, E.Wout, E.APAD, E.YT
        node, SRC, GS, SRCT, DSTT, SRClo, SRChi, NEG = \
            E.node, E.SRC, E.GS, E.SRCT, E.DSTT, E.SRClo, E.SRChi, E.NEG
        LOGA, X, ES, mhalf, x_in = \
            E.LOGA, E.X, E.ES, E.mhalf, E.x_in
        XR2 = sb("b_xr", [P, 2, TILES, D])
        FT = sb("b_ft", [P, 2, GT])
        HT = sb("b_ht", [P, GT])
        Y = sb("b_y", [P, TILES, D])
        QH = sb("b_q_high", [P, 2, TILES, D], F32R)
        QL = sb("b_q_low", [P, 2, TILES, D], F32R)
        VAL = sb("b_values", [P, 2, TILES, D])
        ABS = sb("b_abs", [P, 2, EDGES])
        LR = sb("b_lrelu", [P, 2, 2, EDGES])[:, :, :, :]
        EX = sb("b_ex", [ROWS, EDGES])
        JUNK = 8
        mjunk = LR.rearrange("p s c e -> p (s c e)").bitcast(BF16).rearrange("p (j e) -> p j e", e=EDGES)
        m = sb("b_m", [P, NH])
        mT = sb("b_mT", [NH, P])
        EXT = sb("b_ext", [P, CH, ROWS])
        RD = sb("b_rd", [N, ROWS])
        AT = sb("b_at", [P, CH, ROWS])
        ATH = sb("b_at_high", [P, CH, ROWS], F32R)
        ATL = sb("b_at_low", [P, CH, ROWS])
        PROH = sb("b_pro_high", [P, RING, 8, N], F32R)
        PROL = sb("b_pro_low", [P, RING, 8, N], F32R)
        PT = sb("b_pt", [P, 2, HEADS, N])
        stats = sb("b_stats", [P, HALF, 6])
        mv = sb("b_mv", [P, HALF, 2])
        var = sb("b_var", [P, HALF])
        rstd = sb("b_rstd", [P, HALF])

        ux_ps, ux_sb = sem("ux_ps"), sem("ux_sb")
        hid_ps, hid_sb = sem("hid_ps"), sem("hid_sb")
        o2_ps, o2_sb = sem("o2_ps"), sem("o2_sb")
        x3_ps, x3_sb = sem("x3_ps"), sem("x3_sb")
        xt_ps, xt_sb = sem("xt_ps"), sem("xt_sb")
        qv_ps, qv_sb = sem("qv_ps"), sem("qv_sb")
        ql_sb = sem("q_low_sb")
        pair_ps, abs_sb, lr_sb = sem("pair_ps"), sem("abs_sb"), sem("lr_sb")
        score_ps, es_sb = sem("score_ps"), sem("es_sb")
        m_sb, mT_ps, mT_sb, mg_ps, d_sb, ex_sb = (sem("m_sb"), sem("mT_ps"), sem("mT_sb"), sem("mg_ps"), sem("d_sb"),
                                                  sem("ex_sb"))
        ext_ps, ext_sb, den_ps, rd_sb, rg_ps, at_sb = (sem("ext_ps"), sem("ext_sb"), sem("den_ps"), sem("rd_sb"),
                                                       sem("rg_ps"), sem("at_sb"))
        proh_sb, prol0_sb, prol_sb = sem("proh_sb"), sem("prol0_sb"), sem("prol_sb")
        pt_ps, pt_sb, yt_ps, yt_sb = sem("pt_ps"), sem("pt_sb"), sem("yt_ps"), sem("yt_sb")
        fin_ps, fin_sb = sem("fin_ps"), sem("fin_sb")
        fin_read = sem("fin_ps_read")
        var_ready, rstd_ready = sem("b_var_ready"), sem("b_rstd_ready")
        stored = sem("out_stored")
        dve_passed, pe_passed = sem("b_dve_passed"), sem("b_pe_passed")
        own = sem("b_dve_own")
        LN_CALLS = 4
        SPECTRAL_AT = [2, 3, 4, 5, 8, 9, 10, 11]
        STATISTICS_AT = [6, 12]
        SCALE_AT = [7, 13]

        def product(eng, v, turn, t, c, pro, part, pro_sb):
            q = t * CH + c
            if q >= RING:
                eng.wait_ge(pt_ps, at(turn, TILES * CH, q - RING + 1))
            v.tensor_tensor(pro[:, q % RING, :, :],
                            SRCT[:, c, :].rearrange("p (o n) -> p o n", o=1).to_broadcast([P, 8, N]),
                            col(part[:, c, 8 * t:8 * t + 8]).to_broadcast([P, 8, N]), ALU.mult).then_inc(pro_sb, 1)

        block = ctx.enter_context(nc.Block())

        @block.sync
        def _(sp):
            src = dram["x2"].rearrange("(g t p) d -> g p t d", p=P, t=TILES)
            dst = dram["out"].rearrange("(g t p) d -> g p t d", p=P, t=TILES)
            sp.sem_inc(stored, 32)
            for g in range(NGRP):
                if g + 1 < NGRP:
                    sp.wait_ge(x3_sb, 2 * (g + 1))
                    sp.dma_start(X[:, :, :], src[g + 1]).then_inc(x_in, 16)
                if g >= 1:
                    sp.wait_ge(fin_sb, 2 * (g + 1))
                    sp.dma_start(dst[g - 1], XR2[:, (g - 1) % 2, :, :]).then_inc(stored, 16)
            sp.wait_ge(fin_sb, 2 * (NGRP + 1))
            sp.dma_start(dst[NGRP - 1], XR2[:, (NGRP - 1) % 2, :, :]).then_inc(stored, 16)
            sp.wait_ge(stored, 16 * (NGRP + 2))

        @block.gpsimd
        def _(pool):
            g = nc.gpsimd

            def row_scales(turn, n):
                pool.wait_ge(var_ready, at(turn, LN_CALLS, n))
                g.tensor_tensor(rstd[:, :], var[:, :], mhalf[:, :], ALU.pow).then_inc(rstd_ready, 1)

            def queries(turn, par):
                for h in range(2):
                    pool.wait_ge(qv_sb, at(turn, 2, h + 1))
                    g.tensor_tensor(QL[:, par, 4 * h:4 * h + 4, :], Y[:, 4 * h:4 * h + 4, :],
                                    QH[:, par, 4 * h:4 * h + 4, :].bitcast(F32), ALU.subtract).then_inc(ql_sb, 1)

            def one_turn(turn, nxt, par):
                if nxt:
                    row_scales(turn, 3)
                    row_scales(turn, 4)
                    queries(nxt, 1 - par)
                pool.wait_ge(at_sb, at(turn, 1, 1))
                for t in range(TILES):
                    for c in range(1, CH):
                        product(pool, g, turn, t, c, PROL, ATL, prol_sb)
                row_scales(turn, 5 if nxt else 3)
                row_scales(turn, 6 if nxt else 4)

            row_scales(FIRST, 1)
            row_scales(FIRST, 2)
            queries(FIRST, 0)
            with pool.Fori(0, NGRP // 2 - 1) as j:
                one_turn((j, 0), (j, 1), 0)
                one_turn((j, 1), (j, 2), 1)
            j = NGRP // 2 - 1
            one_turn((j, 0), (j, 1), 0)
            one_turn((j, 1), None, 1)

        @block.tensor
        def _(pe):
            mm = nc.tensor.matmul
            def spectral(turn, h, step):
                if step == 0:
                    pe.wait_ge(x_in, at(turn, 16, 16))
                    if h == 0:
                        pe.wait_ge(fin_read, at(turn, 2, 0))
                    else:
                        pe.wait_ge(x3_sb, at(turn, 2, 1))
                    for c in range(2):
                        for t in range(HALF):
                            last = mm(ps[:, 5 + c, t * P:(t + 1) * P], X[:, 4 * h + t, c * P:(c + 1) * P],
                                      bdu[:, :], start=True, stop=True)
                    last.then_inc(ux_ps, 1)
                elif step == 1:
                    pe.wait_ge(ux_sb, at(turn, 2, h + 1))
                    for kc in range(2):
                        last = mm(ps[:, 7, :], W1[:, kc, :], FT[:, kc, h * HN:(h + 1) * HN],
                                  start=(kc == 0), stop=(kc == 1))
                    last.then_inc(hid_ps, 1)
                elif step == 2:
                    pe.wait_ge(hid_sb, at(turn, 2, h + 1))
                    for t in range(HALF):
                        last = mm(ps[:, 5 + t // 2, (t % 2) * D:(t % 2 + 1) * D],
                                  HT[:, (4 * h + t) * P:(4 * h + t + 1) * P], W2[:, :], start=True, stop=True)
                    last.then_inc(o2_ps, 1)
                else:
                    pe.wait_ge(o2_sb, at(turn, 2, h + 1))
                    for u in range(2):
                        last = mm(ps[:, 5 + u, :], bdut[:, :], Y[:, 4 * h + 2 * u:4 * h + 2 * u + 2, :],
                                  start=True, stop=True)
                    last.then_inc(x3_ps, 1)

            def queries(turn, par):
                for h in range(2):
                    pe.wait_ge(x3_sb, at(turn, 2, h + 1))
                    for c in range(2):
                        for t in range(HALF):
                            last = nc.tensor.transpose(ps[:, 2 * h + c, t * P:(t + 1) * P],
                                                       XR2[:, par, 4 * h + t, c * P:(c + 1) * P], ident[:, :])
                    last.then_inc(xt_ps, 1)
                pe.wait_ge(es_sb, at(turn, 1, 1))
                for h in range(2):
                    pe.wait_ge(xt_sb, at(turn, 2, 1 if h == 0 else 2))
                    for t in range(HALF):
                        for kc in range(2):
                            last = mm(ps[:, 4 * (1 - h) + t, :], FT[:, kc, (4 * h + t) * P:(4 * h + t + 1) * P],
                                      Wlv[:, kc, :], start=(kc == 0), stop=(kc == 1))
                    last.then_inc(qv_ps, 1)

            def pairs(turn, par, b):
                r = slice((b % 2) * N, (b % 2 + 1) * N)
                if b >= 2:
                    pe.wait_ge(lr_sb, at(turn, GB, b - 1))
                for c in range(2):
                    o = ps[:, 2 * (b % 2) + c, :]
                    mm(o, QH[r, par, b // 2, c * P:(c + 1) * P], GS[r, :], start=True, stop=False)
                    last = mm(o, QL[r, par, b // 2, c * P:(c + 1) * P], GS[r, :], start=False, stop=True)
                last.then_inc(pair_ps, 1)

            def scores(turn, b):
                pe.wait_ge(lr_sb, at(turn, GB, b + 1))
                if b == 0:
                    pe.wait_ge(fin_read, at(turn, 2, 2))
                for c in range(2):
                    col0 = ROWS - HEADS - HEADS * b
                    last = mm(ps[:, 4, :], APAD[:, c, col0:col0 + P], LR[:, b % 2, c, :],
                              start=(b == 0 and c == 0), stop=(b == GB - 1 and c == 1))
                last.then_inc(score_ps, 1)

            def softmax(turn):
                pe.wait_ge(m_sb, at(turn, 1, 1))
                nc.tensor.transpose(ps[0:NH, 5, 0:P], m[:, :], ident[:, :]).then_inc(mT_ps, 1)
                pe.wait_ge(mT_sb, at(turn, 1, 1))
                mm(ps[0:ROWS, 6, :], mT[:, 0:ROWS], SRClo, start=True, stop=False)
                mm(ps[0:ROWS, 6, :], mT[:, ROWS:P], SRChi[:, :], start=False, stop=True).then_inc(mg_ps, 1)
                pe.wait_ge(ex_sb, at(turn, 1, 1))
                settle(pe, pe_passed)
                for c in range(CH):
                    last = nc.tensor.transpose(ps[:, 7, c * ROWS:(c + 1) * ROWS], EX[:, c * P:(c + 1) * P],
                                               ident[0:ROWS, 0:ROWS])
                last.then_inc(ext_ps, 1)
                pe.wait_ge(ext_sb, at(turn, 1, 1))
                for c in range(CH):
                    last = mm(ps[0:N, 5, 0:ROWS], SRCT[:, c, :], EXT[:, c, :], start=(c == 0), stop=(c == CH - 1))
                last.then_inc(den_ps, 1)
                pe.wait_ge(rd_sb, at(turn, 1, 1))
                for c in range(CH):
                    last = mm(ps[:, 6, c * ROWS:(c + 1) * ROWS], SRC[0:N, c * P:(c + 1) * P], RD[:, :], start=True,
                              stop=True)
                last.then_inc(rg_ps, 1)

            def node_matrices(turn, t):
                if t >= 2:
                    pe.wait_ge(pt_sb, at(turn, TILES, t - 1))
                for c in range(CH):
                    q = t * CH + c
                    pe.wait_ge(proh_sb, at(turn, TILES * CH, q + 1))
                    mm(ps[:, t % 2, :], DSTT[:, c, :], PROH[:, q % RING, :, :], start=(c == 0), stop=False)
                    if c == 0:
                        pe.wait_ge(prol0_sb, at(turn, TILES, t + 1))
                    else:
                        pe.wait_ge(prol_sb, at(turn, TILES * (CH - 1), t * (CH - 1) + c))
                    mm(ps[:, t % 2, :], DSTT[:, c, :], PROL[:, q % RING, :, :], start=False, stop=(c == CH - 1))\
                        .then_inc(pt_ps, 1)

            def values(turn, par, t):
                pe.wait_ge(pt_sb, at(turn, TILES, t + 1))
                if t >= 2:
                    pe.wait_ge(yt_sb, at(turn, TILES, t - 1))
                for b in range(2):
                    r = slice(b * N, (b + 1) * N)
                    for c in range(2):
                        last = mm(ps[:, 2 + 2 * (t % 2) + b, c * P:(c + 1) * P],
                                  VAL[r, par, t, c * P:(c + 1) * P], PT[r, t % 2, 2 * c:2 * c + 2, :],
                                  start=True, stop=True)
                last.then_inc(yt_ps, 1)

            def one_turn(turn, nxt, par):
                pe.wait_ge(ql_sb, at(turn, 2, 2))
                pairs(turn, par, 0)
                for b in range(1, GB + 1):
                    if b < GB:
                        pairs(turn, par, b)
                    scores(turn, b - 1)
                    if nxt and b in SPECTRAL_AT:
                        spectral(nxt, *divmod(SPECTRAL_AT.index(b), 4))
                if nxt:
                    queries(nxt, 1 - par)
                    pe.wait_ge(qv_sb, at(nxt, 2, 1))
                softmax(turn)
                if nxt:
                    pe.wait_ge(qv_sb, at(nxt, 2, 2))
                node_matrices(turn, 0)
                for t in range(1, TILES + 1):
                    if t < TILES:
                        node_matrices(turn, t)
                    values(turn, par, t - 1)
                pe.wait_ge(yt_sb, at(turn, TILES, TILES))
                for h in range(2):
                    for t in range(HALF):
                        for kc in range(2):
                            last = mm(ps[:, 4 + 2 * h + t // 2, (t % 2) * D:(t % 2 + 1) * D],
                                      YT[:, kc, (4 * h + t) * P:(4 * h + t + 1) * P], Wout[:, kc, :],
                                      start=(kc == 0), stop=(kc == 1))
                    last.then_inc(fin_ps, 1)

            for h in range(2):
                for step in range(4):
                    spectral((0, 0), h, step)
            queries((0, 0), 0)
            with pe.Fori(0, NGRP // 2 - 1) as j:
                one_turn((j, 0), (j, 1), 0)
                one_turn((j, 1), (j, 2), 1)
            j = NGRP // 2 - 1
            one_turn((j, 0), (j, 1), 0)
            one_turn((j, 1), None, 1)

        @block.scalar
        def _(act):
            a = nc.scalar.activation
            def spectral(turn, h, step):
                if step == 0:
                    act.wait_ge(ux_ps, at(turn, 2, h + 1))
                    a(FT[:, :, h * HN:(h + 1) * HN], ps[:, 5:7, :], ACT.Copy).then_inc(ux_sb, 1)
                elif step == 1:
                    act.wait_ge(hid_ps, at(turn, 2, h + 1))
                    a(HT[:, h * HN:(h + 1) * HN], ps[:, 7, :], ACT.Relu, bias=b1[:, 0:1]).then_inc(hid_sb, 1)

            def queries(turn, par):
                for h in range(2):
                    act.wait_ge(xt_ps, at(turn, 2, h + 1))
                    a(FT[:, :, h * HN:(h + 1) * HN], ps[:, 2 * h:2 * h + 2, :], ACT.Copy).then_inc(xt_sb, 1)
                for h in range(2):
                    act.wait_ge(qv_ps, at(turn, 2, h + 1))
                    b = 4 * (1 - h)
                    a(Y[:, 4 * h:4 * h + 4, :], ps[:, b:b + 4, 0:D], ACT.Copy)
                    a(QH[:, par, 4 * h:4 * h + 4, :], ps[:, b:b + 4, 0:D], ACT.Copy)
                    a(VAL[:, par, 4 * h:4 * h + 4, :], ps[:, b:b + 4, D:2 * D], ACT.Copy).then_inc(qv_sb, 1)

            def one_turn(turn, nxt, par):
                for b in range(GB):
                    act.wait_ge(pair_ps, at(turn, GB, b + 1))
                    if b >= 1:
                        act.wait_ge(lr_sb, at(turn, GB, b))
                    a(ABS[:, :, :], ps[:, 2 * (b % 2):2 * (b % 2) + 2, :], ACT.Abs, scale=0.4).then_inc(abs_sb, 1)
                    if nxt and b in SPECTRAL_AT:
                        spectral(nxt, *divmod(SPECTRAL_AT.index(b), 4))
                if nxt:
                    queries(nxt, 1 - par)
                act.wait_ge(mT_ps, at(turn, 1, 1))
                a(mT[:, :], ps[0:NH, 5, 0:P], ACT.Copy).then_inc(mT_sb, 1)
                act.wait_ge(d_sb, at(turn, 1, 1))
                a(EX[:, :], ES[0:ROWS, :], ACT.Exp).then_inc(ex_sb, 1)
                act.wait_ge(ext_ps, at(turn, 1, 1))
                a(EXT[:, :, :], ps[:, 7, 0:CH * ROWS].rearrange("p (c r) -> p c r", c=CH), ACT.Copy)\
                    .then_inc(ext_sb, 1)
                for t in range(TILES + 1):
                    if t < TILES:
                        act.wait_ge(pt_ps, at(turn, TILES * CH, CH * (t + 1)))
                        for b in range(2):
                            r = slice(b * N, (b + 1) * N)
                            last = a(PT[r, t % 2, :, :],
                                     ps[r, t % 2, b * HEADS * N:(b + 1) * HEADS * N]
                                     .rearrange("p (h n) -> p h n", n=N), ACT.Copy)
                        last.then_inc(pt_sb, 1)
                    if t > 0:
                        q = t - 1
                        act.wait_ge(yt_ps, at(turn, TILES, q + 1))
                        o = ps[:, 2 + 2 * (q % 2):4 + 2 * (q % 2), 0:D].rearrange("p b (c s n) -> p b c s n", c=2, s=2)
                        y = YT[:, :, q * P:(q + 1) * P].rearrange("p c (b n) -> p b c n", b=2)
                        for s in range(2):
                            r = slice(s * N, (s + 1) * N)
                            last = a(y[r, :, :, :], o[r, :, :, s, :], ACT.Copy)
                        last.then_inc(yt_sb, 1)

            for h in range(2):
                for step in range(2):
                    spectral((0, 0), h, step)
            queries((0, 0), 0)
            with act.Fori(0, NGRP // 2 - 1) as j:
                one_turn((j, 0), (j, 1), 0)
                one_turn((j, 1), (j, 2), 1)
            j = NGRP // 2 - 1
            one_turn((j, 0), (j, 1), 0)
            one_turn((j, 1), None, 1)

        @block.vector
        def _(dve):
            v = nc.vector
            v.memset(var[:, :], 0.0).then_inc(fin_sb, 2)
            dve.sem_inc(fin_read, 2)
            v.memset(m[:, :], 0.0).then_inc(es_sb, 1)

            def link(ins):
                n_own[0] += 1
                ins.then_inc(own, 1)
                dve.wait_ge(own, add(link_base[0], n_own[0]))

            def residual(h, dst, banks, x):
                link(v.tensor_tensor(dst[:, 4 * h:4 * h + 4, :], x[:, 4 * h:4 * h + 4, :],
                                     ps[:, banks:banks + 2, :].rearrange("p b (t n) -> p (b t) n", n=D), ALU.add))

            def spectral(turn, par, h, step):
                if step == 2:
                    dve.wait_ge(o2_ps, at(turn, 2, h + 1))
                    v.tensor_tensor(Y[:, 4 * h:4 * h + 4, :],
                                    ps[:, 5:7, :].rearrange("p b (t n) -> p (b t) n", n=D), across(b2, HALF),
                                    ALU.add).then_inc(o2_sb, 1)
                elif step == 3:
                    dve.wait_ge(x3_ps, at(turn, 2, h + 1))
                    if h == 0:
                        dve.wait_ge(stored, at(turn, 16, 16))
                    residual(h, XR2[:, par, :, :], 5, X)

            def statistics(turn, par, h):
                row_statistics(nc, dve, link, XR2[:, par, 4 * h:4 * h + 4, :], stats, mv, var, var_ready, dve_passed)

            def scale(turn, par, h):
                scale_rows(nc, dve, [h if turn is FIRST else at(turn, LN_CALLS, h - 2)],
                           XR2[:, par, 4 * h:4 * h + 4, :], mv, rstd, rstd_ready).then_inc(x3_sb, 1)

            def leaky_relu(turn, b):
                dve.wait_ge(abs_sb, at(turn, GB, b + 1))
                if b >= 2:
                    dve.wait_ge(score_ps, at(turn, GB, b - 1))
                v.scalar_tensor_tensor(LR[:, b % 2, :, :], ps[:, 2 * (b % 2):2 * (b % 2) + 2, :], 0.6,
                                       ABS[:, :, :], ALU.mult, ALU.add).then_inc(lr_sb, 1)

            def one_turn(turn, nxt, par):
                XR = XR2[:, par, :, :]
                for b in range(GB):
                    if b >= 4:
                        leaky_relu(turn, b)
                    if nxt and b in SPECTRAL_AT:
                        spectral(nxt, 1 - par, *divmod(SPECTRAL_AT.index(b), 4))
                    if nxt and b in STATISTICS_AT:
                        statistics(nxt, 1 - par, STATISTICS_AT.index(b))
                    if nxt and b in SCALE_AT:
                        scale(nxt, 1 - par, SCALE_AT.index(b))
                dve.wait_ge(score_ps, at(turn, GB, GB))
                v.tensor_tensor(ES[:, :], ps[:, 4, :], LOGA[:, :], ALU.add).then_inc(es_sb, 1)
                dve.wait_ge(es_sb, at(turn, 1, 2))
                settle(dve, dve_passed)
                for n in range(NH):
                    last = v.tensor_tensor_reduce(mjunk[:, n % JUNK, :], ES[:, :], NEG[:, n, :], 1.0, -3e38, ALU.add,
                                                  ALU.max, m[:, n:n + 1])
                    if n % JUNK == JUNK - 1 and n < NH - 1:
                        link(last)
                        settle(dve, dve_passed)
                last.then_inc(m_sb, 1)
                dve.wait_ge(mg_ps, at(turn, 1, 1))
                v.tensor_tensor(ES[0:ROWS, :], ES[0:ROWS, :], ps[0:ROWS, 6, :], ALU.subtract).then_inc(d_sb, 1)
                dve.wait_ge(den_ps, at(turn, 1, 1))
                link(v.tensor_scalar(RD[:, :], ps[0:N, 5, 0:ROWS], TINY, None, ALU.max))
                v.reciprocal(RD[:, :], RD[:, :]).then_inc(rd_sb, 1)
                dve.wait_ge(rg_ps, at(turn, 1, 1))
                link(v.tensor_tensor(AT[:, :, :], EXT[:, :, :],
                                     ps[:, 6, 0:CH * ROWS].rearrange("p (c r) -> p c r", c=CH), ALU.mult))
                link(v.tensor_copy(ATH[:, :, :], AT[:, :, :]))
                v.tensor_tensor(ATL[:, :, :], AT[:, :, :], ATH[:, :, :].bitcast(F32), ALU.subtract).then_inc(at_sb, 1)
                dve.wait_ge(at_sb, at(turn, 1, 1))
                for t in range(TILES):
                    for c in range(CH):
                        product(dve, v, turn, t, c, PROH, ATH[:, :, :].bitcast(F32), proh_sb)
                        if c == 0:
                            product(dve, v, turn, t, c, PROL, ATL, prol0_sb)
                for h in range(2):
                    dve.wait_ge(fin_ps, at(turn, 2, h + 1))
                    residual(h, XR, 4 + 2 * h, XR)
                    dve.sem_inc(fin_read, 1)
                for h in range(2):
                    rows = XR[:, 4 * h:4 * h + 4, :]
                    if nxt:
                        leaky_relu(nxt, 2 * h)
                    row_statistics(nc, dve, link, rows, stats, mv, var, var_ready, dve_passed)
                    if nxt:
                        leaky_relu(nxt, 2 * h + 1)
                    scale_rows(nc, dve, [at(turn, LN_CALLS, (4 if nxt else 2) + h)], rows, mv, rstd, rstd_ready)\
                        .then_inc(fin_sb, 1)

            n_own, link_base = [0], [0]
            for h in range(2):
                spectral(FIRST, 0, h, 2)
                spectral(FIRST, 0, h, 3)
                statistics(FIRST, 0, h)
                scale(FIRST, 0, h)
            for b in range(4):
                leaky_relu(FIRST, b)
            first, per = n_own[0], keep["dve_links_b"]
            with dve.Fori(0, NGRP // 2 - 1) as j:
                n_own[0], link_base[0] = first, dve.snap(j * (2 * per))
                one_turn((j, 0), (j, 1), 0)
                one_turn((j, 1), (j, 2), 1)
                assert n_own[0] == first + 2 * per, n_own[0] - first
            j = NGRP // 2 - 1
            link_base[0] = (j - 1) * 2 * per
            one_turn((j, 0), (j, 1), 0)
            one_turn((j, 1), None, 1)


B_DMAS = 20


def build(nc, x, adj, adjT, Wg0, bg0, Wg1, bg1, WihT, WhhT, bih, bhh, L1_W1, L1_W2, L1_W3, L2_W1, L2_b1, L2_W2, L2_b2,
          W_linT, W_valT, W_outT, a, src, dst, src_col,
          dst_col, out):
    dram = dict(x=x, adj=adj, adjT=adjT, L2_W1=L2_W1, L2_b1=L2_b1, L2_W2=L2_W2, L2_b2=L2_b2, W_linT=W_linT,
                W_valT=W_valT, W_outT=W_outT, a=a, src=src, dst=dst, src_col=src_col,
                dst_col=dst_col, out=out)
    dram["x2"] = nc.dram_tensor("x2_scratch", (BATCH * T, D), F32).ap()
    with ExitStack() as ctx:
        keep = {n: ctx.enter_context(nc.sbuf_tensor(n, [P, P], F32))
                for n in ("ident", "bd_adjT", "bd_wT", "bd_U", "bd_UT")}
        keep["lap"] = Laplacian(lambda n, sh, dt: ctx.enter_context(nc.sbuf_tensor(n, sh, dt)),
                                lambda n: ctx.enter_context(nc.semaphore(n)))
        keep["lap"].ident = keep["ident"]
        weights_in = {n: ctx.enter_context(nc.semaphore("weights_in_" + n.replace(" ", "")))
                      for n in ("layer 0", "lstm", "layer 1")}

        def wait_stored(eng, stored, i):
            eng.wait_ge(stored, i * 16 + 16)

        keep["wait_stored"] = wait_stored
        with ExitStack() as ctx_w:
            def sb(name, shape):
                return ctx_w.enter_context(nc.sbuf_tensor(name, shape, F32))

            w = dict(bg0=sb("w_bg0", [1, D]), rowsum=sb("w_rowsum", [1, HN]), Wg0=sb("w_g0", [P, 2, D]),
                     Wg1=sb("w_g1", [P, 2, D]), bg1=sb("w_bg1", [P, D]), Wih=sb("w_ih", [P, MAX_SKIP, 2, 4 * D]),
                     Whh=sb("w_hh", [P, MAX_SKIP - 1, 2, 4 * D]), bias=sb("w_bias", [P, 32]),
                     bih=sb("w_bih", [P, 32]), W1=sb("w_1", [P, 2, 512]), W2=sb("w_2", [P, 4, 1024]),
                     W3=sb("w_3", [P, 8, D]))
            keep["w"] = w
            by_rows = "(c p) n -> p c n"
            loads = {
                "layer 0": [(w["bg0"][:, :], bg0.rearrange("(o d) -> o d", o=1)),
                            (w["Wg0"][:, :, :], Wg0.rearrange(by_rows, p=P)),
                            (w["Wg1"][:, :, :], Wg1.rearrange(by_rows, p=P)),
                            (w["bg1"][:, :], bg1.rearrange("(o d) -> o d", o=1).to_broadcast([P, D])),
                            (w["bias"][:, :], bih), (w["bih"][:, :], bhh)],
                "lstm": [(w["Wih"][:, p, :, :], WihT[p].rearrange(by_rows, p=P)) for p in range(MAX_SKIP)] +
                        [(w["Whh"][:, p - 1, :, :], WhhT[p].rearrange(by_rows, p=P)) for p in range(1, MAX_SKIP)],
                "layer 1": [(w["W1"][:, :, :], L1_W1.rearrange(by_rows, p=P)),
                            (w["W2"][:, :, :], L1_W2.rearrange(by_rows, p=P)),
                            (w["W3"][:, :, :], L1_W3.rearrange(by_rows, p=P))]}

            def load_weights(sp, part):
                for d, s in loads[part]:
                    sp.dma_start(d, s).then_inc(weights_in[part], 16)

            keep["load_weights"] = load_weights
            keep["weights_wait"] = lambda eng, part: eng.wait_ge(weights_in[part], 16 * len(loads[part]))
            keep["dve_links_a"] = LINKS_A
            prepare(nc, dram, keep)
            layers_0_1(nc, dram, keep)
        keep["dve_links_b"] = LINKS_B
        keep["edges"] = EdgeData(lambda n, sh, dt=F32: ctx.enter_context(nc.sbuf_tensor(n, sh, dt)),
                                 lambda n: ctx.enter_context(nc.semaphore(n)))
        eigenvectors(nc, dram, keep)
        layers_2_3(nc, dram, keep)


LINKS_A = 24 + 24 * STEPS_A_TURN
LINKS_B = 18

_OUT = (BATCH, T, D)


def kernel(**inputs):
    import numpy as _np
    import concourse.bacc as _bacc
    from concourse import mybir as _mybir
    from concourse.bass_utils import run_bass_kernel_spmd as _run

    i = {k: _np.asarray(v) for k, v in inputs.items()}

    def by_chunk(b):
        return b.reshape(MAX_SKIP, 8, P).transpose(2, 0, 1).reshape(P, MAX_SKIP * 8)

    laid = dict(
        x=i["x"].reshape(BATCH * T, D), adj=i["adj"], adjT=i["adj"].T, Wg0=i["L0_gnn_Wg0"], bg0=i["L0_gnn_bg0"],
        Wg1=i["L0_gnn_Wg1"], bg1=i["L0_gnn_bg1"], WihT=i["L0_gnn_Wih"].transpose(0, 2, 1),
        WhhT=i["L0_gnn_Whh"].transpose(0, 2, 1), bih=by_chunk(i["L0_gnn_bih"]), bhh=by_chunk(i["L0_gnn_bhh"]),
        L1_W1=i["L1_gnn_W1"], L1_W2=i["L1_gnn_W2"], L1_W3=i["L1_gnn_W3"], L2_W1=i["L2_gnn_W1"],
        L2_b1=i["L2_gnn_b1"], L2_W2=i["L2_gnn_W2"], L2_b2=i["L2_gnn_b2"], W_linT=i["L3_gnn_W_lin"].T,
        W_valT=i["L3_gnn_W_val"].T, W_outT=i["L3_gnn_W_out"].T, a=i["L3_gnn_a"], src=i["L3_gnn_src"],
        dst=i["L3_gnn_dst"], src_col=i["L3_gnn_src"].reshape(-1, P).T, dst_col=i["L3_gnn_dst"].reshape(-1, P).T)
    nc = _bacc.Bacc("TRN2", target_bir_lowering=False, num_devices=1)
    arrays, args = {}, {}
    for name, a in laid.items():
        a = _np.ascontiguousarray(a)
        arrays[f"in_{name}"] = a
        args[name] = nc.dram_tensor(f"in_{name}", a.shape, _mybir.dt.from_np(a.dtype), kind="ExternalInput").ap()
    out = nc.dram_tensor("out_0", (BATCH * T, D), _mybir.dt.float32, kind="ExternalOutput").ap()
    build(nc, out=out, **args)
    r = _run(nc, [arrays], core_ids=[0])
    return r.results[0]["out_0"].reshape(_OUT)
```
